# Optimizing a Trainium2 kernel written in Bass

```python
import numpy as np
import jax
import jax.numpy as jnp

def _softmax(x, axis=-1):
    return jax.nn.softmax(x, axis=axis)

def _gelu(x):
    return jax.nn.gelu(x, approximate=True)

def _silu(x):
    return jax.nn.silu(x)

def _sigmoid(x):
    return jax.nn.sigmoid(x)

def _layernorm(x, axis=-1, eps=1e-05):
    m = jnp.mean(x, axis=axis, keepdims=True)
    v = jnp.var(x, axis=axis, keepdims=True)
    return (x - m) / jnp.sqrt(v + eps)

def _scatter_add(tgt, idx, src, axis=0):
    return tgt.at[idx].add(src)

def _segment_sum(src, seg, n):
    return jax.ops.segment_sum(src, seg, n)
kernel_name = 'mk_gnn_preln_d4_gnn_r8_3b8757'

def setup_inputs(seed: int=0):
    np.random.seed(seed)
    _w = jnp.asarray

    def _rec_inputs():
        import jax
        import jax.numpy as jnp
        _gk = jax.random.key(seed)
        x = -0.0005121 + 1.001 * jax.random.normal(jax.random.fold_in(_gk, 1), (12500, 32), jnp.float32)
        src = jax.random.randint(jax.random.fold_in(_gk, 2), (400000,), 0, 12500, jnp.int32)
        dst = jax.random.randint(jax.random.fold_in(_gk, 3), (400000,), 0, 12500, jnp.int32)
        _o = jnp.argsort(dst, stable=True)
        src = src[_o]
        dst = dst[_o]
        edge_attr_3 = 0.000549083 + 1.00031 * jax.random.normal(jax.random.fold_in(_gk, 12), (400000, 3), jnp.float32)
        edge_attr_32 = jax.random.uniform(jax.random.fold_in(_gk, 13), (400000, 32), jnp.float32, 0.0, 1)
        edge_attr_5 = -0.000325185 + 1.00005 * jax.random.normal(jax.random.fold_in(_gk, 14), (400000, 5), jnp.float32)
        edge_weight1 = 0.000452788 + 0.999756 * jax.random.normal(jax.random.fold_in(_gk, 16), (400000, 1), jnp.float32)
        return (x, src, dst, edge_attr_3, edge_attr_32, edge_attr_5, edge_weight1)
    x, src, dst, edge_attr_3, edge_attr_32, edge_attr_5, edge_weight1 = _rec_inputs()

    def _L0_gnn_setup():
        import jax, jax.numpy as jnp
        import numpy as np
        N_NODES = 12500
        N_EDGES = 200000
        D_FEAT = 32
        key = jax.random.key(seed)
        k1, k2, k3, k4 = jax.random.split(key, 4)
        rel = jax.random.normal(k1, (N_NODES, D_FEAT), dtype=jnp.float32)
        pattern = jax.random.uniform(k2, (N_EDGES, D_FEAT), dtype=jnp.float32)
        src = jax.random.randint(k3, (N_EDGES,), 0, N_NODES, dtype=jnp.int64)
        dst = jax.random.randint(k4, (N_EDGES,), 0, N_NODES, dtype=jnp.int64)
        return {'rel': rel, 'pattern': pattern, 'src': src, 'dst': dst}
    _L0_gnn_all = _L0_gnn_setup()
    _L0_gnn_in = {k: v for k, v in _L0_gnn_all.items() if k in ()}
    del _L0_gnn_all

    def _L1_gnn_setup():
        import jax, jax.numpy as jnp
        import numpy as np
        N = 12500
        E = 200000
        D = 32
        key = jax.random.key(seed)
        k_x, k_e, kq, kk, kv, ko = jax.random.split(key, 6)
        s = 1.0 / np.sqrt(D).astype(np.float32)
        x = jax.random.normal(k_x, (N, D), dtype=jnp.float32)
        edge_index = jax.random.randint(k_e, (2, E), 0, N, dtype=jnp.int64)
        Wq = jax.random.normal(kq, (D, D), dtype=jnp.float32) * s
        Wk = jax.random.normal(kk, (D, D), dtype=jnp.float32) * s
        Wv = jax.random.normal(kv, (D, D), dtype=jnp.float32) * s
        Wo = jax.random.normal(ko, (D, D), dtype=jnp.float32) * s
        return {'x': x, 'edge_index': edge_index, 'Wq': Wq, 'Wk': Wk, 'Wv': Wv, 'Wo': Wo}
    _L1_gnn_all = _L1_gnn_setup()
    _L1_gnn_in = {k: v for k, v in _L1_gnn_all.items() if k in ('Wq', 'Wk', 'Wv', 'Wo')}
    del _L1_gnn_all

    def _L2_gnn_setup():
        import jax, jax.numpy as jnp
        import numpy as np
        import math
        N_NODES = 12500
        N_EDGES = 200000
        IN_DIM = 32
        OUT_DIM = 32
        key = jax.random.key(seed)
        k1, k2, k3, k4 = jax.random.split(key, 4)
        X = jax.random.normal(k1, (N_NODES, IN_DIM), dtype=jnp.float32)
        src_idx = jax.random.randint(k2, (N_EDGES,), 0, N_NODES, dtype=jnp.int64)
        dst_idx = jax.random.randint(k3, (N_EDGES,), 0, N_NODES, dtype=jnp.int64)
        stdv = 1.0 / math.sqrt(OUT_DIM)
        W = jax.random.uniform(k4, (IN_DIM, OUT_DIM), dtype=jnp.float32, minval=-stdv, maxval=stdv)
        return {'X': X, 'W': W, 'src_idx': src_idx, 'dst_idx': dst_idx}
    _L2_gnn_all = _L2_gnn_setup()
    _L2_gnn_in = {k: v for k, v in _L2_gnn_all.items() if k in ('W',)}
    del _L2_gnn_all

    def _L3_gnn_setup():
        import jax, jax.numpy as jnp
        import numpy as np
        import math
        M = 8
        COMBOS = [(0, 0, 0), (0, 1, 1), (1, 0, 1), (1, 1, 0), (1, 1, 1), (2, 1, 1)]

        def _cg_coeff(j1, m1, j2, m2, j3, m3):
            if m3 != m1 + m2:
                return 0.0
            f = math.factorial
            vmin = max(0, j2 - j3 - m1, j1 + m2 - j3)
            vmax = min(j1 + j2 - j3, j1 - m1, j2 + m2)
            pref = (2 * j3 + 1) * f(j3 + j1 - j2) * f(j3 - j1 + j2) * f(j1 + j2 - j3) / f(j1 + j2 + j3 + 1)
            pref *= f(j3 + m3) * f(j3 - m3) * f(j1 - m1) * f(j1 + m1) * f(j2 - m2) * f(j2 + m2)
            s = 0.0
            for v in range(vmin, vmax + 1):
                s += (-1) ** v / (f(v) * f(j1 + j2 - j3 - v) * f(j1 - m1 - v) * f(j2 + m2 - v) * f(j3 - j2 + m1 + v) * f(j3 - j1 - m2 + v))
            return math.sqrt(pref) * s

        def _su2_cg(l1, l2, l3):
            C = np.zeros((2 * l1 + 1, 2 * l2 + 1, 2 * l3 + 1), dtype=np.complex128)
            for m1 in range(-l1, l1 + 1):
                for m2 in range(-l2, l2 + 1):
                    m3 = m1 + m2
                    if -l3 <= m3 <= l3:
                        C[m1 + l1, m2 + l2, m3 + l3] = _cg_coeff(l1, m1, l2, m2, l3, m3)
            return C

        def _qmat(l):
            q = np.zeros((2 * l + 1, 2 * l + 1), dtype=np.complex128)
            for m in range(-l, 0):
                q[l + m, l + abs(m)] = 1 / np.sqrt(2)
                q[l + m, l - abs(m)] = -1j / np.sqrt(2)
            q[l, l] = 1.0
            for m in range(1, l + 1):
                q[l + m, l + abs(m)] = (-1) ** m / np.sqrt(2)
                q[l + m, l - abs(m)] = 1j * (-1) ** m / np.sqrt(2)
            return (-1j) ** l * q

        def _so3_cg(l1, l2, l3):
            C = np.einsum('ij,kl,mn,ikn->jlm', _qmat(l1), _qmat(l2), np.conj(_qmat(l3)).T, _su2_cg(l1, l2, l3))
            assert np.abs(C.imag).max() < 1e-06
            C = C.real
            return C / np.linalg.norm(C)
        CG = {c: jnp.asarray(_so3_cg(*c), dtype=jnp.float32) for c in COMBOS}
        N, E = (12500, 200000)
        ks = jax.random.split(jax.random.key(seed), 6)
        return {'node_irreps': jax.random.normal(ks[0], (N, 4 * M), jnp.float32), 'edge_index': jax.random.randint(ks[1], (2, E), 0, N, dtype=jnp.int32), 'sh0': jax.random.normal(ks[2], (E, 1), jnp.float32), 'sh1': jax.random.normal(ks[3], (E, 3), jnp.float32), 'sh2': jax.random.normal(ks[4], (E, 5), jnp.float32), 'W': jax.random.normal(ks[5], (len(COMBOS), M, M), jnp.float32)}
    _L3_gnn_all = _L3_gnn_setup()
    _L3_gnn_in = {k: v for k, v in _L3_gnn_all.items() if k in ('W',)}
    del _L3_gnn_all
    return {'x': x, 'src': src, 'dst': dst, 'edge_attr_3': edge_attr_3, 'edge_attr_32': edge_attr_32, 'edge_attr_5': edge_attr_5, 'edge_weight1': edge_weight1, 'L1_gnn_Wq': _L1_gnn_in['Wq'], 'L1_gnn_Wk': _L1_gnn_in['Wk'], 'L1_gnn_Wv': _L1_gnn_in['Wv'], 'L1_gnn_Wo': _L1_gnn_in['Wo'], 'L2_gnn_W': _L2_gnn_in['W'], 'L3_gnn_W': _L3_gnn_in['W']}

def reference(x, src, dst, edge_attr_3, edge_attr_32, edge_attr_5, edge_weight1, L1_gnn_Wq, L1_gnn_Wk, L1_gnn_Wv, L1_gnn_Wo, L2_gnn_W, L3_gnn_W):
    import jax
    import jax.numpy as jnp

    def _L0_gnn_ref(rel, pattern, src, dst):
        import jax, jax.numpy as jnp
        import numpy as np
        N_NODES = 12500
        N_EDGES = 200000
        D_FEAT = 32
        msg = rel[src] * pattern
        sums = jax.ops.segment_sum(msg, dst, num_segments=N_NODES)
        deg = jax.ops.segment_sum(jnp.ones((msg.shape[0],), msg.dtype), dst, num_segments=N_NODES)
        h_N = sums / jnp.maximum(deg, 1.0)[:, None]
        return h_N + rel

    def _L1_gnn_ref(x, edge_index, Wq, Wk, Wv, Wo):
        import jax, jax.numpy as jnp
        import numpy as np
        N = 12500
        E = 200000
        D = 32
        sender, receiver = (edge_index[0], edge_index[1])
        n = x.shape[0]
        scale = x.shape[1] ** (-0.5)
        Q = x @ Wq
        K = x @ Wk
        V = x @ Wv
        scores = jnp.sum(Q[receiver] * K[sender], axis=1) * scale
        smax = jax.ops.segment_max(scores, receiver, num_segments=n)
        alpha = jnp.exp(scores - smax[receiver])
        Z = jax.ops.segment_sum(alpha, receiver, num_segments=n)
        alpha = alpha / (Z[receiver] + 1e-06)
        out = jax.ops.segment_sum(alpha[:, None] * V[sender], receiver, num_segments=n)
        return x + out @ Wo

    def _L2_gnn_ref(X, W, src_idx, dst_idx):
        import jax, jax.numpy as jnp
        import numpy as np
        import math
        N_NODES = 12500
        N_EDGES = 200000
        IN_DIM = 32
        OUT_DIM = 32
        agg = jax.ops.segment_sum(X[src_idx], dst_idx, num_segments=N_NODES)
        return agg @ W

    def _L3_gnn_ref(node_irreps, edge_index, sh0, sh1, sh2, W):
        import jax, jax.numpy as jnp
        import numpy as np
        import math
        M = 8
        COMBOS = [(0, 0, 0), (0, 1, 1), (1, 0, 1), (1, 1, 0), (1, 1, 1), (2, 1, 1)]

        def _cg_coeff(j1, m1, j2, m2, j3, m3):
            if m3 != m1 + m2:
                return 0.0
            f = math.factorial
            vmin = max(0, j2 - j3 - m1, j1 + m2 - j3)
            vmax = min(j1 + j2 - j3, j1 - m1, j2 + m2)
            pref = (2 * j3 + 1) * f(j3 + j1 - j2) * f(j3 - j1 + j2) * f(j1 + j2 - j3) / f(j1 + j2 + j3 + 1)
            pref *= f(j3 + m3) * f(j3 - m3) * f(j1 - m1) * f(j1 + m1) * f(j2 - m2) * f(j2 + m2)
            s = 0.0
            for v in range(vmin, vmax + 1):
                s += (-1) ** v / (f(v) * f(j1 + j2 - j3 - v) * f(j1 - m1 - v) * f(j2 + m2 - v) * f(j3 - j2 + m1 + v) * f(j3 - j1 - m2 + v))
            return math.sqrt(pref) * s

        def _su2_cg(l1, l2, l3):
            C = np.zeros((2 * l1 + 1, 2 * l2 + 1, 2 * l3 + 1), dtype=np.complex128)
            for m1 in range(-l1, l1 + 1):
                for m2 in range(-l2, l2 + 1):
                    m3 = m1 + m2
                    if -l3 <= m3 <= l3:
                        C[m1 + l1, m2 + l2, m3 + l3] = _cg_coeff(l1, m1, l2, m2, l3, m3)
            return C

        def _qmat(l):
            q = np.zeros((2 * l + 1, 2 * l + 1), dtype=np.complex128)
            for m in range(-l, 0):
                q[l + m, l + abs(m)] = 1 / np.sqrt(2)
                q[l + m, l - abs(m)] = -1j / np.sqrt(2)
            q[l, l] = 1.0
            for m in range(1, l + 1):
                q[l + m, l + abs(m)] = (-1) ** m / np.sqrt(2)
                q[l + m, l - abs(m)] = 1j * (-1) ** m / np.sqrt(2)
            return (-1j) ** l * q

        def _so3_cg(l1, l2, l3):
            C = np.einsum('ij,kl,mn,ikn->jlm', _qmat(l1), _qmat(l2), np.conj(_qmat(l3)).T, _su2_cg(l1, l2, l3))
            assert np.abs(C.imag).max() < 1e-06
            C = C.real
            return C / np.linalg.norm(C)
        CG = {c: jnp.asarray(_so3_cg(*c), dtype=jnp.float32) for c in COMBOS}
        N, E = (node_irreps.shape[0], edge_index.shape[1])
        src = node_irreps[edge_index[0]]
        feats = {0: src[:, :M][:, :, None], 1: src[:, M:].reshape(E, M, 3)}
        sh = {0: sh0, 1: sh1, 2: sh2}
        msg = {0: jnp.zeros((E, M, 1), node_irreps.dtype), 1: jnp.zeros((E, M, 3), node_irreps.dtype)}
        for idx, (le, ln, lo) in enumerate(COMBOS):
            base = jnp.einsum('ijk,ei,emj->emk', CG[le, ln, lo], sh[le], feats[ln])
            msg[lo] = msg[lo] + jnp.einsum('io,eik->eok', W[idx], base)
        tgt = edge_index[1]
        agg0 = jax.ops.segment_sum(msg[0].reshape(E, M), tgt, num_segments=N)
        agg1 = jax.ops.segment_sum(msg[1].reshape(E, 3 * M), tgt, num_segments=N)
        return jnp.concatenate([agg0, agg1], axis=1)
    edge_index = jnp.stack([src, dst])
    h = jnp.maximum(_layernorm(x, axis=-1), 0.0)
    x = x + _L0_gnn_ref(h, edge_attr_32, src, dst)
    h = jnp.maximum(_layernorm(x, axis=-1), 0.0)
    x = x + _L1_gnn_ref(h, edge_index, L1_gnn_Wq, L1_gnn_Wk, L1_gnn_Wv, L1_gnn_Wo)
    h = jnp.maximum(_layernorm(x, axis=-1), 0.0)
    x = x + _L2_gnn_ref(h, L2_gnn_W, src, dst)
    h = jnp.maximum(_layernorm(x, axis=-1), 0.0)
    x = x + _L3_gnn_ref(h, edge_index, edge_weight1, edge_attr_3, edge_attr_5, L3_gnn_W)
    return x

_drawn_inputs = setup_inputs


def setup_inputs(seed=0):
    import zlib

    import numpy as np

    out = dict(_drawn_inputs(seed))
    spreads = {}
    factors = {'edge_attr_32': 4.846, 'L1_gnn_Wk': 3.029}
    for name, (base, spread) in spreads.items():
        noise = np.random.default_rng([zlib.crc32(name.encode()), seed]).standard_normal(out[name].shape)
        drawn = base * np.exp(spread * noise) if base else spread * noise
        out[name] = jnp.asarray(drawn.astype(out[name].dtype))
    for name, factor in factors.items():
        out[name] = (out[name] * factor).astype(out[name].dtype)
    return out
```

```python
from contextlib import ExitStack
import math

import numpy as np
import concourse.bass as bass
from concourse import mybir

F32 = mybir.dt.float32
I32 = mybir.dt.int32
BF16 = mybir.dt.bfloat16
ALU = mybir.AluOpType
ACT = mybir.ActivationFunctionType
AX_X = mybir.AxisListType.X

P = 128
D = 32
G = 4
J = 25
CH = D * J
RING = 5
LAYERS = 4
PT = 14
SH = 9
BIG = 1.0e30
LN_EPS = 1.0e-5
Z_EPS = 1.0e-6
HALF = CH // 2
M_COL, Z_COL = D, D + D // 2
LAYER3_TERMS = [(0, 0), (0, 1)] + [(c, i) for c in (1, 2, 3) for i in (2, 3, 4)] + [(c, 5) for c in range(4, 9)]


def gnn_kernel(nc, x_in, src_c, dst_c, dst_w, pattern_c, sh_c, wq, wk, wv, wo, w2, w3,
               c_ones, c_tri, c_group, c_iota, c_half, c_sel, c_expand, c_coupling, out):
    KT = x_in.shape[1]
    NCH = src_c.shape[0]
    TURNS = NCH // RING
    PIECES = KT // PT
    N_PAD = KT * P
    GE = NCH * CH
    E = G * GE
    PC = PT * D
    ROW_BYTES_SEM = 16 * J
    assert NCH % RING == 0 and KT % PT == 0

    h_table = nc.dram_tensor("h_table", [N_PAD, D], F32, kind="Internal").ap()
    q_table = nc.dram_tensor("q_table", [N_PAD, D], F32, kind="Internal").ap()
    q_edges = nc.dram_tensor("q_edges", [E + N_PAD, D], F32, kind="Internal").ap()
    sums = nc.dram_tensor("sums", [E, D], F32, kind="Internal").ap()
    attn = nc.dram_tensor("attn", [E, 2 * D], F32, kind="Internal").ap()
    q_chunks = q_edges[0:E, :].rearrange("(c p j) f -> c p (j f)", p=P, j=J)
    sums_chunks = sums.rearrange("(c p j) f -> c p (j f)", p=P, j=J)
    attn_chunks = attn.rearrange("(c p j) f -> c p (j f)", p=P, j=J)

    with ExitStack() as ctx:
        def sb(name, shape, dt=F32):
            return ctx.enter_context(nc.sbuf_tensor(name, shape, dt))

        def sem(name):
            return ctx.enter_context(nc.semaphore(name))

        def sems(name, n=RING):
            return [sem(f"{name}{r}") for r in range(n)]

        xs = sb("xs", [P, KT, D])
        hs = sb("hs", [P, KT, D])
        node_rows = sb("node_rows", [P, max(KT * 2 * D, RING * CH)])
        end_row = sb("end_row", [P, KT], I32)
        begin_row = sb("begin_row", [P, KT], I32)
        part_mask = sb("part_mask", [P, 4, KT])
        part_mean = sb("part_mean", [P, 4, KT])
        part_bias = sb("part_bias", [P, 4, KT])
        counts = sb("counts", [P, KT])
        border = sb("border", [P, 3, 2 * D])
        ln = sb("ln", [P, 4, PT])
        aw = sb("aw", [P, 6, PT])
        idx = sb("idx", [P, RING, J], I32)
        first_idx = sb("first_idx", [G, 1], I32)
        first_q = sb("first_q", [G, D])
        rows = sb("rows", [P, RING, CH])
        edge_in = sb("edge_in", [P, RING, CH])
        dwin = sb("dwin", [P, RING, CH + 1], I32)
        outs = sb("outs", [P, RING, 2 * CH])
        dst_t = sb("dst_t", [P, RING, J], I32)
        work = sb("work", [P, 14, CH])
        (hT, qT, keep, qh, prod, u, d, Z, ph, O, mz_m, mz, nb, s_sb) = (work[:, k, :] for k in range(14))
        one_hot_lo = work[:, 5:7, :].rearrange("p a c -> p (a c)").bitcast(BF16).rearrange("p (j n) -> p j n", n=P)
        one_hot_hi = work[:, 7:9, :].rearrange("p a c -> p (a c)").bitcast(BF16)[:, 0:J * KT]\
            .rearrange("p (j n) -> p j n", n=KT)
        nT, nt = work[:, 10:12, 0:PC], work[:, 12:14, 0:PC]
        mx = sb("mx", [P, CH + 1])
        carry = sb("carry", [P, 4])
        dst_lo = sb("dst_lo", [P, J], I32)
        dst_hi = sb("dst_hi", [P, J], I32)
        sh_rest = sb("sh_rest", [P, J, SH])
        sh_parts = sb("sh_parts", [P, CH], BF16)
        shT = sb("shT", [P, CH], BF16)
        weighted = [qT, qh, prod]
        ones = sb("ones", [P, P])
        tri = sb("tri", [P, P])
        group_ones = sb("group_ones", [P, P])
        iota = sb("iota", [P, P], I32)
        half = sb("half", [P, 3])
        sel = sb("sel", [P, SH, P], BF16)
        expand = sb("expand", [8, P])
        coupling = sb("coupling", [P, len(LAYER3_TERMS), D])
        eps = sb("eps", [P, 1])
        w_in = sb("w_in", [D, 4, D])
        w_t = sb("w_t", [D, 3, D])
        w_t_wide = sb("w_t_wide", [D, 2, P])
        w3_in = sb("w3_in", [8, 6, 8])
        w3_wide = sb("w3_wide", [8, 6, D])
        w3_full = sb("w3_full", [P, 6, D])
        t_sum = sb("t_sum", [P, SH, D])
        t_tmp = sb("t_tmp", [P, D])
        bd_q = sb("bd_q", [P, P])
        bd_vo = sb("bd_vo", [P, P])
        bd_w2 = sb("bd_w2", [P, P])
        bd_t = sb("bd_t", [P, SH, P])

        banks = [ctx.enter_context(nc.psum_tensor(f"bank{b}", [P, 2, 512], F32)) for b in range(4)]
        bcast = banks[0:3]
        acc = banks[3]
        node_ps = banks[0]

        consts_loaded, weights_loaded, x_loaded = sem("consts_loaded"), sem("weights_loaded"), sem("x_loaded")
        zeros_ready, q_zeroed = sem("zeros_ready"), sem("q_zeroed")
        idx_loaded, dwin_loaded, edge_loaded = sems("idx_loaded"), sems("dwin_loaded"), sems("edge_loaded")
        dst_loaded = sems("dst_loaded")
        rows_gathered = [sems(f"rows_gathered{a}_") for a in range(2)]
        chunk_begun = sem("chunk_begun")
        rows_used, edge_used, keep_ready = sems("rows_used"), sems("edge_used"), sems("keep_ready")
        outs_ready, outs_stored = sems("outs_ready"), sems("outs_stored")
        one_hot_ready, counts_ready, counts_added = sem("one_hot_ready"), sem("counts_ready"), sem("counts_added")
        prod_ready, score_ready, score_copied, nb_ready = sem("prod_ready"), sem("score_ready"), sem("score_copied"), sem("nb_ready")
        decay_in, decay_ready, p_in, p_ready = sem("decay_in"), sem("decay_ready"), sem("p_in"), sem("p_ready")
        mx_ready, mz_m_ready = sem("mx_ready"), sem("mz_m_ready")
        shT_ready = sem("shT_ready")
        bcast_ready, weighted_ready, weighted_used = sems("bcast_ready", 3), sems("weighted_ready", 3), sems("weighted_used", 3)
        msg_copied = sem("msg_copied")
        step = sem("step")
        h_ready, h_stored = sem("h_ready"), sem("h_stored")
        q_ready, q_stored, q_scattered = sem("q_ready"), sem("q_stored"), sem("q_scattered")
        first_loaded, first_gathered, first_stored = sem("first_loaded"), sem("first_gathered"), sem("first_stored")
        node_index_ready, node_gathered = sem("node_index_ready"), sems("node_gathered", PIECES)
        border_loaded = sem("border_loaded")
        prep_lhs, prep_ps = sem("prep_lhs"), sem("prep_ps")
        var_ready, std_ready = sem("var_ready"), sem("std_ready")
        part_in, part_exp = sem("part_in"), sem("part_exp")
        mix_in, mix_ps, mix_out = sem("mix_in"), sem("mix_ps"), sem("mix_out")
        x_ready, x_stored = sem("x_ready"), sem("x_stored")

        block = ctx.enter_context(nc.Block())

        def use(l, t):
            return t + (l * TURNS + 1)

        def gathers(l, t, after=1):
            return t * ROW_BYTES_SEM + ((l // 2) * TURNS + after) * ROW_BYTES_SEM

        def chunk_no(l, t, r):
            return t * RING + (l * NCH + r + 1)

        mix_count = {0: 0, 1: PIECES, 2: 2 * PIECES}

        @block.sync
        def _(sp):
            sp.dma_start(xs[:, :, :], x_in).then_inc(x_loaded, 16)
            for tile, const in ((ones, c_ones), (tri, c_tri), (group_ones, c_group), (iota, c_iota), (half, c_half),
                                (expand, c_expand)):
                sp.dma_start(tile[:, :], const).then_inc(consts_loaded, 16)
            sp.dma_start(outs[:, 0, 0:SH * P], c_sel).then_inc(consts_loaded, 16)
            sp.dma_start(coupling[:, :, :], c_coupling).then_inc(consts_loaded, 16)
            for n, w in enumerate((wq, wk, wv, wo)):
                sp.dma_start(w_in[:, n, :], w).then_inc(weights_loaded, 16)
            sp.dma_start(w3_in[:, :, :], w3.rearrange("n i o -> i n o")).then_inc(weights_loaded, 16)
            sp.wait_ge(zeros_ready, 1)
            for g in range(G):
                sp.dma_start(bd_w2[D * g:D * g + D, D * g:D * g + D], w2).then_inc(weights_loaded, 16)
            sp.dma_start(first_idx[:, :], dst_c[0, 0:P:D, 0:1], allow_slow_non_contiguous=True).then_inc(first_loaded, 16)

            def store_h(n):
                q = n % PIECES
                sp.wait_ge(h_ready, n + 1)
                sp.dma_start(h_table[q * PT * P:(q + 1) * PT * P, :].rearrange("(k p) f -> p k f", p=P),
                             hs[:, q * PT:(q + 1) * PT, :]).then_inc(h_stored, 16)

            for q in range(PIECES):
                store_h(q)
            for l in range(LAYERS):
                for r in range(RING):
                    if l >= 1:
                        sp.wait_ge(rows_gathered[(l - 1) % 2][r], gathers(l - 1, 0, TURNS))
                with sp.Fori(0, TURNS) as t:
                    for r in range(RING):
                        c = bass.ds(t * RING + r, 1)
                        sp.wait_ge(rows_gathered[l % 2][r], gathers(l, t, 0))
                        sp.dma_start(idx[:, r, :], src_c[c].rearrange("o p j -> (o p) j")).then_inc(idx_loaded[r], 16)
                        sp.wait_ge(keep_ready[r], use(l, t) - 1)
                        for g in range(G):
                            sp.dma_start(dwin[D * g:D * g + D, r, :],
                                         dst_w[c, g, :].broadcast_to([D, CH + 1])).then_inc(dwin_loaded[r], 16)
                        if l == 0:
                            sp.wait_ge(rows_used[r], t)
                            sp.dma_start(edge_in[:, r, :], pattern_c[c].rearrange("o p c -> (o p) c")).then_inc(edge_loaded[r], 16)
                            sp.wait_ge(one_hot_ready, t * RING)
                            sp.dma_start(dst_t[:, r, :], dst_c[c].rearrange("o p j -> (o p) j")).then_inc(dst_loaded[r], 16)
                        if l == 1:
                            sp.wait_ge(first_stored, 16)
                            sp.wait_ge(edge_used[r], t)
                            sp.dma_start(edge_in[:, r, :], q_chunks[c].rearrange("o p c -> (o p) c")).then_inc(edge_loaded[r], 16)
                        if l == 3:
                            sp.wait_ge(edge_used[r], t + TURNS)
                            sp.dma_start(edge_in[:, r, 0:J * SH], sh_c[c].rearrange("o p c -> (o p) c")).then_inc(edge_loaded[r], 16)
                for r in range(RING):
                    sp.wait_ge(outs_stored[r], 16 * (l + 1) * TURNS)
                if l == 1:
                    last = attn_chunks[NCH - 1:NCH, D - 1:3 * D:D, (J - 1) * 2 * D:J * 2 * D]
                    sp.dma_start(border[:, :, :], last.broadcast_to([P, 3, 2 * D])).then_inc(border_loaded, 16)
                else:
                    last = sums_chunks[NCH - 1:NCH, D - 1:3 * D:D, (J - 1) * D:J * D]
                    sp.dma_start(border[:, :, 0:D], last.broadcast_to([P, 3, D])).then_inc(border_loaded, 16)
                for q in range(PIECES):
                    if l < LAYERS - 1:
                        store_h((l + 1) * PIECES + q)
                    if l == 0:
                        sp.wait_ge(q_ready, q + 1)
                        sp.dma_start(q_table[q * PT * P:(q + 1) * PT * P, :].rearrange("(k p) f -> p k f", p=P),
                                     node_rows[:, q * PC:(q + 1) * PC].rearrange("p (k f) -> p k f", f=D)).then_inc(q_stored, 16)
                    if l == LAYERS - 1:
                        sp.wait_ge(x_ready, q + 1)
                        sp.dma_start(out[:, q * PT:(q + 1) * PT, :], xs[:, q * PT:(q + 1) * PT, :]).then_inc(x_stored, 16)
            sp.wait_ge(x_stored, 16 * PIECES)

        @block.gpsimd
        def _(pool):
            for l in range(LAYERS):
                if l == 1:
                    pool.wait_ge(q_zeroed, 16 * TURNS)
                    for q in range(PIECES):
                        pool.wait_ge(q_ready, q + 1)
                        for k in range(q * PT, (q + 1) * PT):
                            nc.gpsimd.indirect_dma_start(
                                out=q_edges[:, :], out_offset=bass.IndirectOffsetOnAxis(ap=begin_row[:, k:k + 1], axis=0),
                                in_=node_rows[:, k * D:(k + 1) * D], in_offset=None).then_inc(q_scattered, 16)
                    pool.wait_ge(first_loaded, 16)
                    pool.wait_ge(q_stored, 16 * PIECES)
                    nc.gpsimd.indirect_dma_start(
                        out=first_q[:, :], out_offset=None, in_=q_table[:, :],
                        in_offset=bass.IndirectOffsetOnAxis(ap=first_idx[:, :], axis=0)).then_inc(first_gathered, 16)
                    pool.wait_ge(first_gathered, 16)
                    pool.wait_ge(q_scattered, 16 * KT)
                    pool.dma_start(q_chunks[0, 0:P:D, 0:D], first_q[:, :]).then_inc(first_stored, 16)
                pool.wait_ge(h_stored, 16 * PIECES * (l + 1))
                with pool.Fori(0, TURNS) as t:
                    for r in range(RING):
                        pool.wait_ge(rows_used[r], use(l, t) - 1)
                        pool.wait_ge(idx_loaded[r], use(l, t) * 16)
                        pool.sem_inc(chunk_begun, 1)
                        for j in range(J):
                            nc.gpsimd.indirect_dma_start(
                                out=rows[:, r, j * D:(j + 1) * D], out_offset=None, in_=h_table[:, :],
                                in_offset=bass.IndirectOffsetOnAxis(ap=idx[:, r, j:j + 1], axis=0)).then_inc(rows_gathered[l % 2][r], 16)
                if l == 0:
                    pool.wait_ge(node_index_ready, 1)
                for r in range(RING):
                    pool.wait_ge(outs_stored[r], 16 * (l + 1) * TURNS)
                table, width = (attn, 2 * D) if l == 1 else (sums, D)
                for k in range(KT):
                    nc.gpsimd.indirect_dma_start(
                        out=node_rows[:, k * width:(k + 1) * width], out_offset=None, in_=table[:, :],
                        in_offset=bass.IndirectOffsetOnAxis(ap=end_row[:, k:k + 1], axis=0)).then_inc(node_gathered[k // PT], 16)

        @block.scalar
        def _(act):
            def std(n):
                act.wait_ge(var_ready, n + 1)
                nc.scalar.activation(ln[:, 2, :], ln[:, 1, :], ACT.Sqrt, bias=eps[:, :], scale=1.0 / D).then_inc(std_ready, 1)

            def mix_copy(n, scale):
                act.wait_ge(mix_ps, n + 1)
                nc.scalar.activation(nT[:, 1, :], node_ps[:, 0, 0:PC], ACT.Copy, scale=scale).then_inc(mix_out, 1)

            def store(l, t, r, chunks, width):
                act.wait_ge(outs_ready[r], use(l, t))
                act.dma_start(chunks[bass.ds(t * RING + r, 1)].rearrange("o p c -> (o p) c"),
                              outs[:, r, 0:width]).then_inc(outs_stored[r], 16)

            for q in range(PIECES):
                std(q)
            act.wait_ge(zeros_ready, 1)
            with act.Fori(0, TURNS) as t:
                act.dma_start(q_edges[bass.ds(t * (RING * P * J), RING * P * J), :].rearrange("(p a) f -> p (a f)", p=P),
                              node_rows[:, 0:RING * CH]).then_inc(q_zeroed, 16)
                for r in range(RING):
                    store(0, t, r, sums_chunks, CH)
            for q in range(PIECES):
                std(PIECES + q)
                mix_copy(q, float(D) ** -0.5)
            with act.Fori(0, TURNS) as t:
                for r in range(RING):
                    n = chunk_no(0, t, r)
                    act.wait_ge(keep_ready[r], use(1, t))
                    nc.scalar.activation(nb, keep, ACT.Copy, scale=BIG, bias=-BIG).then_inc(nb_ready, 1)
                    act.wait_ge(score_ready, n)
                    nc.scalar.activation(s_sb.rearrange("p (a c) -> p a c", a=2), acc[:, :, 0:HALF], ACT.Copy).then_inc(score_copied, 1)
                    act.wait_ge(decay_in, n)
                    nc.scalar.activation(u, u, ACT.Exp).then_inc(decay_ready, 1)
                    act.wait_ge(p_in, n)
                    nc.scalar.activation(d, d, ACT.Exp).then_inc(p_ready, 1)
                    act.wait_ge(mx_ready, n)
                    nc.scalar.activation(mz_m, mx[:, 1:CH + 1], ACT.Copy, scale=half[:, 0:1]).then_inc(mz_m_ready, 1)
                    store(1, t, r, attn_chunks, 2 * CH)
            for q in range(PIECES):
                act.wait_ge(part_in, q + 1)
                nc.scalar.activation(aw[:, 0:4, :], aw[:, 0:4, :], ACT.Exp).then_inc(part_exp, 1)
                mix_copy(PIECES + q, 1.0)
                std(2 * PIECES + q)
            with act.Fori(0, TURNS) as t:
                for r in range(RING):
                    store(2, t, r, sums_chunks, CH)
            for q in range(PIECES):
                mix_copy(2 * PIECES + q, 1.0)
                std(3 * PIECES + q)
            with act.Fori(0, TURNS) as t:
                for r in range(RING):
                    act.wait_ge(weighted_used[2], t * (3 * RING) + (3 * r + 3))
                    nc.scalar.activation(s_sb.rearrange("p (a c) -> p a c", a=2), acc[:, :, 0:HALF], ACT.Copy).then_inc(msg_copied, 1)
                    store(3, t, r, sums_chunks, CH)

        @block.tensor
        def _(pe):
            pe.wait_ge(prep_lhs, 1)
            nc.tensor.matmul(acc[:, 0, 0:D], w_t_wide[:, 0, :], w_t[:, 1, :], start=True, stop=True)
            nc.tensor.matmul(acc[:, 0, D:2 * D], w_t_wide[:, 1, :], w_in[:, 3, :], start=True, stop=True)
            nc.tensor.matmul(acc[:, 1, 0:6 * D], expand[:, :], w3_wide[:, :, :], start=True, stop=True).then_inc(prep_ps, 1)
            pe.wait_ge(prep_lhs, 2)
            with pe.Fori(0, TURNS) as t:
                for r in range(RING):
                    pe.wait_ge(one_hot_ready, chunk_no(0, t, r))
                    pe.wait_ge(counts_added, t * RING + r)
                    for j in range(J):
                        last = nc.tensor.matmul(acc[:, 0, 0:KT], one_hot_lo[:, j, :], one_hot_hi[:, j, :],
                                                start=(j == 0), stop=(j == J - 1))
                    last.then_inc(counts_ready, 1)
            pe.wait_ge(counts_added, NCH)
            nc.tensor.matmul(acc[:, 0, 0:KT], tri[:, :], counts[:, :], start=True, stop=True)
            nc.tensor.matmul(acc[:, 1, 0:KT], ones[:, :], counts[:, :], start=True, stop=True).then_inc(prep_ps, 1)

            def mix(n, weight):
                pe.wait_ge(mix_in, n + 1)
                nc.tensor.matmul(node_ps[:, 0, 0:PC], weight[:, :], nT[:, 0, :], start=True, stop=True).then_inc(mix_ps, 1)

            for q in range(PIECES):
                mix(q, bd_q)
            with pe.Fori(0, TURNS) as t:
                for r in range(RING):
                    pe.wait_ge(prod_ready, chunk_no(0, t, r))
                    pe.wait_ge(score_copied, t * RING + r)
                    for a in range(2):
                        last = nc.tensor.matmul(acc[:, a, 0:HALF], group_ones[:, :], prod[:, a * HALF:(a + 1) * HALF],
                                                start=True, stop=True)
                    last.then_inc(score_ready, 1)
            for q in range(PIECES):
                mix(PIECES + q, bd_vo)
            for q in range(PIECES):
                mix(2 * PIECES + q, bd_w2)

            def spread(t, r, c):
                pe.wait_ge(weighted_ready[c % 3], t * (3 * RING) + (3 * r + c // 3))
                if c == 0:
                    pe.wait_ge(shT_ready, chunk_no(0, t, r))
                for a in range(2):
                    last = nc.tensor.matmul(bcast[c % 3][:, a, 0:HALF], sel[:, c, :], shT[:, a * HALF:(a + 1) * HALF],
                                            start=True, stop=True)
                last.then_inc(bcast_ready[c % 3], 1)

            def couple(t, r, c):
                pe.wait_ge(weighted_ready[c % 3], t * (3 * RING) + (3 * r + c // 3 + 1))
                if c == 0:
                    pe.wait_ge(msg_copied, t * RING + r)
                for a in range(2):
                    last = nc.tensor.matmul(acc[:, a, 0:HALF], bd_t[:, c, :], weighted[c % 3][:, a * HALF:(a + 1) * HALF],
                                            start=(c == 0), stop=(c == SH - 1))
                last.then_inc(weighted_used[c % 3], 1)
                return last

            with pe.Fori(0, TURNS) as t:
                for r in range(RING):
                    for c in range(SH):
                        spread(t, r, c)
                        if c >= 1:
                            couple(t, r, c - 1)
                    couple(t, r, SH - 1)

        @block.vector
        def _(v):
            steps = [0]

            def link(ins):
                steps[0] += 1
                ins.then_inc(step, 1)
                v.wait_ge(step, steps[0])

            def by_edge(ap):
                return ap.rearrange("p (i j) -> p j i", j=J)

            def spread_over(ap, n):
                return ap.unsqueeze(2).broadcast_to([P, ap.shape[1], n])

            nc.vector.memset(bd_w2[:, :], 0.0)
            link(nc.vector.memset(node_rows[:, 0:RING * CH], 0.0))
            nc.vector.memset(carry[:, :], 0.0).then_inc(zeros_ready, 1)
            nc.vector.memset(eps[:, :], LN_EPS)
            nc.vector.memset(bd_q[:, :], 0.0)
            nc.vector.memset(bd_vo[:, :], 0.0)
            nc.vector.memset(bd_t[:, :, :], 0.0)
            nc.vector.memset(counts[:, :], 0.0)
            link(nc.vector.memset(sh_parts[:, :], 0.0))

            def layer_norm(n, q):
                x = xs[:, q * PT:(q + 1) * PT, :]
                xc = nt[:, 0, :].rearrange("p (k f) -> p k f", f=D)
                sq = nt[:, 1, :].rearrange("p (k f) -> p k f", f=D)
                link(nc.vector.reduce_sum(ln[:, 0, :], x, axis=AX_X))
                link(nc.vector.tensor_scalar(ln[:, 0, :], ln[:, 0, :], -1.0 / D, None, ALU.mult))
                link(nc.vector.tensor_tensor(xc, x, spread_over(ln[:, 0, :], D), ALU.add))
                link(nc.vector.tensor_tensor(sq, xc, xc, ALU.mult))
                nc.vector.reduce_sum(ln[:, 1, :], sq, axis=AX_X).then_inc(var_ready, 1)
                v.wait_ge(std_ready, n + 1)
                link(nc.vector.reciprocal(ln[:, 3, :], ln[:, 2, :]))
                nc.vector.scalar_tensor_tensor(out=hs[:, q * PT:(q + 1) * PT, :], in0=xc, scalar=0.0,
                                               in1=spread_over(ln[:, 3, :], D), op0=ALU.max, op1=ALU.mult).then_inc(h_ready, 1)

            v.wait_ge(x_loaded, 16)
            for q in range(PIECES):
                layer_norm(q, q)
                v.wait_ge(h_ready, q + 1)

            v.wait_ge(consts_loaded, 8 * 16)
            v.wait_ge(weights_loaded, (5 + G) * 16)
            nc.vector.tensor_copy(sel[:, :, :].rearrange("p c m -> p (c m)"), outs[:, 0, 0:SH * P])
            for n in range(3):
                nc.vector.transpose(w_t[:, n, :], w_in[:, n, :])
            nc.vector.tensor_copy(w3_wide[:, :, 0:8], w3_in[:, :, :])
            for k in range(3):
                last = nc.vector.tensor_copy(w3_wide[:, :, 8 + k:D:3], w3_in[:, :, :])
            link(last)
            for n, m in ((0, 0), (1, 2)):
                last = nc.vector.tensor_copy(w_t_wide[:, n, :].rearrange("p (g f) -> p g f", g=G),
                                             w_t[:, m:m + 1, :].broadcast_to([D, G, D]))
            last.then_inc(prep_lhs, 1)
            v.wait_ge(prep_ps, 1)
            for g in range(G):
                q = slice(D * g, D * g + D)
                nc.vector.tensor_copy(bd_q[q, q], acc[q, 0, 0:D])
                nc.vector.tensor_copy(bd_vo[q, q], acc[q, 0, D:2 * D])
            link(nc.vector.tensor_copy(w3_full[:, :, :].rearrange("p n f -> p (n f)"), acc[:, 1, 0:6 * D]))
            seen = set()
            for n, (c, i) in enumerate(LAYER3_TERMS):
                to = t_tmp[:, :] if c in seen else t_sum[:, c, :]
                link(nc.vector.tensor_tensor(to, w3_full[:, i, :], coupling[:, n, :], ALU.mult))
                if c in seen:
                    link(nc.vector.tensor_tensor(t_sum[:, c, :], t_sum[:, c, :], t_tmp[:, :], ALU.add))
                seen.add(c)
            for g in range(G):
                q = slice(D * g, D * g + D)
                last = nc.vector.tensor_copy(bd_t[q, :, q], t_sum[q, :, :])
            link(last)
            nc.vector.memset(aw[:, :, :], 0.0).then_inc(prep_lhs, 1)

            def start_chunk(l, t, r):
                v.wait_ge(dwin_loaded[r], use(l, t) * (16 * G))
                nc.vector.tensor_tensor(keep, dwin[:, r, 1:CH + 1], dwin[:, r, 0:CH], ALU.is_equal).then_inc(keep_ready[r], 1)

            steps0 = steps[0]
            per_chunk = 4
            with v.Fori(0, TURNS) as t:
                for r in range(RING):
                    at = [0]

                    def then(ins, r=r, at=at, t=t):
                        at[0] += 1
                        ins.then_inc(step, 1)
                        v.wait_ge(step, t * (RING * per_chunk) + (steps0 + r * per_chunk + at[0]))

                    start_chunk(0, t, r)
                    v.wait_ge(dst_loaded[r], use(0, t) * 16)
                    nc.vector.tensor_scalar(dst_lo[:, :], dst_t[:, r, :], P - 1, None, ALU.bitwise_and)
                    then(nc.vector.tensor_scalar(dst_hi[:, :], dst_t[:, r, :], P.bit_length() - 1, None, ALU.logical_shift_right))
                    nc.vector.tensor_tensor(one_hot_lo, dst_lo[:, :].unsqueeze(2).broadcast_to([P, J, P]),
                                            iota[:, :].unsqueeze(1).broadcast_to([P, J, P]), ALU.is_equal)
                    nc.vector.tensor_tensor(one_hot_hi, dst_hi[:, :].unsqueeze(2).broadcast_to([P, J, KT]),
                                            iota[:, 0:KT].unsqueeze(1).broadcast_to([P, J, KT]), ALU.is_equal).then_inc(one_hot_ready, 1)
                    v.wait_ge(rows_gathered[0][r], gathers(0, t))
                    v.wait_ge(edge_loaded[r], use(0, t) * 16)
                    nc.vector.tensor_tensor(prod, rows[:, r, :], edge_in[:, r, :], ALU.mult).then_inc(rows_used[r], 1)
                    v.wait_ge(rows_used[r], use(0, t))
                    then(nc.vector.transpose(by_edge(hT), prod))
                    then(nc.vector.tensor_tensor_scan(O, keep, hT, carry[:, 3:4], ALU.mult, ALU.add))
                    then(nc.vector.tensor_copy(carry[:, 3:4], O[:, CH - 1:CH]))
                    v.wait_ge(outs_stored[r], (use(0, t) - 1) * 16)
                    nc.vector.transpose(outs[:, r, 0:CH], by_edge(O)).then_inc(outs_ready[r], 1)
                    v.wait_ge(counts_ready, chunk_no(0, t, r))
                    v.wait_ge(counts_added, t * RING + r)
                    nc.vector.tensor_tensor(counts[:, :], counts[:, :], acc[:, 0, 0:KT], ALU.add).then_inc(counts_added, 1)
                    assert at[0] == per_chunk
            steps[0] += NCH * per_chunk

            v.wait_ge(prep_ps, 2)
            v.wait_ge(q_zeroed, 16 * TURNS)
            A = [node_rows[:, k * KT:(k + 1) * KT] for k in range(8)]
            end, begin, e, grp, a, b, ne, no = A
            link(nc.vector.tensor_copy(b, acc[:, 1, 0:KT]))
            link(nc.vector.memset(a, 1.0))
            link(nc.vector.tensor_tensor_scan(e, a, b, 0.0, ALU.mult, ALU.add))
            link(nc.vector.tensor_tensor(e, e, b, ALU.subtract))
            link(nc.vector.tensor_tensor(end, e, acc[:, 0, 0:KT], ALU.add))
            link(nc.vector.tensor_tensor(begin, end, counts[:, :], ALU.subtract))
            link(nc.vector.tensor_scalar(ne, counts[:, :], 0.5, None, ALU.is_ge))
            link(nc.vector.tensor_copy(part_mask[:, 0, :], ne))
            for g in range(3):
                link(nc.vector.tensor_scalar(a, begin, float((g + 1) * GE) - 0.5, None, ALU.is_lt))
                link(nc.vector.tensor_scalar(b, end, float((g + 1) * GE) + 0.5, None, ALU.is_gt))
                link(nc.vector.tensor_tensor(part_mask[:, g + 1, :], a, b, ALU.mult))
            link(nc.vector.tensor_scalar(part_bias[:, :, :], part_mask[:, :, :], BIG, -BIG, ALU.mult, ALU.add))
            link(nc.vector.tensor_scalar(a, counts[:, :], 1.0, None, ALU.max))
            link(nc.vector.reciprocal(b, a))
            link(nc.vector.tensor_tensor(part_mean[:, :, :], part_mask[:, :, :],
                                         b.unsqueeze(1).broadcast_to([P, 4, KT]), ALU.mult))

            def row_of(edge):
                link(nc.vector.tensor_scalar(grp, edge, float(GE) - 0.5, None, ALU.is_gt))
                for g in range(2, G):
                    link(nc.vector.tensor_scalar(a, edge, float(g * GE) - 0.5, None, ALU.is_gt))
                    link(nc.vector.tensor_tensor(grp, grp, a, ALU.add))
                link(nc.vector.scalar_tensor_tensor(out=edge, in0=grp, scalar=-float(GE), in1=edge, op0=ALU.mult, op1=ALU.add))
                link(nc.vector.tensor_scalar(a, edge, 1.0 / CH, 0.5 / CH - 0.5, ALU.mult, ALU.add))
                link(nc.vector.tensor_scalar(a, a, 2.0 ** 23 + 2.0 ** 22, None, ALU.add))
                link(nc.vector.tensor_scalar(a, a, -(2.0 ** 23 + 2.0 ** 22), None, ALU.add))
                link(nc.vector.scalar_tensor_tensor(out=edge, in0=a, scalar=float((G - 1) * CH), in1=edge, op0=ALU.mult, op1=ALU.add))
                link(nc.vector.scalar_tensor_tensor(out=edge, in0=grp, scalar=float(CH), in1=edge, op0=ALU.mult, op1=ALU.add))

            link(nc.vector.tensor_scalar(e, end, -1.0, 0.0, ALU.add, ALU.max))
            row_of(e)
            link(nc.vector.tensor_copy(end_row[:, :], e))
            link(nc.vector.tensor_scalar(begin, begin, float(E - 1), None, ALU.min))
            row_of(begin)
            link(nc.vector.tensor_copy(no, iota[:, 0:KT]))
            link(nc.vector.tensor_scalar(no, no, float(P), float(E), ALU.mult, ALU.add))
            link(nc.vector.tensor_scalar(no, no, half[:, 2:3], None, ALU.add))
            link(nc.vector.tensor_tensor(a, begin, no, ALU.subtract))
            link(nc.vector.tensor_tensor(a, a, ne, ALU.mult))
            link(nc.vector.tensor_tensor(a, a, no, ALU.add))
            nc.vector.tensor_copy(begin_row[:, :], a).then_inc(node_index_ready, 1)
            v.wait_ge(node_index_ready, 1)

            def piece(q, width=D, at=0):
                return node_rows[:, q * PT * width:(q + 1) * PT * width].rearrange("p (k f) -> p k f", f=width)[:, :, at:at + D]

            agg = nt[:, 0, :].rearrange("p (k f) -> p k f", f=D)
            part = nt[:, 1, :].rearrange("p (k f) -> p k f", f=D)

            def parts_sum(rows_of_piece, weights):
                link(nc.vector.tensor_tensor(agg, rows_of_piece, spread_over(weights[:, 0, :], D), ALU.mult))
                for g in range(3):
                    link(nc.vector.tensor_tensor(part, spread_over(weights[:, g + 1, :], D),
                                                 border[:, g:g + 1, 0:D].broadcast_to([P, PT, D]), ALU.mult))
                    link(nc.vector.tensor_tensor(agg, agg, part, ALU.add))

            def mixed(n, rows_in, rows_out):
                nc.vector.transpose(nT[:, 0, :], rows_in).then_inc(mix_in, 1)
                v.wait_ge(mix_out, n + 1)
                return nc.vector.transpose(rows_out, nT[:, 1, :])

            def node_start(l, q):
                if q == 0:
                    v.wait_ge(border_loaded, 16 * (l + 1))
                v.wait_ge(node_gathered[q], 16 * PT * (l + 1))
                return xs[:, q * PT:(q + 1) * PT, :], slice(q * PT, (q + 1) * PT)

            for q in range(PIECES):
                x, ks = node_start(0, q)
                parts_sum(piece(q), part_mean[:, :, ks])
                link(nc.vector.tensor_tensor(agg, agg, hs[:, ks, :], ALU.add))
                link(nc.vector.tensor_tensor(x, x, agg, ALU.add))
                layer_norm(PIECES + q, q)
                v.wait_ge(h_ready, PIECES + q + 1)
                mixed(q, hs[:, ks, :].rearrange("p k f -> p (k f)"), node_rows[:, q * PC:(q + 1) * PC]).then_inc(q_ready, 1)
                v.wait_ge(q_ready, q + 1)

            nc.vector.memset(mx[:, 0:1], -BIG)
            link(nc.vector.memset(carry[:, :], 0.0))
            steps1 = steps[0]
            per_chunk1 = 11
            with v.Fori(0, TURNS) as t:
                for r in range(RING):
                    at = [0]

                    def then(ins, r=r, at=at, t=t):
                        at[0] += 1
                        ins.then_inc(step, 1)
                        v.wait_ge(step, t * (RING * per_chunk1) + (steps1 + r * per_chunk1 + at[0]))

                    n = chunk_no(0, t, r)
                    start_chunk(1, t, r)
                    v.wait_ge(rows_gathered[1][r], gathers(1, t))
                    nc.vector.transpose(by_edge(hT), rows[:, r, :]).then_inc(rows_used[r], 1)
                    v.wait_ge(edge_loaded[r], use(1, t) * 16)
                    nc.vector.transpose(by_edge(qT), edge_in[:, r, :]).then_inc(edge_used[r], 1)
                    v.wait_ge(edge_used[r], t + 1)
                    then(nc.vector.tensor_tensor_scan(qh, keep, qT, carry[:, 0:1], ALU.mult, ALU.add))
                    nc.vector.tensor_tensor(prod, qh, hT, ALU.mult).then_inc(prod_ready, 1)
                    then(nc.vector.tensor_copy(carry[:, 0:1], qh[:, CH - 1:CH]))
                    v.wait_ge(nb_ready, n)
                    v.wait_ge(score_copied, n)
                    nc.vector.tensor_tensor_scan(mx[:, 1:CH + 1], nb, s_sb, mx[:, 0:1], ALU.add, ALU.max).then_inc(mx_ready, 1)
                    v.wait_ge(mx_ready, n)
                    then(nc.vector.tensor_tensor(u, mx[:, 0:CH], nb, ALU.add))
                    nc.vector.tensor_tensor(u, u, mx[:, 1:CH + 1], ALU.subtract).then_inc(decay_in, 1)
                    nc.vector.tensor_tensor(d, s_sb, mx[:, 1:CH + 1], ALU.subtract).then_inc(p_in, 1)
                    v.wait_ge(decay_ready, n)
                    v.wait_ge(p_ready, n)
                    then(nc.vector.tensor_tensor(ph, d, hT, ALU.mult))
                    then(nc.vector.tensor_tensor_scan(Z, u, d, carry[:, 1:2], ALU.mult, ALU.add))
                    then(nc.vector.tensor_tensor_scan(O, u, ph, carry[:, 2:3], ALU.mult, ALU.add))
                    then(nc.vector.tensor_copy(carry[:, 1:2], Z[:, CH - 1:CH]))
                    then(nc.vector.tensor_copy(carry[:, 2:3], O[:, CH - 1:CH]))
                    v.wait_ge(mz_m_ready, n)
                    then(nc.vector.tensor_copy(mx[:, 0:1], mx[:, CH:CH + 1]))
                    then(nc.vector.scalar_tensor_tensor(out=mz, in0=Z, scalar=half[:, 1:2], in1=mz_m, op0=ALU.mult, op1=ALU.add))
                    v.wait_ge(outs_stored[r], (use(1, t) - 1) * 16)
                    row = outs[:, r, :].rearrange("p (j f) -> p j f", j=J)
                    then(nc.vector.transpose(row[:, :, 0:D], by_edge(O)))
                    nc.vector.transpose(row[:, :, D:2 * D], by_edge(mz)).then_inc(outs_ready[r], 1)
                    assert at[0] == per_chunk1
            steps[0] += NCH * per_chunk1

            for q in range(PIECES):
                x, ks = node_start(1, q)
                at_m, at_z = piece(q, 2 * D, D)[:, :, 0], piece(q, 2 * D, D)[:, :, Z_COL - M_COL]
                w, top, z = aw[:, 0:4, :], aw[:, 4, :], aw[:, 5, :]
                link(nc.vector.tensor_tensor(w[:, 0, :], at_m, part_mask[:, 0, ks], ALU.mult))
                link(nc.vector.tensor_tensor(w[:, 0, :], w[:, 0, :], part_bias[:, 0, ks], ALU.add))
                link(nc.vector.tensor_copy(top, w[:, 0, :]))
                for g in range(3):
                    link(nc.vector.scalar_tensor_tensor(out=w[:, g + 1, :], in0=part_mask[:, g + 1, ks], scalar=border[:, g, M_COL:M_COL + 1],
                                                        in1=part_bias[:, g + 1, ks], op0=ALU.mult, op1=ALU.add))
                    link(nc.vector.tensor_tensor(top, top, w[:, g + 1, :], ALU.max))
                nc.vector.tensor_tensor(w, w, top.unsqueeze(1).broadcast_to([P, 4, PT]), ALU.subtract).then_inc(part_in, 1)
                v.wait_ge(part_exp, q + 1)
                link(nc.vector.tensor_tensor(w, w, part_mask[:, :, ks], ALU.mult))
                link(nc.vector.tensor_tensor(z, w[:, 0, :], at_z, ALU.mult))
                for g in range(3):
                    link(nc.vector.scalar_tensor_tensor(out=z, in0=w[:, g + 1, :], scalar=border[:, g, Z_COL:Z_COL + 1], in1=z,
                                                        op0=ALU.mult, op1=ALU.add))
                link(nc.vector.tensor_scalar(z, z, Z_EPS, None, ALU.add))
                link(nc.vector.reciprocal(top, z))
                link(nc.vector.tensor_tensor(w, w, top.unsqueeze(1).broadcast_to([P, 4, PT]), ALU.mult))
                parts_sum(piece(q, 2 * D), w)
                link(mixed(PIECES + q, nt[:, 0, :], nt[:, 1, :]))
                link(nc.vector.tensor_tensor(agg, part, hs[:, ks, :], ALU.add))
                link(nc.vector.tensor_tensor(x, x, agg, ALU.add))
                layer_norm(2 * PIECES + q, q)
                v.wait_ge(h_ready, 2 * PIECES + q + 1)

            def plain_chunk(l, t, r, messages, then):
                then(nc.vector.tensor_tensor_scan(O, keep, messages, carry[:, 3:4], ALU.mult, ALU.add))
                then(nc.vector.tensor_copy(carry[:, 3:4], O[:, CH - 1:CH]))
                v.wait_ge(outs_stored[r], (use(l, t) - 1) * 16)
                nc.vector.transpose(outs[:, r, 0:CH], by_edge(O)).then_inc(outs_ready[r], 1)
                v.wait_ge(outs_ready[r], use(l, t))

            link(nc.vector.memset(carry[:, :], 0.0))
            steps2 = steps[0]
            per_chunk2 = 2
            with v.Fori(0, TURNS) as t:
                for r in range(RING):
                    at = [0]

                    def then(ins, r=r, at=at, t=t):
                        at[0] += 1
                        ins.then_inc(step, 1)
                        v.wait_ge(step, t * (RING * per_chunk2) + (steps2 + r * per_chunk2 + at[0]))

                    start_chunk(2, t, r)
                    v.wait_ge(rows_gathered[0][r], gathers(2, t))
                    nc.vector.transpose(by_edge(hT), rows[:, r, :]).then_inc(rows_used[r], 1)
                    v.wait_ge(rows_used[r], use(2, t))
                    plain_chunk(2, t, r, hT, then)
                    assert at[0] == per_chunk2
            steps[0] += NCH * per_chunk2

            for q in range(PIECES):
                x, ks = node_start(2, q)
                parts_sum(piece(q), part_mask[:, :, ks])
                link(mixed(2 * PIECES + q, nt[:, 0, :], nt[:, 1, :]))
                link(nc.vector.tensor_tensor(x, x, part, ALU.add))
                layer_norm(3 * PIECES + q, q)
                v.wait_ge(h_ready, 3 * PIECES + q + 1)

            link(nc.vector.memset(carry[:, :], 0.0))
            steps3 = steps[0]
            per_chunk3 = 5
            sh3 = sh_parts[:, :].rearrange("p (j c) -> p j c", c=D)
            with v.Fori(0, TURNS) as t:
                for r in range(RING):
                    at = [0]

                    def then(ins, r=r, at=at, t=t):
                        at[0] += 1
                        ins.then_inc(step, 1)
                        v.wait_ge(step, t * (RING * per_chunk3) + (steps3 + r * per_chunk3 + at[0]))

                    start_chunk(3, t, r)
                    v.wait_ge(edge_loaded[r], (t + (2 * TURNS + 1)) * 16)
                    sh_f = edge_in[:, r, 0:J * SH].rearrange("p (j c) -> p j c", c=SH)
                    then(nc.vector.tensor_copy(sh3[:, :, 0:SH], sh_f))
                    nc.vector.tensor_tensor(sh_rest[:, :, :], sh_f, sh3[:, :, 0:SH], ALU.subtract).then_inc(edge_used[r], 1)
                    v.wait_ge(edge_used[r], t + (TURNS + 1))
                    then(nc.vector.tensor_copy(sh3[:, :, SH:2 * SH], sh_rest[:, :, :]))
                    then(nc.vector.tensor_tensor(sh3[:, :, 2 * SH:3 * SH], sh_rest[:, :, :], sh3[:, :, SH:2 * SH], ALU.subtract))
                    v.wait_ge(bcast_ready[2], t * (3 * RING) + 3 * r)
                    nc.vector.transpose(by_edge(shT[:, :]), sh_parts[:, :]).then_inc(shT_ready, 1)
                    v.wait_ge(rows_gathered[1][r], gathers(3, t))
                    nc.vector.transpose(by_edge(hT), rows[:, r, :]).then_inc(rows_used[r], 1)
                    v.wait_ge(rows_used[r], use(3, t))
                    for c in range(SH):
                        use3 = t * (3 * RING) + (3 * r + c // 3)
                        v.wait_ge(bcast_ready[c % 3], use3 + 1)
                        v.wait_ge(weighted_used[c % 3], use3)
                        nc.vector.tensor_tensor(weighted[c % 3].rearrange("p (a c) -> p a c", a=2), bcast[c % 3][:, :, 0:HALF],
                                                hT.rearrange("p (a c) -> p a c", a=2), ALU.mult).then_inc(weighted_ready[c % 3], 1)
                    v.wait_ge(msg_copied, chunk_no(0, t, r))
                    plain_chunk(3, t, r, s_sb, then)
                    assert at[0] == per_chunk3
            steps[0] += NCH * per_chunk3

            for q in range(PIECES):
                x, ks = node_start(3, q)
                parts_sum(piece(q), part_mask[:, :, ks])
                nc.vector.tensor_tensor(x, x, agg, ALU.add).then_inc(x_ready, 1)
                v.wait_ge(x_ready, q + 1)


def coupling_coefficients():
    f = math.factorial

    def coefficient(j1, m1, j2, m2, j3, m3):
        if m3 != m1 + m2:
            return 0.0
        pref = (2 * j3 + 1) * f(j3 + j1 - j2) * f(j3 - j1 + j2) * f(j1 + j2 - j3) / f(j1 + j2 + j3 + 1)
        pref *= f(j3 + m3) * f(j3 - m3) * f(j1 - m1) * f(j1 + m1) * f(j2 - m2) * f(j2 + m2)
        s = 0.0
        for k in range(max(0, j2 - j3 - m1, j1 + m2 - j3), min(j1 + j2 - j3, j1 - m1, j2 + m2) + 1):
            s += (-1) ** k / (f(k) * f(j1 + j2 - j3 - k) * f(j1 - m1 - k) * f(j2 + m2 - k)
                              * f(j3 - j2 + m1 + k) * f(j3 - j1 - m2 + k))
        return math.sqrt(pref) * s

    def complex_cg(l1, l2, l3):
        C = np.zeros((2 * l1 + 1, 2 * l2 + 1, 2 * l3 + 1), np.complex128)
        for m1 in range(-l1, l1 + 1):
            for m2 in range(-l2, l2 + 1):
                if -l3 <= m1 + m2 <= l3:
                    C[m1 + l1, m2 + l2, m1 + m2 + l3] = coefficient(l1, m1, l2, m2, l3, m1 + m2)
        return C

    def to_real(l):
        q = np.zeros((2 * l + 1, 2 * l + 1), np.complex128)
        for m in range(-l, 0):
            q[l + m, l + abs(m)] = 1 / np.sqrt(2)
            q[l + m, l - abs(m)] = -1j / np.sqrt(2)
        q[l, l] = 1.0
        for m in range(1, l + 1):
            q[l + m, l + abs(m)] = (-1) ** m / np.sqrt(2)
            q[l + m, l - abs(m)] = 1j * (-1) ** m / np.sqrt(2)
        return (-1j) ** l * q

    found = []
    for l1, l2, l3 in ((0, 0, 0), (0, 1, 1), (1, 0, 1), (1, 1, 0), (1, 1, 1), (2, 1, 1)):
        C = np.einsum("ij,kl,mn,ikn->jlm", to_real(l1), to_real(l2), np.conj(to_real(l3)).T, complex_cg(l1, l2, l3)).real
        found.append(((l1, l2, l3), (C / np.linalg.norm(C)).astype(np.float32)))
    return found


def constants(KT):
    mul = D // 4
    p = np.arange(P)
    feature, group = p % D, p // D
    inner = np.where(feature < mul, feature, (feature - mul) // 3)
    sel = np.zeros((P, SH, P), np.float32)
    for c in range(SH):
        sel[:, c, :] = (group[:, None] == group[None]) & np.isin(feature, (c, SH + c, 2 * SH + c))[:, None]
    cg = coupling_coefficients()
    first = (0, 1, 4)
    coupling = np.zeros((P, len(LAYER3_TERMS), D), np.float32)
    f_in, f_out = feature, np.arange(D)
    for n, (c, i) in enumerate(LAYER3_TERMS):
        (le, ln, lo), C = cg[i]
        m_in = np.where(f_in < mul, 0, (f_in - mul) % 3)
        m_out = np.where(f_out < mul, 0, (f_out - mul) % 3)
        ok = ((f_in >= mul) == (ln == 1))[:, None] & ((f_out >= mul) == (lo == 1))[None]
        table = C[c - first[le]]
        coupling[:, n, :] = np.where(ok, table[np.minimum(m_in, 2 * ln)[:, None], np.minimum(m_out, 2 * lo)[None]], 0.0)
    half = np.zeros((P, 3), np.float32)
    half[:, 0] = feature < D // 2
    half[:, 1] = feature >= D // 2
    half[:, 2] = p
    return {
        "c_ones": np.ones((P, P), np.float32),
        "c_tri": (p[:, None] <= p[None]).astype(np.float32),
        "c_group": (group[:, None] == group[None]).astype(np.float32),
        "c_iota": np.broadcast_to(p.astype(np.int32), (P, P)).copy(),
        "c_half": half,
        "c_sel": sel.reshape(P, SH * P),
        "c_expand": (np.arange(mul)[:, None] == inner[None]).astype(np.float32),
        "c_coupling": coupling,
    }


_INS = ("x_in", "src_c", "dst_c", "dst_w", "pattern_c", "sh_c", "wq", "wk", "wv", "wo", "w2", "w3",
        "c_ones", "c_tri", "c_group", "c_iota", "c_half", "c_sel", "c_expand", "c_coupling")


def laid_out(a):
    n, e = a["x"].shape[0], a["src"].shape[0]
    KT = -(-n // (P * PT)) * PT
    NCH = e // (G * CH)
    assert NCH * G * CH == e and NCH % RING == 0

    def by_chunk(edges):
        return edges.reshape(G, NCH, D, J, -1).transpose(1, 0, 2, 3, 4).reshape(NCH, P, -1)

    dst = a["dst"]
    before = np.concatenate([np.full(1, -1, dst.dtype), dst[:-1]]).reshape(G, NCH, CH)[:, :, :1]
    windows = np.concatenate([before, dst.reshape(G, NCH, CH)], axis=2).transpose(1, 0, 2)
    sh = np.concatenate([a["edge_weight1"], a["edge_attr_3"], a["edge_attr_5"]], axis=1)
    x = np.concatenate([a["x"], np.zeros((KT * P - n, D), a["x"].dtype)])
    laid = {
        "x_in": x.reshape(KT, P, D).transpose(1, 0, 2),
        "src_c": by_chunk(a["src"]), "dst_c": by_chunk(dst), "dst_w": windows,
        "pattern_c": by_chunk(a["edge_attr_32"]), "sh_c": by_chunk(sh),
        "wq": a["L1_gnn_Wq"], "wk": a["L1_gnn_Wk"], "wv": a["L1_gnn_Wv"], "wo": a["L1_gnn_Wo"],
        "w2": a["L2_gnn_W"], "w3": a["L3_gnn_W"], **constants(KT),
    }
    return {name: np.ascontiguousarray(laid[name]) for name in _INS}


def kernel(**inputs):
    import concourse.bacc as bacc
    from concourse.bass_utils import run_bass_kernel_spmd

    arrays = laid_out({name: np.asarray(a) for name, a in inputs.items()})
    n = inputs["x"].shape[0]
    nc = bacc.Bacc("TRN2", target_bir_lowering=False, num_devices=1)
    args = [nc.dram_tensor(name, a.shape, mybir.dt.from_np(a.dtype), kind="ExternalInput").ap() for name, a in arrays.items()]
    args.append(nc.dram_tensor("out", arrays["x_in"].shape, F32, kind="ExternalOutput").ap())
    gnn_kernel(nc, *args)
    result = run_bass_kernel_spmd(nc, [arrays], core_ids=[0])
    y = result.results[0]["out"]
    return y.transpose(1, 0, 2).reshape(-1, D)[:n]
```

```python
from contextlib import ExitStack
import math

import numpy as np
import concourse.bass as bass
from concourse import mybir

F32 = mybir.dt.float32
I32 = mybir.dt.int32
I16 = mybir.dt.int16
BF16 = mybir.dt.bfloat16
ALU = mybir.AluOpType
ACT = mybir.ActivationFunctionType
AX_X = mybir.AxisListType.X

P = 128
D = 32
G = 4
J = 25
CH = D * J
RING = 5
LAYERS = 4
PT = 14
SH = 9
BIG = 1.0e30
H0 = 14
PE_COLS = (4, 3, 5, 2)
PE_MAX = max(PE_COLS)
TILE_BUFS = (2, 3, 5, 2)
LN_EPS = 1.0e-5
Z_EPS = 1.0e-6
HALF = CH // 2
M_COL, Z_COL = D, D + D // 2
LAYER3_TERMS = [(0, 0), (0, 1)] + [(c, i) for c in (1, 2, 3) for i in (2, 3, 4)] + [(c, 5) for c in range(4, 9)]


def gnn_kernel(nc, x_in, src_c, src_pe, dst_c, dst_w, pattern_c, sh_c, wq, wk, wv, wo, w2, w3,
               c_ones, c_tri, c_group, c_iota, c_half, c_sel, c_expand, c_coupling, c_target, out):
    KT = x_in.shape[1]
    NCH = src_c.shape[0]
    TURNS = NCH // RING
    PIECES = KT // PT
    N_PAD = KT * P
    GE = NCH * CH
    E = G * GE
    PC = PT * D
    H1 = KT // H0
    KEYS = PE_MAX * (NCH + 2)
    assert NCH % RING == 0 and KT % PT == 0

    h_table = nc.dram_tensor("h_table", [N_PAD, D], F32, kind="Internal").ap()
    q_table = nc.dram_tensor("q_table", [N_PAD, D], F32, kind="Internal").ap()
    q_edges = nc.dram_tensor("q_edges", [E + N_PAD, D], F32, kind="Internal").ap()
    key_rows = nc.dram_tensor("key_rows", [NCH + 2, PE_MAX * P], I16, kind="Internal").ap()
    sums = nc.dram_tensor("sums", [E, D], F32, kind="Internal").ap()
    attn = nc.dram_tensor("attn", [E, 2 * D], F32, kind="Internal").ap()
    q_chunks = q_edges[0:E, :].rearrange("(c p j) f -> c p (j f)", p=P, j=J)
    sums_chunks = sums.rearrange("(c p j) f -> c p (j f)", p=P, j=J)
    attn_chunks = attn.rearrange("(c p j) f -> c p (j f)", p=P, j=J)

    with ExitStack() as ctx:
        def sb(name, shape, dt=F32):
            return ctx.enter_context(nc.sbuf_tensor(name, shape, dt))

        def sem(name):
            return ctx.enter_context(nc.semaphore(name))

        def sems(name, n=RING):
            return [sem(f"{name}{r}") for r in range(n)]

        xs = sb("xs", [P, KT, D])
        hs = sb("hs", [P, KT, D])
        end_row = sb("end_row", [P, KT], I32)
        begin_row = sb("begin_row", [P, KT], I32)
        part_mask = sb("part_mask", [P, 4, KT])
        part_mean = sb("part_mean", [P, 4, KT])
        part_bias = sb("part_bias", [P, 4, KT])
        counts = sb("counts", [P, KT])
        border = sb("border", [P, 3, 2 * D])
        ln = sb("ln", [P, 4, PT])
        aw = sb("aw", [P, 6, PT])
        idx = sb("idx", [P, RING, J], I32)
        first_idx = sb("first_idx", [G, 1], I32)
        first_q = sb("first_q", [G, D])
        rows = sb("rows", [P, RING, CH])
        edge_in = sb("edge_in", [P, RING, CH])
        dwin = sb("dwin", [P, RING, CH + 1], I32)
        outs = sb("outs", [P, RING, 2 * CH])
        node_rows = outs[:, :, :].rearrange("p r c -> p (r c)")
        h_parts = sb("h_parts", [P, 3, KT * D], BF16)
        keys = sb("keys", [P, RING, PE_MAX * P], I16)
        h0_of = sb("h0_of", [P, KEYS], I16)
        h0_mask = sb("h0_mask", [P, PE_MAX, H0])
        tile_rows = sb("tile_rows", [P, H0 * D])
        target = sb("target", [P, H1, 2], I16)
        one_hots = [sb(f"one_hot{b}", [P, H1, P], BF16)[:, :, :] for b in range(3)]
        dst_t = sb("dst_t", [P, RING, J], I32)
        work = sb("work", [P, 14, CH])
        (hT, qT, keep, qh, prod, u, d, Z, ph, O, mz_m, mz, nb, s_sb) = (work[:, k, :] for k in range(14))
        one_hot_lo = work[:, 5:7, :].rearrange("p a c -> p (a c)").bitcast(BF16).rearrange("p (j n) -> p j n", n=P)
        one_hot_hi = work[:, 7:9, :].rearrange("p a c -> p (a c)").bitcast(BF16)[:, 0:J * KT]\
            .rearrange("p (j n) -> p j n", n=KT)
        nT, nt = work[:, 10:12, 0:PC], work[:, 12:14, 0:PC]
        mx = sb("mx", [P, CH + 1])
        carry = sb("carry", [P, 4])
        one_hots += [work[:, k, 0:H1 * P // 2].bitcast(BF16).rearrange("p (h n) -> p h n", n=P) for k in (5, 6)]
        dst_parts = sb("dst_parts", [P, 2, J], I32)
        dst_pairs = sb("dst_pairs", [P, 2, J, 2], I16)
        sh_rest = sb("sh_rest", [P, J, SH])
        sh_parts = sb("sh_parts", [P, CH], BF16)
        shT = sb("shT", [P, CH], BF16)
        weighted = [qT, qh, prod]
        ones = sb("ones", [P, P])
        tri = sb("tri", [P, P])
        group_ones = sb("group_ones", [P, P])
        iota = sb("iota", [P, P], I16)
        half = sb("half", [P, 3])
        sel = sb("sel", [P, SH, P], BF16)
        staged = [0]

        def stage(parts, *shape):
            n = int(np.prod(shape))
            at, staged[0] = staged[0], staged[0] + n
            flat = node_rows[0:parts, at:at + n]
            return flat if len(shape) == 1 else flat.rearrange("p (a b) -> p a b", b=shape[1])

        sel_f = stage(P, SH * P)
        expand = stage(8, P)
        coupling = stage(P, len(LAYER3_TERMS), D)
        eps = sb("eps", [P, 1])
        w_in = stage(D, 4, D)
        w_t = stage(D, 3, D)
        w_t_wide = stage(D, 2, P)
        w3_in = stage(8, 6, 8)
        w3_wide = stage(8, 6, D)
        w3_full = stage(P, 6, D)
        t_sum = stage(P, SH, D)
        t_tmp = stage(P, D)
        early = work[:, 2:10, :].rearrange("p a c -> p (a c)")[:, 0:8 * KEYS].rearrange("p (a k) -> p a k", a=4)
        src_i, src_f = [early[:, k, :].bitcast(I32) for k in (0, 1)], [early[:, k, :] for k in (2, 3)]
        key_i16 = stage(P, -(-KEYS // 2)).bitcast(I16)[:, 0:KEYS]
        bd_q = sb("bd_q", [P, P])
        bd_vo = sb("bd_vo", [P, P])
        bd_w2 = sb("bd_w2", [P, P])
        bd_t = sb("bd_t", [P, SH, P])

        banks = [ctx.enter_context(nc.psum_tensor(f"bank{b}", [P, 512], F32)) for b in range(6)]
        bcast = banks[0:3]
        tile_banks = banks[3:5] + banks[0:3]
        node_ps = banks[5]
        acc = ctx.enter_context(nc.psum_tensor("acc", [P, 2, 512], F32))

        consts_loaded, weights_loaded, x_loaded = sem("consts_loaded"), sem("weights_loaded"), sem("x_loaded")
        zeros_ready, q_zeroed = sem("zeros_ready"), sem("q_zeroed")
        idx_loaded, dwin_loaded, edge_loaded = sems("idx_loaded"), sems("dwin_loaded"), sems("edge_loaded")
        dst_loaded = sems("dst_loaded")
        rows_gathered = [sems(f"rows_gathered{a}_") for a in range(2)]
        chunk_begun = sem("chunk_begun")
        parts_ready, keys_ready, keys_stored, keys_loaded = sem("parts_ready"), sem("keys_ready"), sem("keys_stored"), sems("keys_loaded")
        one_hot_made, tile_ready, tile_used, picked = sem("one_hot_made"), sem("tile_ready"), sem("tile_used"), sem("picked")
        rows_used, edge_used, keep_ready = sems("rows_used"), sems("edge_used"), sems("keep_ready")
        outs_ready, outs_stored = sems("outs_ready"), sems("outs_stored")
        one_hot_ready, counts_ready, counts_added = sem("one_hot_ready"), sem("counts_ready"), sem("counts_added")
        prod_ready, score_ready, score_copied, nb_ready = sem("prod_ready"), sem("score_ready"), sem("score_copied"), sem("nb_ready")
        decay_in, decay_ready, p_in, p_ready = sem("decay_in"), sem("decay_ready"), sem("p_in"), sem("p_ready")
        mx_ready, mz_m_ready = sem("mx_ready"), sem("mz_m_ready")
        shT_ready = sem("shT_ready")
        bcast_ready, weighted_ready, weighted_used = sems("bcast_ready", 3), sems("weighted_ready", 3), sems("weighted_used", 3)
        msg_copied = sem("msg_copied")
        mask_made = sem("mask_made")
        step = sem("step")
        h_ready, h_stored = sem("h_ready"), sem("h_stored")
        q_ready, q_stored, q_scattered = sem("q_ready"), sem("q_stored"), sem("q_scattered")
        first_loaded, first_gathered, first_stored = sem("first_loaded"), sem("first_gathered"), sem("first_stored")
        node_index_ready, node_gathered = sem("node_index_ready"), sems("node_gathered", PIECES)
        border_loaded = sem("border_loaded")
        prep_lhs, prep_ps = sem("prep_lhs"), sem("prep_ps")
        var_ready, std_ready = sem("var_ready"), sem("std_ready")
        part_in, part_exp = sem("part_in"), sem("part_exp")
        mix_in, mix_ps, mix_out = sem("mix_in"), sem("mix_ps"), sem("mix_out")
        x_ready, x_stored = sem("x_ready"), sem("x_stored")

        block = ctx.enter_context(nc.Block())

        def use(l, t):
            return t + (l * TURNS + 1)

        def gathers(l, t, after=1):
            each = 16 * (J - PE_COLS[l])
            return t * each + (after * each + (16 * TURNS * (J - PE_COLS[l - 2]) if l >= 2 else 0))

        tile_base = [sum((NCH + 1) * PE_COLS[k] for k in range(l)) for l in range(LAYERS)]
        one_hot_base = [tile_base[l] + sum(TILE_BUFS[0:l]) for l in range(LAYERS)]

        def tile_no(base, l, t, i):
            return base[l] + i if t is None else t * (RING * PE_COLS[l]) + (base[l] + i)

        def keys_use(l, t, chunk):
            n = l * (TURNS + (1 if chunk % RING < 2 else 0)) + chunk // RING + 1
            return n if t is None else t + n

        def chunk_no(l, t, r):
            return t * RING + (l * NCH + r + 1)

        mix_count = {0: 0, 1: PIECES, 2: 2 * PIECES}

        @block.sync
        def _(sp):
            sp.dma_start(xs[:, :, :], x_in).then_inc(x_loaded, 16)
            sp.dma_start(src_i[0], src_pe).then_inc(consts_loaded, 16)
            for tile, const in ((ones, c_ones), (tri, c_tri), (group_ones, c_group), (iota, c_iota), (half, c_half),
                                (expand, c_expand)):
                sp.dma_start(tile[:, :], const).then_inc(consts_loaded, 16)
            sp.dma_start(sel_f, c_sel).then_inc(consts_loaded, 16)
            sp.dma_start(coupling[:, :, :], c_coupling).then_inc(consts_loaded, 16)
            sp.dma_start(target[:, :, :], c_target).then_inc(consts_loaded, 16)
            for n, w in enumerate((wq, wk, wv, wo)):
                sp.dma_start(w_in[:, n, :], w).then_inc(weights_loaded, 16)
            sp.dma_start(w3_in[:, :, :], w3.rearrange("n i o -> i n o")).then_inc(weights_loaded, 16)
            sp.wait_ge(zeros_ready, 1)
            for g in range(G):
                sp.dma_start(bd_w2[D * g:D * g + D, D * g:D * g + D], w2).then_inc(weights_loaded, 16)
            sp.dma_start(first_idx[:, :], dst_c[0, 0:P:D, 0:1], allow_slow_non_contiguous=True).then_inc(first_loaded, 16)

            def store_h(n):
                q = n % PIECES
                sp.wait_ge(h_ready, n + 1)
                sp.dma_start(h_table[q * PT * P:(q + 1) * PT * P, :].rearrange("(k p) f -> p k f", p=P),
                             hs[:, q * PT:(q + 1) * PT, :]).then_inc(h_stored, 16)

            for q in range(PIECES):
                store_h(q)
            sp.wait_ge(keys_ready, 1)
            sp.dma_start(key_rows.rearrange("c k -> (c k)").rearrange("(p n) -> p n", p=P), key_i16).then_inc(keys_stored, 16)

            def load_keys(l, t, chunk):
                n = PE_COLS[l] * P
                c = bass.ds(chunk if t is None else t * RING + chunk, 1)
                sp.dma_start(keys[:, chunk % RING, 0:n], key_rows[c, PE_MAX * P - n:PE_MAX * P].broadcast_to([P, n]))\
                    .then_inc(keys_loaded[chunk % RING], 16)

            for l in range(LAYERS):
                if l == 0:
                    sp.wait_ge(keys_stored, 16)
                else:
                    sp.wait_ge(one_hot_made, one_hot_base[l])
                load_keys(l, None, 0)
                load_keys(l, None, 1)
                for r in range(RING):
                    if l >= 1:
                        sp.wait_ge(rows_gathered[(l - 1) % 2][r], gathers(l - 1, 0, TURNS))
                with sp.Fori(0, TURNS) as t:
                    for r in range(RING):
                        c = bass.ds(t * RING + r, 1)
                        sp.wait_ge(rows_gathered[l % 2][r], gathers(l, t, 0))
                        sp.dma_start(idx[:, r, :], src_c[c].rearrange("o p j -> (o p) j")).then_inc(idx_loaded[r], 16)
                        sp.wait_ge(keep_ready[r], use(l, t) - 1)
                        for g in range(G):
                            sp.dma_start(dwin[D * g:D * g + D, r, :],
                                         dst_w[c, g, :].broadcast_to([D, CH + 1])).then_inc(dwin_loaded[r], 16)
                        if l == 0:
                            sp.wait_ge(rows_used[r], t)
                            sp.dma_start(edge_in[:, r, :], pattern_c[c].rearrange("o p c -> (o p) c")).then_inc(edge_loaded[r], 16)
                            sp.wait_ge(one_hot_ready, t * RING)
                            sp.dma_start(dst_t[:, r, :], dst_c[c].rearrange("o p j -> (o p) j")).then_inc(dst_loaded[r], 16)
                        if l == 1:
                            sp.wait_ge(first_stored, 16)
                            sp.wait_ge(edge_used[r], t)
                            sp.dma_start(edge_in[:, r, :], q_chunks[c].rearrange("o p c -> (o p) c")).then_inc(edge_loaded[r], 16)
                        if l == 3:
                            sp.wait_ge(edge_used[r], t + TURNS)
                            sp.dma_start(edge_in[:, r, 0:J * SH], sh_c[c].rearrange("o p c -> (o p) c")).then_inc(edge_loaded[r], 16)
                        sp.wait_ge(one_hot_made, tile_no(one_hot_base, l, t, max(r - 2, 0) * PE_COLS[l]))
                        load_keys(l, t, r + 2)
                if l == 3:
                    sp.wait_ge(edge_used[0], 2 * TURNS)
                    sp.dma_start(edge_in[:, 0, 0:J * SH], sh_c[NCH]).then_inc(edge_loaded[0], 16)
                for r in range(RING):
                    sp.wait_ge(outs_stored[r], 16 * (l + 1) * TURNS)
                if l == 1:
                    last = attn_chunks[NCH - 1:NCH, D - 1:3 * D:D, (J - 1) * 2 * D:J * 2 * D]
                    sp.dma_start(border[:, :, :], last.broadcast_to([P, 3, 2 * D])).then_inc(border_loaded, 16)
                else:
                    last = sums_chunks[NCH - 1:NCH, D - 1:3 * D:D, (J - 1) * D:J * D]
                    sp.dma_start(border[:, :, 0:D], last.broadcast_to([P, 3, D])).then_inc(border_loaded, 16)
                for q in range(PIECES):
                    if l < LAYERS - 1:
                        store_h((l + 1) * PIECES + q)
                    if l == 0:
                        sp.wait_ge(q_ready, q + 1)
                        sp.dma_start(q_table[q * PT * P:(q + 1) * PT * P, :].rearrange("(k p) f -> p k f", p=P),
                                     node_rows[:, q * PC:(q + 1) * PC].rearrange("p (k f) -> p k f", f=D)).then_inc(q_stored, 16)
                    if l == LAYERS - 1:
                        sp.wait_ge(x_ready, q + 1)
                        sp.dma_start(out[:, q * PT:(q + 1) * PT, :], xs[:, q * PT:(q + 1) * PT, :]).then_inc(x_stored, 16)
            sp.wait_ge(x_stored, 16 * PIECES)

        @block.gpsimd
        def _(pool):
            for l in range(LAYERS):
                if l == 1:
                    pool.wait_ge(q_zeroed, 16 * TURNS)
                    for q in range(PIECES):
                        pool.wait_ge(q_ready, q + 1)
                        for k in range(q * PT, (q + 1) * PT):
                            nc.gpsimd.indirect_dma_start(
                                out=q_edges[:, :], out_offset=bass.IndirectOffsetOnAxis(ap=begin_row[:, k:k + 1], axis=0),
                                in_=node_rows[:, k * D:(k + 1) * D], in_offset=None).then_inc(q_scattered, 16)
                    pool.wait_ge(first_loaded, 16)
                    pool.wait_ge(q_stored, 16 * PIECES)
                    nc.gpsimd.indirect_dma_start(
                        out=first_q[:, :], out_offset=None, in_=q_table[:, :],
                        in_offset=bass.IndirectOffsetOnAxis(ap=first_idx[:, :], axis=0)).then_inc(first_gathered, 16)
                    pool.wait_ge(first_gathered, 16)
                    pool.wait_ge(q_scattered, 16 * KT)
                    pool.dma_start(q_chunks[0, 0:P:D, 0:D], first_q[:, :]).then_inc(first_stored, 16)
                pool.wait_ge(h_stored, 16 * PIECES * (l + 1))
                with pool.Fori(0, TURNS) as t:
                    for r in range(RING):
                        pool.wait_ge(rows_used[r], use(l, t) - 1)
                        pool.wait_ge(idx_loaded[r], use(l, t) * 16)
                        pool.sem_inc(chunk_begun, 1)
                        for j in range(J - PE_COLS[l]):
                            nc.gpsimd.indirect_dma_start(
                                out=rows[:, r, j * D:(j + 1) * D], out_offset=None, in_=h_table[:, :],
                                in_offset=bass.IndirectOffsetOnAxis(ap=idx[:, r, j:j + 1], axis=0)).then_inc(rows_gathered[l % 2][r], 16)
                if l == 0:
                    pool.wait_ge(node_index_ready, 1)
                for r in range(RING):
                    pool.wait_ge(outs_stored[r], 16 * (l + 1) * TURNS)
                table, width = (attn, 2 * D) if l == 1 else (sums, D)
                for k in range(KT):
                    nc.gpsimd.indirect_dma_start(
                        out=node_rows[:, k * width:(k + 1) * width], out_offset=None, in_=table[:, :],
                        in_offset=bass.IndirectOffsetOnAxis(ap=end_row[:, k:k + 1], axis=0)).then_inc(node_gathered[k // PT], 16)

        @block.scalar
        def _(act):
            def std(n):
                act.wait_ge(var_ready, n + 1)
                nc.scalar.activation(ln[:, 2, :], ln[:, 1, :], ACT.Sqrt, bias=eps[:, :], scale=1.0 / D).then_inc(std_ready, 1)

            def mix_copy(n, scale):
                act.wait_ge(mix_ps, n + 1)
                nc.scalar.activation(nT[:, 1, :], node_ps[:, 0:PC], ACT.Copy, scale=scale).then_inc(mix_out, 1)

            def store(l, t, r, chunks, width):
                act.wait_ge(outs_ready[r], use(l, t))
                act.dma_start(chunks[bass.ds(t * RING + r, 1)].rearrange("o p c -> (o p) c"),
                              outs[:, r, 0:width]).then_inc(outs_stored[r], 16)

            for q in range(PIECES):
                std(q)
            act.wait_ge(zeros_ready, 1)
            with act.Fori(0, TURNS) as t:
                act.dma_start(q_edges[bass.ds(t * (RING * P * J), RING * P * J), :].rearrange("(p r a) f -> p r (a f)", p=P, r=RING),
                              qT.unsqueeze(1).broadcast_to([P, RING, CH])).then_inc(q_zeroed, 16)
                for r in range(RING):
                    store(0, t, r, sums_chunks, CH)
            for q in range(PIECES):
                std(PIECES + q)
                mix_copy(q, float(D) ** -0.5)
            with act.Fori(0, TURNS) as t:
                for r in range(RING):
                    n = chunk_no(0, t, r)
                    act.wait_ge(keep_ready[r], use(1, t))
                    nc.scalar.activation(nb, keep, ACT.Copy, scale=BIG, bias=-BIG).then_inc(nb_ready, 1)
                    act.wait_ge(score_ready, n)
                    nc.scalar.activation(s_sb.rearrange("p (a c) -> p a c", a=2), acc[:, :, 0:HALF], ACT.Copy).then_inc(score_copied, 1)
                    act.wait_ge(decay_in, n)
                    nc.scalar.activation(u, u, ACT.Exp).then_inc(decay_ready, 1)
                    act.wait_ge(p_in, n)
                    nc.scalar.activation(d, d, ACT.Exp).then_inc(p_ready, 1)
                    act.wait_ge(mx_ready, n)
                    nc.scalar.activation(mz_m, mx[:, 1:CH + 1], ACT.Copy, scale=half[:, 0:1]).then_inc(mz_m_ready, 1)
                    store(1, t, r, attn_chunks, 2 * CH)
            for q in range(PIECES):
                act.wait_ge(part_in, q + 1)
                nc.scalar.activation(aw[:, 0:4, :], aw[:, 0:4, :], ACT.Exp).then_inc(part_exp, 1)
                mix_copy(PIECES + q, 1.0)
                std(2 * PIECES + q)
            with act.Fori(0, TURNS) as t:
                for r in range(RING):
                    store(2, t, r, sums_chunks, CH)
            for q in range(PIECES):
                mix_copy(2 * PIECES + q, 1.0)
                std(3 * PIECES + q)
            with act.Fori(0, TURNS) as t:
                for r in range(RING):
                    act.wait_ge(weighted_used[2], t * (6 * RING) + (6 * r + 6))
                    nc.scalar.activation(s_sb.rearrange("p (a c) -> p a c", a=2), acc[:, :, 0:HALF], ACT.Copy).then_inc(msg_copied, 1)
                    store(3, t, r, sums_chunks, CH)

        @block.tensor
        def _(pe):
            pe.wait_ge(prep_lhs, 1)
            nc.tensor.matmul(acc[:, 0, 0:D], w_t_wide[:, 0, :], w_t[:, 1, :], start=True, stop=True)
            nc.tensor.matmul(acc[:, 0, D:2 * D], w_t_wide[:, 1, :], w_in[:, 3, :], start=True, stop=True)
            nc.tensor.matmul(acc[:, 1, 0:6 * D], expand[:, :], w3_wide[:, :, :], start=True, stop=True).then_inc(prep_ps, 1)
            def gather_tile(l, t, i):
                b = i % TILE_BUFS[l]
                pe.wait_ge(one_hot_made, tile_no(one_hot_base, l, t, i + 1))
                if t is not None or i >= TILE_BUFS[l]:
                    pe.wait_ge(tile_used, tile_no(tile_base, l, t, i + 1 - TILE_BUFS[l]))
                for h1 in range(H1):
                    for part in range(3):
                        last = nc.tensor.matmul(tile_banks[b][:, 0:H0 * D], one_hots[b][:, h1, :],
                                                h_parts[:, part, h1 * H0 * D:(h1 + 1) * H0 * D],
                                                start=(h1 == 0 and part == 0), stop=(h1 == H1 - 1 and part == 2))
                last.then_inc(tile_ready, 1)

            def gather_first(l):
                pe.wait_ge(parts_ready, PIECES * (l + 1))
                for i in range(PE_COLS[l]):
                    gather_tile(l, None, i)

            def gather_next(l, t, r, which):
                for q in which:
                    gather_tile(l, t, (r + 1) * PE_COLS[l] + q)

            pe.wait_ge(prep_lhs, 2)
            gather_first(0)
            with pe.Fori(0, TURNS) as t:
                for r in range(RING):
                    gather_next(0, t, r, range(2))
                    pe.wait_ge(one_hot_ready, chunk_no(0, t, r))
                    pe.wait_ge(counts_added, t * RING + r)
                    for j in range(J):
                        last = nc.tensor.matmul(acc[:, 0, 0:KT], one_hot_lo[:, j, :], one_hot_hi[:, j, :],
                                                start=(j == 0), stop=(j == J - 1))
                    last.then_inc(counts_ready, 1)
                    gather_next(0, t, r, range(2, PE_COLS[0]))
            pe.wait_ge(counts_added, NCH)
            nc.tensor.matmul(acc[:, 0, 0:KT], tri[:, :], counts[:, :], start=True, stop=True)
            nc.tensor.matmul(acc[:, 1, 0:KT], ones[:, :], counts[:, :], start=True, stop=True).then_inc(prep_ps, 1)

            def mix(n, weight):
                pe.wait_ge(mix_in, n + 1)
                nc.tensor.matmul(node_ps[:, 0:PC], weight[:, :], nT[:, 0, :], start=True, stop=True).then_inc(mix_ps, 1)

            for q in range(PIECES):
                mix(q, bd_q)
            gather_first(1)
            with pe.Fori(0, TURNS) as t:
                for r in range(RING):
                    gather_next(1, t, r, range(1))
                    pe.wait_ge(prod_ready, chunk_no(0, t, r))
                    pe.wait_ge(score_copied, t * RING + r)
                    for a in range(2):
                        last = nc.tensor.matmul(acc[:, a, 0:HALF], group_ones[:, :], prod[:, a * HALF:(a + 1) * HALF],
                                                start=True, stop=True)
                    last.then_inc(score_ready, 1)
                    gather_next(1, t, r, range(1, PE_COLS[1]))
            for q in range(PIECES):
                mix(PIECES + q, bd_vo)
            gather_first(2)
            with pe.Fori(0, TURNS) as t:
                for r in range(RING):
                    gather_next(2, t, r, range(PE_COLS[2]))
            for q in range(PIECES):
                mix(2 * PIECES + q, bd_w2)

            def spread(t, r, n):
                pe.wait_ge(weighted_ready[n % 3], t * (6 * RING) + (6 * r + n // 3))
                if n == 0:
                    pe.wait_ge(shT_ready, chunk_no(0, t, r))
                half_n = slice((n % 2) * HALF, (n % 2 + 1) * HALF)
                nc.tensor.matmul(bcast[n % 3][:, 0:HALF], sel[:, n // 2, :], shT[:, half_n],
                                 start=True, stop=True).then_inc(bcast_ready[n % 3], 1)

            def couple(t, r, n):
                pe.wait_ge(weighted_ready[n % 3], t * (6 * RING) + (6 * r + n // 3 + 1))
                if n == 0:
                    pe.wait_ge(msg_copied, t * RING + r)
                nc.tensor.matmul(acc[:, n % 2, 0:HALF], bd_t[:, n // 2, :], weighted[n % 3][:, 0:HALF],
                                 start=(n // 2 == 0), stop=(n // 2 == SH - 1)).then_inc(weighted_used[n % 3], 1)

            gather_first(3)
            with pe.Fori(0, TURNS) as t:
                for r in range(RING):
                    gather_next(3, t, r, range(PE_COLS[3]))
                    for n in range(2 * SH):
                        spread(t, r, n)
                        if n >= 2:
                            couple(t, r, n - 2)
                    couple(t, r, 2 * SH - 2)
                    couple(t, r, 2 * SH - 1)

        @block.vector
        def _(v):
            steps = [0]

            def link(ins):
                steps[0] += 1
                ins.then_inc(step, 1)
                v.wait_ge(step, steps[0])

            def by_edge(ap):
                return ap.rearrange("p (i j) -> p j i", j=J)

            def pairs(ap):
                return ap.rearrange("p a (n b) -> p a n b", b=2)

            def spread_over(ap, n):
                return ap.unsqueeze(2).broadcast_to([P, ap.shape[1], n])

            nc.vector.memset(bd_w2[:, :], 0.0)
            link(nc.vector.memset(qT, 0.0))
            nc.vector.memset(carry[:, :], 0.0).then_inc(zeros_ready, 1)
            nc.vector.memset(eps[:, :], LN_EPS)
            nc.vector.memset(bd_q[:, :], 0.0)
            nc.vector.memset(bd_vo[:, :], 0.0)
            nc.vector.memset(bd_t[:, :, :], 0.0)
            nc.vector.memset(counts[:, :], 0.0)
            link(nc.vector.memset(sh_parts[:, :], 0.0))

            def layer_norm(n, q):
                x = xs[:, q * PT:(q + 1) * PT, :]
                xc = nt[:, 0, :].rearrange("p (k f) -> p k f", f=D)
                sq = nt[:, 1, :].rearrange("p (k f) -> p k f", f=D)
                link(nc.vector.reduce_sum(ln[:, 0, :], x, axis=AX_X))
                link(nc.vector.tensor_scalar(ln[:, 0, :], ln[:, 0, :], -1.0 / D, None, ALU.mult))
                link(nc.vector.tensor_tensor(xc, x, spread_over(ln[:, 0, :], D), ALU.add))
                link(nc.vector.tensor_tensor(sq, xc, xc, ALU.mult))
                nc.vector.reduce_sum(ln[:, 1, :], sq, axis=AX_X).then_inc(var_ready, 1)
                v.wait_ge(std_ready, n + 1)
                link(nc.vector.reciprocal(ln[:, 3, :], ln[:, 2, :]))
                nc.vector.scalar_tensor_tensor(out=hs[:, q * PT:(q + 1) * PT, :], in0=xc, scalar=0.0,
                                               in1=spread_over(ln[:, 3, :], D), op0=ALU.max, op1=ALU.mult).then_inc(h_ready, 1)

            def split_h(q):
                h = hs[:, q * PT:(q + 1) * PT, :].rearrange("p k f -> p (k f)")
                part = [h_parts[:, k, q * PC:(q + 1) * PC] for k in range(3)]
                link(nc.vector.tensor_copy(part[0], h))
                link(nc.vector.tensor_tensor(nt[:, 0, :], h, part[0], ALU.subtract))
                link(nc.vector.tensor_copy(part[1], nt[:, 0, :]))
                nc.vector.tensor_tensor(part[2], nt[:, 0, :], part[1], ALU.subtract).then_inc(parts_ready, 1)

            v.wait_ge(x_loaded, 16)
            for q in range(PIECES):
                layer_norm(q, q)
                v.wait_ge(h_ready, q + 1)

            v.wait_ge(consts_loaded, 10 * 16)
            link(nc.vector.tensor_scalar(src_i[1], src_i[0], P.bit_length() - 1, None, ALU.logical_shift_right))
            link(nc.vector.tensor_copy(src_f[0], src_i[1]))
            link(nc.vector.tensor_scalar(src_f[1], src_f[0], 1.0 / H0, 0.5 / H0 - 0.5, ALU.mult, ALU.add))
            link(nc.vector.tensor_scalar(src_f[1], src_f[1], 2.0 ** 23 + 2.0 ** 22, None, ALU.add))
            link(nc.vector.tensor_scalar(src_f[1], src_f[1], -(2.0 ** 23 + 2.0 ** 22), None, ALU.add))
            link(nc.vector.scalar_tensor_tensor(out=src_f[0][:, KEYS:2 * KEYS], in0=src_f[1][:, KEYS:2 * KEYS], scalar=-float(H0),
                                                in1=src_f[0][:, KEYS:2 * KEYS], op0=ALU.mult, op1=ALU.add))
            link(nc.vector.tensor_copy(h0_of[:, :], src_f[0][:, KEYS:2 * KEYS]))
            link(nc.vector.tensor_scalar(src_i[1], src_i[0], P - 1, None, ALU.bitwise_and))
            link(nc.vector.tensor_copy(src_f[0][:, 0:KEYS], src_i[1][:, 0:KEYS]))
            nc.vector.scalar_tensor_tensor(out=key_i16, in0=src_f[1][:, 0:KEYS], scalar=float(P), in1=src_f[0][:, 0:KEYS],
                                           op0=ALU.mult, op1=ALU.add).then_inc(keys_ready, 1)
            for q in range(PIECES):
                split_h(q)
                v.wait_ge(parts_ready, q + 1)

            def make_one_hot(l, t, i):
                chunk, q = i // PE_COLS[l], i % PE_COLS[l]
                v.wait_ge(keys_loaded[chunk % RING], keys_use(l, t, chunk) * 16)
                by_pair = [P, H1, P // 2, 2]
                nc.vector.tensor_tensor(pairs(one_hots[i % TILE_BUFS[l]]),
                                        pairs(keys[:, chunk % RING, q * P:(q + 1) * P].unsqueeze(1)).broadcast_to(by_pair),
                                        target[:, :, :].unsqueeze(2).broadcast_to(by_pair), ALU.is_equal).then_inc(one_hot_made, 1)

            def mask_h0(l, t, chunk):
                n = PE_COLS[l]
                at = chunk * PE_MAX + PE_MAX - n
                of = h0_of[:, bass.ds(at if t is None else t * (RING * PE_MAX) + at, n)]
                nc.vector.tensor_tensor(h0_mask[:, 0:n, :], of.unsqueeze(2).broadcast_to([P, n, H0]),
                                        iota[:, 0:H0].unsqueeze(1).broadcast_to([P, n, H0]), ALU.is_equal).then_inc(mask_made, 1)

            def pick(l, t, i):
                chunk, q, b = i // PE_COLS[l], i % PE_COLS[l], i % TILE_BUFS[l]
                if q == 0:
                    mask_h0(l, t, chunk)
                    v.wait_ge(mask_made, (t * RING if t is not None else 0) + (l * (NCH + 1) + chunk + 1))
                v.wait_ge(tile_ready, tile_no(tile_base, l, t, i + 1))
                if t is not None or tile_base[l] + i > 0:
                    v.wait_ge(picked, tile_no(tile_base, l, t, i))
                nc.vector.tensor_tensor(tile_rows[:, :].rearrange("p (h f) -> p h f", f=D),
                                        tile_banks[b][:, 0:H0 * D].rearrange("p (h f) -> p h f", f=D),
                                        spread_over(h0_mask[:, q, :], D), ALU.mult).then_inc(tile_used, 1)
                make_one_hot(l, t, i + TILE_BUFS[l])
                v.wait_ge(tile_used, tile_no(tile_base, l, t, i + 1))
                j = J - PE_COLS[l] + q
                nc.vector.reduce_sum(rows[:, chunk % RING, j * D:(j + 1) * D], tile_rows[:, :].rearrange("p (h f) -> p f h", f=D),
                                     axis=AX_X).then_inc(picked, 1)

            def pick_first(l):
                for i in range(TILE_BUFS[l]):
                    make_one_hot(l, None, i)
                for i in range(PE_COLS[l]):
                    pick(l, None, i)

            def pick_next(l, t, r, which):
                for q in which:
                    pick(l, t, (r + 1) * PE_COLS[l] + q)

            def wait_rows(l, t, r):
                v.wait_ge(rows_gathered[l % 2][r], gathers(l, t))
                v.wait_ge(picked, tile_no(tile_base, l, t, (r + 1) * PE_COLS[l]))

            v.wait_ge(weights_loaded, (5 + G) * 16)
            nc.vector.tensor_copy(sel[:, :, :].rearrange("p c m -> p (c m)"), sel_f)
            for n in range(3):
                nc.vector.transpose(w_t[:, n, :], w_in[:, n, :])
            nc.vector.tensor_copy(w3_wide[:, :, 0:8], w3_in[:, :, :])
            for k in range(3):
                last = nc.vector.tensor_copy(w3_wide[:, :, 8 + k:D:3], w3_in[:, :, :])
            link(last)
            for n, m in ((0, 0), (1, 2)):
                last = nc.vector.tensor_copy(w_t_wide[:, n, :].rearrange("p (g f) -> p g f", g=G),
                                             w_t[:, m:m + 1, :].broadcast_to([D, G, D]))
            last.then_inc(prep_lhs, 1)
            v.wait_ge(prep_ps, 1)
            for g in range(G):
                q = slice(D * g, D * g + D)
                nc.vector.tensor_copy(bd_q[q, q], acc[q, 0, 0:D])
                nc.vector.tensor_copy(bd_vo[q, q], acc[q, 0, D:2 * D])
            link(nc.vector.tensor_copy(w3_full[:, :, :].rearrange("p n f -> p (n f)"), acc[:, 1, 0:6 * D]))
            seen = set()
            for n, (c, i) in enumerate(LAYER3_TERMS):
                to = t_tmp[:, :] if c in seen else t_sum[:, c, :]
                link(nc.vector.tensor_tensor(to, w3_full[:, i, :], coupling[:, n, :], ALU.mult))
                if c in seen:
                    link(nc.vector.tensor_tensor(t_sum[:, c, :], t_sum[:, c, :], t_tmp[:, :], ALU.add))
                seen.add(c)
            for g in range(G):
                q = slice(D * g, D * g + D)
                last = nc.vector.tensor_copy(bd_t[q, :, q], t_sum[q, :, :])
            link(last)
            nc.vector.memset(aw[:, :, :], 0.0).then_inc(prep_lhs, 1)

            def start_chunk(l, t, r):
                v.wait_ge(dwin_loaded[r], use(l, t) * (16 * G))
                nc.vector.tensor_tensor(keep, dwin[:, r, 1:CH + 1], dwin[:, r, 0:CH], ALU.is_equal).then_inc(keep_ready[r], 1)

            pick_first(0)
            steps0 = steps[0]
            per_chunk = 5
            with v.Fori(0, TURNS) as t:
                for r in range(RING):
                    at = [0]

                    def then(ins, r=r, at=at, t=t):
                        at[0] += 1
                        ins.then_inc(step, 1)
                        v.wait_ge(step, t * (RING * per_chunk) + (steps0 + r * per_chunk + at[0]))

                    start_chunk(0, t, r)
                    v.wait_ge(dst_loaded[r], use(0, t) * 16)
                    nc.vector.tensor_scalar(dst_parts[:, 0, :], dst_t[:, r, :], P - 1, None, ALU.bitwise_and)
                    then(nc.vector.tensor_scalar(dst_parts[:, 1, :], dst_t[:, r, :], P.bit_length() - 1, None, ALU.logical_shift_right))
                    then(nc.vector.tensor_copy(dst_pairs[:, :, :, :], dst_parts[:, :, :].unsqueeze(3).broadcast_to([P, 2, J, 2])))
                    for to, of, n in ((one_hot_lo, 0, P), (one_hot_hi, 1, KT)):
                        last = nc.vector.tensor_tensor(pairs(to), dst_pairs[:, of, :, :].unsqueeze(2).broadcast_to([P, J, n // 2, 2]),
                                                       pairs(iota[:, 0:n].unsqueeze(1)).broadcast_to([P, J, n // 2, 2]), ALU.is_equal)
                    last.then_inc(one_hot_ready, 1)
                    pick_next(0, t, r, range(2))
                    wait_rows(0, t, r)
                    v.wait_ge(edge_loaded[r], use(0, t) * 16)
                    nc.vector.tensor_tensor(prod, rows[:, r, :], edge_in[:, r, :], ALU.mult).then_inc(rows_used[r], 1)
                    pick_next(0, t, r, range(2, PE_COLS[0]))
                    v.wait_ge(rows_used[r], use(0, t))
                    then(nc.vector.transpose(by_edge(hT), prod))
                    then(nc.vector.tensor_tensor_scan(O, keep, hT, carry[:, 3:4], ALU.mult, ALU.add))
                    then(nc.vector.tensor_copy(carry[:, 3:4], O[:, CH - 1:CH]))
                    v.wait_ge(outs_stored[r], (use(0, t) - 1) * 16)
                    nc.vector.transpose(outs[:, r, 0:CH], by_edge(O)).then_inc(outs_ready[r], 1)
                    v.wait_ge(counts_ready, chunk_no(0, t, r))
                    v.wait_ge(counts_added, t * RING + r)
                    nc.vector.tensor_tensor(counts[:, :], counts[:, :], acc[:, 0, 0:KT], ALU.add).then_inc(counts_added, 1)
                    assert at[0] == per_chunk
            steps[0] += NCH * per_chunk

            v.wait_ge(prep_ps, 2)
            A = [work[:, k, 0:KT] for k in (2, 3, 4, 5, 6, 7, 8, 9)]
            end, begin, e, grp, a, b, ne, no = A
            link(nc.vector.tensor_copy(b, acc[:, 1, 0:KT]))
            link(nc.vector.memset(a, 1.0))
            link(nc.vector.tensor_tensor_scan(e, a, b, 0.0, ALU.mult, ALU.add))
            link(nc.vector.tensor_tensor(e, e, b, ALU.subtract))
            link(nc.vector.tensor_tensor(end, e, acc[:, 0, 0:KT], ALU.add))
            link(nc.vector.tensor_tensor(begin, end, counts[:, :], ALU.subtract))
            link(nc.vector.tensor_scalar(ne, counts[:, :], 0.5, None, ALU.is_ge))
            link(nc.vector.tensor_copy(part_mask[:, 0, :], ne))
            for g in range(3):
                link(nc.vector.tensor_scalar(a, begin, float((g + 1) * GE) - 0.5, None, ALU.is_lt))
                link(nc.vector.tensor_scalar(b, end, float((g + 1) * GE) + 0.5, None, ALU.is_gt))
                link(nc.vector.tensor_tensor(part_mask[:, g + 1, :], a, b, ALU.mult))
            link(nc.vector.tensor_scalar(part_bias[:, :, :], part_mask[:, :, :], BIG, -BIG, ALU.mult, ALU.add))
            link(nc.vector.tensor_scalar(a, counts[:, :], 1.0, None, ALU.max))
            link(nc.vector.reciprocal(b, a))
            link(nc.vector.tensor_tensor(part_mean[:, :, :], part_mask[:, :, :],
                                         b.unsqueeze(1).broadcast_to([P, 4, KT]), ALU.mult))

            def row_of(edge):
                link(nc.vector.tensor_scalar(grp, edge, float(GE) - 0.5, None, ALU.is_gt))
                for g in range(2, G):
                    link(nc.vector.tensor_scalar(a, edge, float(g * GE) - 0.5, None, ALU.is_gt))
                    link(nc.vector.tensor_tensor(grp, grp, a, ALU.add))
                link(nc.vector.scalar_tensor_tensor(out=edge, in0=grp, scalar=-float(GE), in1=edge, op0=ALU.mult, op1=ALU.add))
                link(nc.vector.tensor_scalar(a, edge, 1.0 / CH, 0.5 / CH - 0.5, ALU.mult, ALU.add))
                link(nc.vector.tensor_scalar(a, a, 2.0 ** 23 + 2.0 ** 22, None, ALU.add))
                link(nc.vector.tensor_scalar(a, a, -(2.0 ** 23 + 2.0 ** 22), None, ALU.add))
                link(nc.vector.scalar_tensor_tensor(out=edge, in0=a, scalar=float((G - 1) * CH), in1=edge, op0=ALU.mult, op1=ALU.add))
                link(nc.vector.scalar_tensor_tensor(out=edge, in0=grp, scalar=float(CH), in1=edge, op0=ALU.mult, op1=ALU.add))

            link(nc.vector.tensor_scalar(e, end, -1.0, 0.0, ALU.add, ALU.max))
            row_of(e)
            link(nc.vector.tensor_copy(end_row[:, :], e))
            link(nc.vector.tensor_scalar(begin, begin, float(E - 1), None, ALU.min))
            row_of(begin)
            link(nc.vector.tensor_copy(no, iota[:, 0:KT]))
            link(nc.vector.tensor_scalar(no, no, float(P), float(E), ALU.mult, ALU.add))
            link(nc.vector.tensor_scalar(no, no, half[:, 2:3], None, ALU.add))
            link(nc.vector.tensor_tensor(a, begin, no, ALU.subtract))
            link(nc.vector.tensor_tensor(a, a, ne, ALU.mult))
            link(nc.vector.tensor_tensor(a, a, no, ALU.add))
            nc.vector.tensor_copy(begin_row[:, :], a).then_inc(node_index_ready, 1)
            v.wait_ge(node_index_ready, 1)

            def piece(q, width=D, at=0):
                return node_rows[:, q * PT * width:(q + 1) * PT * width].rearrange("p (k f) -> p k f", f=width)[:, :, at:at + D]

            agg = nt[:, 0, :].rearrange("p (k f) -> p k f", f=D)
            part = nt[:, 1, :].rearrange("p (k f) -> p k f", f=D)

            def parts_sum(rows_of_piece, weights):
                link(nc.vector.tensor_tensor(agg, rows_of_piece, spread_over(weights[:, 0, :], D), ALU.mult))
                for g in range(3):
                    link(nc.vector.tensor_tensor(part, spread_over(weights[:, g + 1, :], D),
                                                 border[:, g:g + 1, 0:D].broadcast_to([P, PT, D]), ALU.mult))
                    link(nc.vector.tensor_tensor(agg, agg, part, ALU.add))

            def mixed(n, rows_in, rows_out):
                nc.vector.transpose(nT[:, 0, :], rows_in).then_inc(mix_in, 1)
                v.wait_ge(mix_out, n + 1)
                return nc.vector.transpose(rows_out, nT[:, 1, :])

            def node_start(l, q):
                if q == 0:
                    v.wait_ge(border_loaded, 16 * (l + 1))
                v.wait_ge(node_gathered[q], 16 * PT * (l + 1))
                return xs[:, q * PT:(q + 1) * PT, :], slice(q * PT, (q + 1) * PT)

            for q in range(PIECES):
                x, ks = node_start(0, q)
                parts_sum(piece(q), part_mean[:, :, ks])
                link(nc.vector.tensor_tensor(agg, agg, hs[:, ks, :], ALU.add))
                link(nc.vector.tensor_tensor(x, x, agg, ALU.add))
                layer_norm(PIECES + q, q)
                v.wait_ge(h_ready, PIECES + q + 1)
                split_h(q)
                mixed(q, hs[:, ks, :].rearrange("p k f -> p (k f)"), node_rows[:, q * PC:(q + 1) * PC]).then_inc(q_ready, 1)
                v.wait_ge(q_ready, q + 1)

            nc.vector.memset(mx[:, 0:1], -BIG)
            link(nc.vector.memset(carry[:, :], 0.0))
            pick_first(1)
            steps1 = steps[0]
            per_chunk1 = 11
            with v.Fori(0, TURNS) as t:
                for r in range(RING):
                    at = [0]

                    def then(ins, r=r, at=at, t=t):
                        at[0] += 1
                        ins.then_inc(step, 1)
                        v.wait_ge(step, t * (RING * per_chunk1) + (steps1 + r * per_chunk1 + at[0]))

                    n = chunk_no(0, t, r)
                    start_chunk(1, t, r)
                    wait_rows(1, t, r)
                    nc.vector.transpose(by_edge(hT), rows[:, r, :]).then_inc(rows_used[r], 1)
                    v.wait_ge(edge_loaded[r], use(1, t) * 16)
                    nc.vector.transpose(by_edge(qT), edge_in[:, r, :]).then_inc(edge_used[r], 1)
                    v.wait_ge(edge_used[r], t + 1)
                    then(nc.vector.tensor_tensor_scan(qh, keep, qT, carry[:, 0:1], ALU.mult, ALU.add))
                    nc.vector.tensor_tensor(prod, qh, hT, ALU.mult).then_inc(prod_ready, 1)
                    then(nc.vector.tensor_copy(carry[:, 0:1], qh[:, CH - 1:CH]))
                    pick_next(1, t, r, range(1))
                    v.wait_ge(nb_ready, n)
                    v.wait_ge(score_copied, n)
                    nc.vector.tensor_tensor_scan(mx[:, 1:CH + 1], nb, s_sb, mx[:, 0:1], ALU.add, ALU.max).then_inc(mx_ready, 1)
                    v.wait_ge(mx_ready, n)
                    then(nc.vector.tensor_tensor(u, mx[:, 0:CH], nb, ALU.add))
                    nc.vector.tensor_tensor(u, u, mx[:, 1:CH + 1], ALU.subtract).then_inc(decay_in, 1)
                    nc.vector.tensor_tensor(d, s_sb, mx[:, 1:CH + 1], ALU.subtract).then_inc(p_in, 1)
                    pick_next(1, t, r, range(1, 2))
                    v.wait_ge(decay_ready, n)
                    v.wait_ge(p_ready, n)
                    then(nc.vector.tensor_tensor(ph, d, hT, ALU.mult))
                    then(nc.vector.tensor_tensor_scan(Z, u, d, carry[:, 1:2], ALU.mult, ALU.add))
                    then(nc.vector.tensor_tensor_scan(O, u, ph, carry[:, 2:3], ALU.mult, ALU.add))
                    then(nc.vector.tensor_copy(carry[:, 1:2], Z[:, CH - 1:CH]))
                    then(nc.vector.tensor_copy(carry[:, 2:3], O[:, CH - 1:CH]))
                    v.wait_ge(mz_m_ready, n)
                    then(nc.vector.tensor_copy(mx[:, 0:1], mx[:, CH:CH + 1]))
                    then(nc.vector.scalar_tensor_tensor(out=mz, in0=Z, scalar=half[:, 1:2], in1=mz_m, op0=ALU.mult, op1=ALU.add))
                    pick_next(1, t, r, range(2, PE_COLS[1]))
                    v.wait_ge(outs_stored[r], (use(1, t) - 1) * 16)
                    row = outs[:, r, :].rearrange("p (j f) -> p j f", j=J)
                    then(nc.vector.transpose(row[:, :, 0:D], by_edge(O)))
                    nc.vector.transpose(row[:, :, D:2 * D], by_edge(mz)).then_inc(outs_ready[r], 1)
                    assert at[0] == per_chunk1
            steps[0] += NCH * per_chunk1

            for q in range(PIECES):
                x, ks = node_start(1, q)
                at_m, at_z = piece(q, 2 * D, D)[:, :, 0], piece(q, 2 * D, D)[:, :, Z_COL - M_COL]
                w, top, z = aw[:, 0:4, :], aw[:, 4, :], aw[:, 5, :]
                link(nc.vector.tensor_tensor(w[:, 0, :], at_m, part_mask[:, 0, ks], ALU.mult))
                link(nc.vector.tensor_tensor(w[:, 0, :], w[:, 0, :], part_bias[:, 0, ks], ALU.add))
                link(nc.vector.tensor_copy(top, w[:, 0, :]))
                for g in range(3):
                    link(nc.vector.scalar_tensor_tensor(out=w[:, g + 1, :], in0=part_mask[:, g + 1, ks], scalar=border[:, g, M_COL:M_COL + 1],
                                                        in1=part_bias[:, g + 1, ks], op0=ALU.mult, op1=ALU.add))
                    link(nc.vector.tensor_tensor(top, top, w[:, g + 1, :], ALU.max))
                nc.vector.tensor_tensor(w, w, top.unsqueeze(1).broadcast_to([P, 4, PT]), ALU.subtract).then_inc(part_in, 1)
                v.wait_ge(part_exp, q + 1)
                link(nc.vector.tensor_tensor(w, w, part_mask[:, :, ks], ALU.mult))
                link(nc.vector.tensor_tensor(z, w[:, 0, :], at_z, ALU.mult))
                for g in range(3):
                    link(nc.vector.scalar_tensor_tensor(out=z, in0=w[:, g + 1, :], scalar=border[:, g, Z_COL:Z_COL + 1], in1=z,
                                                        op0=ALU.mult, op1=ALU.add))
                link(nc.vector.tensor_scalar(z, z, Z_EPS, None, ALU.add))
                link(nc.vector.reciprocal(top, z))
                link(nc.vector.tensor_tensor(w, w, top.unsqueeze(1).broadcast_to([P, 4, PT]), ALU.mult))
                parts_sum(piece(q, 2 * D), w)
                link(mixed(PIECES + q, nt[:, 0, :], nt[:, 1, :]))
                link(nc.vector.tensor_tensor(agg, part, hs[:, ks, :], ALU.add))
                link(nc.vector.tensor_tensor(x, x, agg, ALU.add))
                layer_norm(2 * PIECES + q, q)
                v.wait_ge(h_ready, 2 * PIECES + q + 1)
                split_h(q)
                v.wait_ge(parts_ready, 2 * PIECES + q + 1)

            def plain_chunk(l, t, r, messages, then):
                then(nc.vector.tensor_tensor_scan(O, keep, messages, carry[:, 3:4], ALU.mult, ALU.add))
                then(nc.vector.tensor_copy(carry[:, 3:4], O[:, CH - 1:CH]))
                v.wait_ge(outs_stored[r], (use(l, t) - 1) * 16)
                nc.vector.transpose(outs[:, r, 0:CH], by_edge(O)).then_inc(outs_ready[r], 1)
                v.wait_ge(outs_ready[r], use(l, t))

            link(nc.vector.memset(carry[:, :], 0.0))
            pick_first(2)
            steps2 = steps[0]
            per_chunk2 = 2
            with v.Fori(0, TURNS) as t:
                for r in range(RING):
                    at = [0]

                    def then(ins, r=r, at=at, t=t):
                        at[0] += 1
                        ins.then_inc(step, 1)
                        v.wait_ge(step, t * (RING * per_chunk2) + (steps2 + r * per_chunk2 + at[0]))

                    start_chunk(2, t, r)
                    pick_next(2, t, r, range(PE_COLS[2]))
                    wait_rows(2, t, r)
                    nc.vector.transpose(by_edge(hT), rows[:, r, :]).then_inc(rows_used[r], 1)
                    v.wait_ge(rows_used[r], use(2, t))
                    plain_chunk(2, t, r, hT, then)
                    assert at[0] == per_chunk2
            steps[0] += NCH * per_chunk2

            for q in range(PIECES):
                x, ks = node_start(2, q)
                parts_sum(piece(q), part_mask[:, :, ks])
                link(mixed(2 * PIECES + q, nt[:, 0, :], nt[:, 1, :]))
                link(nc.vector.tensor_tensor(x, x, part, ALU.add))
                layer_norm(3 * PIECES + q, q)
                v.wait_ge(h_ready, 3 * PIECES + q + 1)
                split_h(q)
                v.wait_ge(parts_ready, 3 * PIECES + q + 1)

            link(nc.vector.memset(carry[:, :], 0.0))
            sh3 = sh_parts[:, :].rearrange("p (j c) -> p j c", c=D)

            def split_sh(t, r, then):
                r1 = (r + 1) % RING
                v.wait_ge(edge_loaded[r1], 16 * (2 * TURNS + 1) if t is None else (t + (2 * TURNS + 1 + (r + 1) // RING)) * 16)
                sh_f = edge_in[:, r1, 0:J * SH].rearrange("p (j c) -> p j c", c=SH)
                then(nc.vector.tensor_copy(sh3[:, :, 0:SH], sh_f))
                nc.vector.tensor_tensor(sh_rest[:, :, :], sh_f, sh3[:, :, 0:SH], ALU.subtract).then_inc(edge_used[r1], 1)
                v.wait_ge(edge_used[r1], TURNS + 1 if t is None else t + (TURNS + 1 + (r + 1) // RING))
                then(nc.vector.tensor_copy(sh3[:, :, SH:2 * SH], sh_rest[:, :, :]))
                then(nc.vector.tensor_tensor(sh3[:, :, 2 * SH:3 * SH], sh_rest[:, :, :], sh3[:, :, SH:2 * SH], ALU.subtract))
                if t is not None:
                    v.wait_ge(bcast_ready[2], t * (6 * RING) + 6 * (r + 1))
                nc.vector.transpose(by_edge(shT[:, :]), sh_parts[:, :]).then_inc(shT_ready, 1)

            split_sh(None, -1, link)
            pick_first(3)
            PICK_AFTER = [(2 * SH * (k + 1)) // (PE_COLS[3] + 1) for k in range(PE_COLS[3])]
            steps3 = steps[0]
            per_chunk3 = 5
            with v.Fori(0, TURNS) as t:
                for r in range(RING):
                    at = [0]

                    def then(ins, r=r, at=at, t=t):
                        at[0] += 1
                        ins.then_inc(step, 1)
                        v.wait_ge(step, t * (RING * per_chunk3) + (steps3 + r * per_chunk3 + at[0]))

                    wait_rows(3, t, r)
                    nc.vector.transpose(by_edge(hT), rows[:, r, :]).then_inc(rows_used[r], 1)
                    start_chunk(3, t, r)
                    v.wait_ge(rows_used[r], use(3, t))
                    for n in range(2 * SH):
                        uses = t * (6 * RING) + (6 * r + n // 3)
                        v.wait_ge(bcast_ready[n % 3], uses + 1)
                        v.wait_ge(weighted_used[n % 3], uses)
                        nc.vector.tensor_tensor(weighted[n % 3][:, 0:HALF], bcast[n % 3][:, 0:HALF],
                                                hT[:, (n % 2) * HALF:(n % 2 + 1) * HALF], ALU.mult).then_inc(weighted_ready[n % 3], 1)
                        if n in PICK_AFTER:
                            pick_next(3, t, r, [PICK_AFTER.index(n)])
                    split_sh(t, r, then)
                    v.wait_ge(msg_copied, chunk_no(0, t, r))
                    plain_chunk(3, t, r, s_sb, then)
                    assert at[0] == per_chunk3
            steps[0] += NCH * per_chunk3

            for q in range(PIECES):
                x, ks = node_start(3, q)
                parts_sum(piece(q), part_mask[:, :, ks])
                nc.vector.tensor_tensor(x, x, agg, ALU.add).then_inc(x_ready, 1)
                v.wait_ge(x_ready, q + 1)


def coupling_coefficients():
    f = math.factorial

    def coefficient(j1, m1, j2, m2, j3, m3):
        if m3 != m1 + m2:
            return 0.0
        pref = (2 * j3 + 1) * f(j3 + j1 - j2) * f(j3 - j1 + j2) * f(j1 + j2 - j3) / f(j1 + j2 + j3 + 1)
        pref *= f(j3 + m3) * f(j3 - m3) * f(j1 - m1) * f(j1 + m1) * f(j2 - m2) * f(j2 + m2)
        s = 0.0
        for k in range(max(0, j2 - j3 - m1, j1 + m2 - j3), min(j1 + j2 - j3, j1 - m1, j2 + m2) + 1):
            s += (-1) ** k / (f(k) * f(j1 + j2 - j3 - k) * f(j1 - m1 - k) * f(j2 + m2 - k)
                              * f(j3 - j2 + m1 + k) * f(j3 - j1 - m2 + k))
        return math.sqrt(pref) * s

    def complex_cg(l1, l2, l3):
        C = np.zeros((2 * l1 + 1, 2 * l2 + 1, 2 * l3 + 1), np.complex128)
        for m1 in range(-l1, l1 + 1):
            for m2 in range(-l2, l2 + 1):
                if -l3 <= m1 + m2 <= l3:
                    C[m1 + l1, m2 + l2, m1 + m2 + l3] = coefficient(l1, m1, l2, m2, l3, m1 + m2)
        return C

    def to_real(l):
        q = np.zeros((2 * l + 1, 2 * l + 1), np.complex128)
        for m in range(-l, 0):
            q[l + m, l + abs(m)] = 1 / np.sqrt(2)
            q[l + m, l - abs(m)] = -1j / np.sqrt(2)
        q[l, l] = 1.0
        for m in range(1, l + 1):
            q[l + m, l + abs(m)] = (-1) ** m / np.sqrt(2)
            q[l + m, l - abs(m)] = 1j * (-1) ** m / np.sqrt(2)
        return (-1j) ** l * q

    found = []
    for l1, l2, l3 in ((0, 0, 0), (0, 1, 1), (1, 0, 1), (1, 1, 0), (1, 1, 1), (2, 1, 1)):
        C = np.einsum("ij,kl,mn,ikn->jlm", to_real(l1), to_real(l2), np.conj(to_real(l3)).T, complex_cg(l1, l2, l3)).real
        found.append(((l1, l2, l3), (C / np.linalg.norm(C)).astype(np.float32)))
    return found


def constants(KT):
    mul = D // 4
    p = np.arange(P)
    feature, group = p % D, p // D
    inner = np.where(feature < mul, feature, (feature - mul) // 3)
    sel = np.zeros((P, SH, P), np.float32)
    for c in range(SH):
        sel[:, c, :] = (group[:, None] == group[None]) & np.isin(feature, (c, SH + c, 2 * SH + c))[:, None]
    cg = coupling_coefficients()
    first = (0, 1, 4)
    coupling = np.zeros((P, len(LAYER3_TERMS), D), np.float32)
    f_in, f_out = feature, np.arange(D)
    for n, (c, i) in enumerate(LAYER3_TERMS):
        (le, ln, lo), C = cg[i]
        m_in = np.where(f_in < mul, 0, (f_in - mul) % 3)
        m_out = np.where(f_out < mul, 0, (f_out - mul) % 3)
        ok = ((f_in >= mul) == (ln == 1))[:, None] & ((f_out >= mul) == (lo == 1))[None]
        table = C[c - first[le]]
        coupling[:, n, :] = np.where(ok, table[np.minimum(m_in, 2 * ln)[:, None], np.minimum(m_out, 2 * lo)[None]], 0.0)
    half = np.zeros((P, 3), np.float32)
    half[:, 0] = feature < D // 2
    half[:, 1] = feature >= D // 2
    half[:, 2] = p
    return {
        "c_ones": np.ones((P, P), np.float32),
        "c_tri": (p[:, None] <= p[None]).astype(np.float32),
        "c_group": (group[:, None] == group[None]).astype(np.float32),
        "c_iota": np.broadcast_to(p.astype(np.int16), (P, P)).copy(),
        "c_half": half,
        "c_sel": sel.reshape(P, SH * P),
        "c_expand": (np.arange(mul)[:, None] == inner[None]).astype(np.float32),
        "c_coupling": coupling,
        "c_target": np.repeat(p[:, None] + P * np.arange(KT // H0)[None], 2, axis=1).reshape(P, -1, 2).astype(np.int16),
    }


_INS = ("x_in", "src_c", "src_pe", "dst_c", "dst_w", "pattern_c", "sh_c", "wq", "wk", "wv", "wo", "w2", "w3",
        "c_ones", "c_tri", "c_group", "c_iota", "c_half", "c_sel", "c_expand", "c_coupling", "c_target")


def laid_out(a):
    n, e = a["x"].shape[0], a["src"].shape[0]
    KT = -(-n // (P * PT)) * PT
    NCH = e // (G * CH)
    assert NCH * G * CH == e and NCH % RING == 0

    def by_chunk(edges):
        return edges.reshape(G, NCH, D, J, -1).transpose(1, 0, 2, 3, 4).reshape(NCH, P, -1)

    dst = a["dst"]
    before = np.concatenate([np.full(1, -1, dst.dtype), dst[:-1]]).reshape(G, NCH, CH)[:, :, :1]
    windows = np.concatenate([before, dst.reshape(G, NCH, CH)], axis=2).transpose(1, 0, 2)
    sh = np.concatenate([a["edge_weight1"], a["edge_attr_3"], a["edge_attr_5"]], axis=1)
    sh_c = by_chunk(sh)
    src_c = by_chunk(a["src"])
    pe_cols = np.concatenate([src_c, src_c, src_c])[0:NCH + 2, :, J - PE_MAX:J]
    src_pe = np.concatenate([pe_cols.transpose(0, 2, 1).reshape(P, -1), pe_cols.transpose(1, 0, 2).reshape(P, -1)], axis=1)
    x = np.concatenate([a["x"], np.zeros((KT * P - n, D), a["x"].dtype)])
    laid = {
        "x_in": x.reshape(KT, P, D).transpose(1, 0, 2),
        "src_c": src_c, "src_pe": src_pe, "dst_c": by_chunk(dst), "dst_w": windows,
        "pattern_c": by_chunk(a["edge_attr_32"]), "sh_c": np.concatenate([sh_c, sh_c[0:1]]),
        "wq": a["L1_gnn_Wq"], "wk": a["L1_gnn_Wk"], "wv": a["L1_gnn_Wv"], "wo": a["L1_gnn_Wo"],
        "w2": a["L2_gnn_W"], "w3": a["L3_gnn_W"], **constants(KT),
    }
    return {name: np.ascontiguousarray(laid[name]) for name in _INS}


def kernel(**inputs):
    import concourse.bacc as bacc
    from concourse.bass_utils import run_bass_kernel_spmd

    arrays = laid_out({name: np.asarray(a) for name, a in inputs.items()})
    n = inputs["x"].shape[0]
    nc = bacc.Bacc("TRN2", target_bir_lowering=False, num_devices=1)
    args = [nc.dram_tensor(name, a.shape, mybir.dt.from_np(a.dtype), kind="ExternalInput").ap() for name, a in arrays.items()]
    args.append(nc.dram_tensor("out", arrays["x_in"].shape, F32, kind="ExternalOutput").ap())
    gnn_kernel(nc, *args)
    result = run_bass_kernel_spmd(nc, [arrays], core_ids=[0])
    y = result.results[0]["out"]
    return y.transpose(1, 0, 2).reshape(-1, D)[:n]
```

```python
from contextlib import ExitStack
import math

import numpy as np
import concourse.bass as bass
from concourse import mybir

F32 = mybir.dt.float32
I32 = mybir.dt.int32
I16 = mybir.dt.int16
BF16 = mybir.dt.bfloat16
F32R = mybir.dt.float32r
ALU = mybir.AluOpType
ACT = mybir.ActivationFunctionType
AX_X = mybir.AxisListType.X

P = 128
D = 32
G = 4
J = 25
CH = D * J
RING = 5
LAYERS = 4
PT = 14
SH = 9
BIG = 1.0e30
H0 = 14
PE_COLS = (6, 4, 6, 3)
PE_MAX = max(PE_COLS)
BIT_BUFS = (3, 2, 3, 3)
TILE_BUFS = (3, 4, 3, 3)
LN_EPS = 1.0e-5
Z_EPS = 1.0e-6
START = 1
HALF = CH // 2
M_COL, Z_COL = D, D + D // 2
LAYER3_TERMS = [(0, 0), (0, 1)] + [(c, i) for c in (1, 2, 3) for i in (2, 3, 4)] + [(c, 5) for c in range(4, 9)]


def gnn_kernel(nc, x_in, src_c, src_pe, dst_c, dst_w, pattern_c, sh_c, wq, wk, wv, wo, w2, w3,
               c_ones, c_tri, c_group, c_iota, c_half, c_sel, c_expand, c_coupling, c_target, out):
    KT = x_in.shape[1]
    NCH = src_c.shape[0]
    TURNS = NCH // RING
    PIECES = KT // PT
    N_PAD = KT * P
    GE = NCH * CH
    E = G * GE
    PC = PT * D
    H1 = KT // H0
    KEYS = PE_MAX * (NCH + 2)
    assert NCH % RING == 0 and KT % PT == 0 and all(RING * PE_COLS[l] % b[l] == 0 for l in range(LAYERS) for b in (TILE_BUFS, BIT_BUFS))

    h_table = nc.dram_tensor("h_table", [N_PAD, D], F32, kind="Internal").ap()
    q_table = nc.dram_tensor("q_table", [N_PAD, D], F32, kind="Internal").ap()
    q_edges = nc.dram_tensor("q_edges", [E + N_PAD, D], F32, kind="Internal").ap()
    key_rows = nc.dram_tensor("key_rows", [NCH + 2, PE_MAX * P], I16, kind="Internal").ap()
    sums = nc.dram_tensor("sums", [E, D], F32, kind="Internal").ap()
    attn = nc.dram_tensor("attn", [E, 2 * D], F32, kind="Internal").ap()
    q_chunks = q_edges[0:E, :].rearrange("(c p j) f -> c p (j f)", p=P, j=J)
    sums_chunks = sums.rearrange("(c p j) f -> c p (j f)", p=P, j=J)
    attn_chunks = attn.rearrange("(c p j) f -> c p (j f)", p=P, j=J)

    with ExitStack() as ctx:
        def sb(name, shape, dt=F32):
            return ctx.enter_context(nc.sbuf_tensor(name, shape, dt))

        def sem(name):
            return ctx.enter_context(nc.semaphore(name))

        def sems(name, n=RING):
            return [sem(f"{name}{r}") for r in range(n)]

        xs = sb("xs", [P, KT, D])
        end_row = sb("end_row", [P, KT], I32)
        begin_row = sb("begin_row", [P, KT], I32)
        part_mask = sb("part_mask", [P, 4, KT])
        part_mean = sb("part_mean", [P, 4, KT])
        part_bias = sb("part_bias", [P, 4, KT])
        counts = sb("counts", [P, KT])
        border = sb("border", [P, 3, 2 * D])
        ln = sb("ln", [P, 4, PT])
        aw = sb("aw", [P, 6, PT])
        idx = sb("idx", [P, RING, J], I32)
        first_idx = sb("first_idx", [G, 1], I32)
        first_q = sb("first_q", [G, D])
        rows = sb("rows", [P, RING, CH])
        edge_in = sb("edge_in", [P, RING, CH])
        dwin = sb("dwin", [P, RING, CH + 1], I32)
        outs = sb("outs", [P, RING, 2 * CH])
        node_rows = outs[:, :, :].rearrange("p r c -> p (r c)")
        h_parts = sb("h_parts", [P, 2, KT * D], F32R)
        keys = sb("keys", [P, RING, PE_MAX * P], I16)
        h0_of = sb("h0_of", [P, KEYS], I16)
        h0_mask = sb("h0_mask", [P, PE_MAX, H0])
        tile_rows = sb("tile_rows", [P, H0 * D])
        target = sb("target", [P, H1, 2], I16)
        one_hots = [sb(f"one_hot{b}", [P, H1, P], F32R) for b in range(max(TILE_BUFS))]
        bit_hots = [sb(f"bit_hot{b}", [P, H1, P], BF16)[:, :, :] for b in range(2)]
        work = sb("work", [P, 14, CH])
        (hT, qT, keep, qh, prod, u, d, Z, ph, O, mz_m, mz, nb, s_sb) = (work[:, k, :] for k in range(14))
        one_hot_lo = work[:, 5:7, :].rearrange("p a c -> p (a c)").bitcast(BF16).rearrange("p (j n) -> p j n", n=P)
        one_hot_hi = work[:, 7:9, :].rearrange("p a c -> p (a c)").bitcast(BF16)[:, 0:J * KT]\
            .rearrange("p (j n) -> p j n", n=KT)
        node_work = work[:, 10:14, :].rearrange("p a c -> p (a c)")[:, 0:6 * PC].rearrange("p (a c) -> p a c", c=PC)
        h_new, nT, nt = node_work[:, 0:2, :], node_work[:, 2:4, :], node_work[:, 4:6, :]
        mx = sb("mx", [P, CH + 1])
        carry = sb("carry", [P, 4])
        sh_parts, shT = u[:, 0:CH // 2].bitcast(BF16), u[:, CH // 2:CH].bitcast(BF16)
        sh_rest = d[:, 0:J * SH].rearrange("p (j c) -> p j c", c=SH)
        rise = qT
        weighted = [qT, qh, prod]
        bit_hots.append(nb[:, 0:H1 * P // 2].bitcast(BF16).rearrange("p (h n) -> p h n", n=P))
        spare = work[:, 13, 6 * PC - 3 * CH:CH]
        dst_t = spare[:, 0:RING * J].bitcast(I32).rearrange("p (r j) -> p r j", j=J)
        dst_parts = spare[:, RING * J:RING * J + 2 * J].bitcast(I32).rearrange("p (a j) -> p a j", j=J)
        dst_pairs = spare[:, RING * J + 2 * J:RING * J + 4 * J].bitcast(I16).rearrange("p (a j b) -> p a j b", j=J, b=2)
        ones, tri = mx[:, 0:P], mx[:, P:2 * P]
        group_ones = sb("group_ones", [P, P])
        iota = sb("iota", [P, P], I16)
        half = sb("half", [P, 3])
        sel = sb("sel", [P, SH, P], BF16)
        staged = [0]

        def stage(parts, *shape):
            n = int(np.prod(shape))
            at, staged[0] = staged[0], staged[0] + n
            flat = node_rows[0:parts, at:at + n]
            return flat if len(shape) == 1 else flat.rearrange("p (a b) -> p a b", b=shape[1])

        sel_f = stage(P, SH * P)
        expand = stage(8, P)
        coupling = stage(P, len(LAYER3_TERMS), D)
        eps = sb("eps", [P, 1])
        w_in = stage(D, 4, D)
        w_t = stage(D, 3, D)
        w_t_wide = stage(D, 2, P)
        w3_in = stage(8, 6, 8)
        w3_wide = stage(8, 6, D)
        w3_full = stage(P, 6, D)
        t_sum = stage(P, SH, D)
        t_tmp = stage(P, D)
        early = work[:, 2:10, :].rearrange("p a c -> p (a c)")[:, 0:8 * KEYS].rearrange("p (a k) -> p a k", a=4)
        src_i, src_f = [early[:, k, :].bitcast(I32) for k in (0, 1)], [early[:, k, :] for k in (2, 3)]
        key_i16 = stage(P, -(-KEYS // 2)).bitcast(I16)[:, 0:KEYS]
        bd_q = sb("bd_q", [P, P])
        bd_vo = sb("bd_vo", [P, P])
        bd_w2 = sb("bd_w2", [P, P])
        bd_t = sb("bd_t", [P, SH, P])

        banks = [ctx.enter_context(nc.psum_tensor(f"bank{b}", [P, 512], F32)) for b in range(6)]
        bcast = banks[0:3]
        tile_banks = banks[3:6] + banks[0:2]
        node_ps = banks[5]
        acc = ctx.enter_context(nc.psum_tensor("acc", [P, 2, 512], F32))

        consts_loaded, weights_loaded, x_loaded = sem("consts_loaded"), sem("weights_loaded"), sem("x_loaded")
        zeros_ready, q_zeroed = sem("zeros_ready"), sem("q_zeroed")
        idx_loaded, dwin_loaded, edge_loaded = sems("idx_loaded"), sems("dwin_loaded"), sems("edge_loaded")
        dst_loaded = sems("dst_loaded")
        rows_gathered = [sems(f"rows_gathered{a}_") for a in range(2)]
        chunk_begun = sem("chunk_begun")
        parts_ready, keys_ready, keys_stored, keys_loaded = sem("parts_ready"), sem("keys_ready"), sem("keys_stored"), sems("keys_loaded")
        one_hot_made, one_hot_cast, tile_ready, tile_used, picked = sem("one_hot_made"), sem("one_hot_cast"), sem("tile_ready"), sem("tile_used"), sem("picked")
        rows_used, edge_used, keep_ready = sems("rows_used"), sems("edge_used"), sems("keep_ready")
        outs_ready, outs_stored = sems("outs_ready"), sems("outs_stored")
        one_hot_ready, counts_ready, counts_added = sem("one_hot_ready"), sem("counts_ready"), sem("counts_added")
        prod_ready, score_ready, score_copied, nb_ready = sem("prod_ready"), sem("score_ready"), sem("score_copied"), sem("nb_ready")
        decay_in, decay_ready, p_in, p_ready = sem("decay_in"), sem("decay_ready"), sem("p_in"), sem("p_ready")
        mx_ready, rise_ready, mz_m_ready = sem("mx_ready"), sem("rise_ready"), sem("mz_m_ready")
        shT_ready = sem("shT_ready")
        bcast_ready, weighted_ready, weighted_used = sems("bcast_ready", 3), sems("weighted_ready", 3), sems("weighted_used", 3)
        msg_copied = sem("msg_copied")
        mask_made = sem("mask_made")
        step = sem("step")
        h_ready, h_stored = sem("h_ready"), sems("h_stored", 2)
        q_ready, q_stored, q_scattered = sem("q_ready"), sem("q_stored"), sem("q_scattered")
        first_loaded, first_gathered, first_stored = sem("first_loaded"), sem("first_gathered"), sem("first_stored")
        node_index_ready, node_gathered = sem("node_index_ready"), sems("node_gathered", PIECES)
        border_loaded = sem("border_loaded")
        prep_lhs, prep_ps = sem("prep_lhs"), sem("prep_ps")
        var_ready, std_ready = sem("var_ready"), sem("std_ready")
        part_in, part_exp = sem("part_in"), sem("part_exp")
        mix_in, mix_ps, mix_out = sem("mix_in"), sem("mix_ps"), sem("mix_out")
        x_ready, x_stored = sem("x_ready"), sem("x_stored")

        block = ctx.enter_context(nc.Block())

        def use(l, t, more=0):
            return t + (l * TURNS + 1 + more)

        def gathers(l, t):
            each = 16 * (J - PE_COLS[l])
            return t * each + (each + (16 * TURNS * (J - PE_COLS[l - 2]) if l >= 2 else 0))

        tile_base = [sum((NCH + 1) * PE_COLS[k] for k in range(l)) for l in range(LAYERS + 1)]
        one_hot_base = [tile_base[l] + sum(TILE_BUFS[0:l]) for l in range(LAYERS + 1)]

        def tile_no(base, l, t, i):
            return base[l] + i if t is None else t * (RING * PE_COLS[l]) + (base[l] + i)

        def keys_use(l, t, chunk):
            n = l * (TURNS + (1 if chunk % RING < 2 else 0)) + chunk // RING + 1
            return n if t is None else t + n

        def chunk_no(l, t, r, more=0):
            return t * RING + (l * NCH + r + 1 + more)

        @block.sync
        def _(sp):
            sp.dma_start(xs[:, :, :], x_in).then_inc(x_loaded, 16)
            sp.dma_start(src_i[0], src_pe).then_inc(consts_loaded, 16)
            for tile, const in ((ones, c_ones), (tri, c_tri), (group_ones, c_group), (iota, c_iota), (half, c_half),
                                (expand, c_expand)):
                sp.dma_start(tile[:, :], const).then_inc(consts_loaded, 16)
            sp.dma_start(sel_f, c_sel).then_inc(consts_loaded, 16)
            sp.dma_start(coupling[:, :, :], c_coupling).then_inc(consts_loaded, 16)
            sp.dma_start(target[:, :, :], c_target).then_inc(consts_loaded, 16)
            for n, w in enumerate((wq, wk, wv, wo)):
                sp.dma_start(w_in[:, n, :], w).then_inc(weights_loaded, 16)
            sp.dma_start(w3_in[:, :, :], w3.rearrange("n i o -> i n o")).then_inc(weights_loaded, 16)
            sp.wait_ge(zeros_ready, 1)
            for g in range(G):
                sp.dma_start(bd_w2[D * g:D * g + D, D * g:D * g + D], w2).then_inc(weights_loaded, 16)
            sp.dma_start(first_idx[:, :], dst_c[0, 0:P:D, 0:1], allow_slow_non_contiguous=True).then_inc(first_loaded, 16)

            def store_h(n):
                q = n % PIECES
                sp.wait_ge(h_ready, n + 1)
                sp.dma_start(h_table[q * PT * P:(q + 1) * PT * P, :].rearrange("(k p) f -> p k f", p=P),
                             h_new[:, n % 2, :].rearrange("p (k f) -> p k f", f=D)).then_inc(h_stored[n % 2], 16)

            for q in range(PIECES):
                store_h(q)
            sp.wait_ge(keys_ready, 1)
            sp.dma_start(key_rows.rearrange("c k -> (c k)").rearrange("(p n) -> p n", p=P), key_i16).then_inc(keys_stored, 16)

            def load_keys(l, t, chunk):
                n = PE_COLS[l] * P
                c = bass.ds(chunk if t is None else t * RING + chunk, 1)
                sp.dma_start(keys[:, chunk % RING, 0:n], key_rows[c, PE_MAX * P - n:PE_MAX * P].broadcast_to([P, n]))\
                    .then_inc(keys_loaded[chunk % RING], 16)

            for l in range(LAYERS):
                if l == 0:
                    sp.wait_ge(keys_stored, 16)
                else:
                    sp.wait_ge(one_hot_made, one_hot_base[l] + START)
                load_keys(l, None, 0)
                load_keys(l, None, 1)
                with sp.Fori(0, TURNS) as t:
                    for r in range(RING):
                        c = bass.ds(t * RING + r, 1)
                        sp.wait_ge(rows_used[r], use(l, t, START - 1))
                        sp.dma_start(idx[:, r, :], src_c[c].rearrange("o p j -> (o p) j")).then_inc(idx_loaded[r], 16)
                        sp.wait_ge(keep_ready[r], use(l, t, START - 1))
                        for g in range(G):
                            sp.dma_start(dwin[D * g:D * g + D, r, :],
                                         dst_w[c, g, :].broadcast_to([D, CH + 1])).then_inc(dwin_loaded[r], 16)
                        if l == 0:
                            sp.dma_start(edge_in[:, r, :], pattern_c[c].rearrange("o p c -> (o p) c")).then_inc(edge_loaded[r], 16)
                            sp.wait_ge(one_hot_ready, t * RING + START)
                            sp.dma_start(dst_t[:, r, :], dst_c[c].rearrange("o p j -> (o p) j")).then_inc(dst_loaded[r], 16)
                        if l == 1:
                            sp.wait_ge(first_stored, 16)
                            sp.wait_ge(edge_used[r], t + START)
                            sp.dma_start(edge_in[:, r, :], q_chunks[c].rearrange("o p c -> (o p) c")).then_inc(edge_loaded[r], 16)
                        if l == 3:
                            sp.wait_ge(edge_used[r], t + (TURNS + START))
                            sp.dma_start(edge_in[:, r, 0:J * SH], sh_c[c].rearrange("o p c -> (o p) c")).then_inc(edge_loaded[r], 16)
                        sp.wait_ge(one_hot_made, tile_no(one_hot_base, l, t, max(r - 2, 0) * PE_COLS[l] + START))
                        load_keys(l, t, r + 2)
                if l == 3:
                    sp.wait_ge(edge_used[0], 2 * TURNS + START)
                    sp.dma_start(edge_in[:, 0, 0:J * SH], sh_c[NCH]).then_inc(edge_loaded[0], 16)
                for r in range(RING):
                    sp.wait_ge(outs_stored[r], 16 * (l + 1) * TURNS + START)
                if l == 1:
                    last = attn_chunks[NCH - 1:NCH, D - 1:3 * D:D, (J - 1) * 2 * D:J * 2 * D]
                    sp.dma_start(border[:, :, :], last.broadcast_to([P, 3, 2 * D])).then_inc(border_loaded, 16)
                else:
                    last = sums_chunks[NCH - 1:NCH, D - 1:3 * D:D, (J - 1) * D:J * D]
                    sp.dma_start(border[:, :, 0:D], last.broadcast_to([P, 3, D])).then_inc(border_loaded, 16)
                for q in range(PIECES):
                    if l < LAYERS - 1:
                        store_h((l + 1) * PIECES + q)
                    if l == 0:
                        sp.wait_ge(q_ready, q + 1)
                        sp.dma_start(q_table[q * PT * P:(q + 1) * PT * P, :].rearrange("(k p) f -> p k f", p=P),
                                     node_rows[:, q * PC:(q + 1) * PC].rearrange("p (k f) -> p k f", f=D)).then_inc(q_stored, 16)
                    if l == LAYERS - 1:
                        sp.wait_ge(x_ready, q + 1)
                        sp.dma_start(out[:, q * PT:(q + 1) * PT, :], xs[:, q * PT:(q + 1) * PT, :]).then_inc(x_stored, 16)
            sp.wait_ge(x_stored, 16 * PIECES)

        @block.gpsimd
        def _(pool):
            for l in range(LAYERS):
                if l == 1:
                    pool.wait_ge(q_zeroed, 16 * TURNS)
                    for q in range(PIECES):
                        pool.wait_ge(q_ready, q + 1)
                        for k in range(q * PT, (q + 1) * PT):
                            nc.gpsimd.indirect_dma_start(
                                out=q_edges[:, :], out_offset=bass.IndirectOffsetOnAxis(ap=begin_row[:, k:k + 1], axis=0),
                                in_=node_rows[:, k * D:(k + 1) * D], in_offset=None).then_inc(q_scattered, 16)
                    pool.wait_ge(first_loaded, 16)
                    pool.wait_ge(q_stored, 16 * PIECES)
                    nc.gpsimd.indirect_dma_start(
                        out=first_q[:, :], out_offset=None, in_=q_table[:, :],
                        in_offset=bass.IndirectOffsetOnAxis(ap=first_idx[:, :], axis=0)).then_inc(first_gathered, 16)
                    pool.wait_ge(first_gathered, 16)
                    pool.wait_ge(q_scattered, 16 * KT)
                    pool.dma_start(q_chunks[0, 0:P:D, 0:D], first_q[:, :]).then_inc(first_stored, 16)
                for a in range(2):
                    pool.wait_ge(h_stored[a], 16 * ((PIECES * (l + 1) + 1 - a) // 2))
                with pool.Fori(0, TURNS) as t:
                    for r in range(RING):
                        pool.wait_ge(rows_used[r], use(l, t, START - 1))
                        pool.wait_ge(idx_loaded[r], use(l, t) * 16)
                        pool.sem_inc(chunk_begun, 1)
                        for j in range(J - PE_COLS[l]):
                            nc.gpsimd.indirect_dma_start(
                                out=rows[:, r, j * D:(j + 1) * D], out_offset=None, in_=h_table[:, :],
                                in_offset=bass.IndirectOffsetOnAxis(ap=idx[:, r, j:j + 1], axis=0)).then_inc(rows_gathered[l % 2][r], 16)
                if l == 0:
                    pool.wait_ge(node_index_ready, 1)
                for r in range(RING):
                    pool.wait_ge(outs_stored[r], 16 * (l + 1) * TURNS + START)
                table, width = (attn, 2 * D) if l == 1 else (sums, D)
                for k in range(KT):
                    nc.gpsimd.indirect_dma_start(
                        out=node_rows[:, k * width:(k + 1) * width], out_offset=None, in_=table[:, :],
                        in_offset=bass.IndirectOffsetOnAxis(ap=end_row[:, k:k + 1], axis=0)).then_inc(node_gathered[k // PT], 16)

        @block.scalar
        def _(act):
            for s in (*outs_stored, score_copied, msg_copied):
                act.sem_inc(s, START)

            def std(n):
                act.wait_ge(var_ready, n + 1)
                nc.scalar.activation(ln[:, 2, :], ln[:, 1, :], ACT.Sqrt, bias=eps[:, :], scale=1.0 / D).then_inc(std_ready, 1)

            def mix_copy(n, scale):
                act.wait_ge(mix_ps, n + 1)
                nc.scalar.activation(nT[:, 1, :], node_ps[:, 0:PC], ACT.Copy, scale=scale).then_inc(mix_out, 1)

            def store(l, t, r, chunks, width):
                act.wait_ge(outs_ready[r], use(l, t))
                act.dma_start(chunks[bass.ds(t * RING + r, 1)].rearrange("o p c -> (o p) c"),
                              outs[:, r, 0:width]).then_inc(outs_stored[r], 16)

            def cast_one_hot(l, t, i):
                act.wait_ge(one_hot_made, tile_no(one_hot_base, l, t, i + 1 + START))
                nc.scalar.activation(one_hots[i % TILE_BUFS[l]][:, :, :], bit_hots[i % BIT_BUFS[l]], ACT.Copy).then_inc(one_hot_cast, 1)

            def cast_first(l):
                for i in range(PE_COLS[l] + TILE_BUFS[l]):
                    cast_one_hot(l, None, i)

            def cast_next(l, t, r, which):
                for q in which:
                    cast_one_hot(l, t, (r + 1) * PE_COLS[l] + q + TILE_BUFS[l])

            for q in range(PIECES):
                std(q)
            act.wait_ge(zeros_ready, 1)
            cast_first(0)
            with act.Fori(0, TURNS) as t:
                act.dma_start(q_edges[bass.ds(t * (RING * P * J), RING * P * J), :].rearrange("(p r a) f -> p r (a f)", p=P, r=RING),
                              qT.unsqueeze(1).broadcast_to([P, RING, CH])).then_inc(q_zeroed, 16)
                for r in range(RING):
                    cast_next(0, t, r, range(PE_COLS[0]))
                    store(0, t, r, sums_chunks, CH)
            for q in range(PIECES):
                std(PIECES + q)
                mix_copy(q, float(D) ** -0.5)
            cast_first(1)
            with act.Fori(0, TURNS) as t:
                for r in range(RING):
                    n = chunk_no(0, t, r)
                    act.wait_ge(keep_ready[r], use(1, t, START))
                    nc.scalar.activation(nb, keep, ACT.Copy, scale=BIG, bias=-BIG).then_inc(nb_ready, 1)
                    act.wait_ge(score_ready, n)
                    nc.scalar.activation(s_sb.rearrange("p (a c) -> p a c", a=2), acc[:, :, 0:HALF], ACT.Copy).then_inc(score_copied, 1)
                    cast_next(1, t, r, range(2))
                    act.wait_ge(rise_ready, n)
                    nc.scalar.activation(d, rise, ACT.Relu, scale=-1.0).then_inc(p_in, 1)
                    nc.scalar.activation(u, rise, ACT.Relu).then_inc(decay_in, 1)
                    act.wait_ge(p_in, n)
                    nc.scalar.activation(d, d, ACT.Exp, scale=-1.0).then_inc(p_ready, 1)
                    act.wait_ge(decay_in, n)
                    nc.scalar.activation(u, u, ACT.Exp, scale=-1.0).then_inc(decay_ready, 1)
                    nc.scalar.activation(mz_m, mx[:, 1:CH + 1], ACT.Copy, scale=half[:, 0:1]).then_inc(mz_m_ready, 1)
                    cast_next(1, t, r, range(2, PE_COLS[1]))
                    store(1, t, r, attn_chunks, 2 * CH)
            for q in range(PIECES):
                act.wait_ge(part_in, q + 1)
                nc.scalar.activation(aw[:, 0:4, :], aw[:, 0:4, :], ACT.Exp).then_inc(part_exp, 1)
                mix_copy(PIECES + q, 1.0)
                std(2 * PIECES + q)
            cast_first(2)
            with act.Fori(0, TURNS) as t:
                for r in range(RING):
                    cast_next(2, t, r, range(PE_COLS[2]))
                    store(2, t, r, sums_chunks, CH)
            for q in range(PIECES):
                mix_copy(2 * PIECES + q, 1.0)
                std(3 * PIECES + q)
            cast_first(3)
            with act.Fori(0, TURNS) as t:
                for r in range(RING):
                    cast_next(3, t, r, range(PE_COLS[3]))
                    act.wait_ge(weighted_used[2], t * (6 * RING) + (6 * r + 6 + START))
                    nc.scalar.activation(s_sb.rearrange("p (a c) -> p a c", a=2), acc[:, :, 0:HALF], ACT.Copy).then_inc(msg_copied, 1)
                    store(3, t, r, sums_chunks, CH)

        @block.tensor
        def _(pe):
            for s in weighted_used:
                pe.sem_inc(s, START)
            pe.wait_ge(prep_lhs, 1)
            nc.tensor.matmul(acc[:, 0, 0:D], w_t_wide[:, 0, :], w_t[:, 1, :], start=True, stop=True)
            nc.tensor.matmul(acc[:, 0, D:2 * D], w_t_wide[:, 1, :], w_in[:, 3, :], start=True, stop=True)
            nc.tensor.matmul(acc[:, 1, 0:6 * D], expand[:, :], w3_wide[:, :, :], start=True, stop=True).then_inc(prep_ps, 1)
            def gather_tile(l, t, i):
                b = i % TILE_BUFS[l]
                pe.wait_ge(one_hot_cast, tile_no(one_hot_base, l, t, i + 1))
                if t is not None or i >= TILE_BUFS[l]:
                    pe.wait_ge(tile_used, tile_no(tile_base, l, t, i + 1 - TILE_BUFS[l]))
                for h1 in range(H1):
                    for part in range(2):
                        last = nc.tensor.matmul(tile_banks[b][:, 0:H0 * D], one_hots[b][:, h1, :],
                                                h_parts[:, part, h1 * H0 * D:(h1 + 1) * H0 * D],
                                                start=(h1 == 0 and part == 0), stop=(h1 == H1 - 1 and part == 1))
                last.then_inc(tile_ready, 1)

            def gather_first(l):
                pe.wait_ge(parts_ready, PIECES * (l + 1))
                for i in range(PE_COLS[l]):
                    gather_tile(l, None, i)

            def gather_next(l, t, r, which):
                for q in which:
                    gather_tile(l, t, (r + 1) * PE_COLS[l] + q)

            pe.wait_ge(prep_lhs, 2)
            gather_first(0)
            with pe.Fori(0, TURNS) as t:
                for r in range(RING):
                    gather_next(0, t, r, range(2))
                    pe.wait_ge(one_hot_ready, chunk_no(0, t, r, START))
                    pe.wait_ge(counts_added, t * RING + (r + START))
                    for j in range(J):
                        last = nc.tensor.matmul(acc[:, 0, 0:KT], one_hot_lo[:, j, :], one_hot_hi[:, j, :],
                                                start=(j == 0), stop=(j == J - 1))
                    last.then_inc(counts_ready, 1)
                    gather_next(0, t, r, range(2, PE_COLS[0]))
            pe.wait_ge(counts_added, NCH + START)
            nc.tensor.matmul(acc[:, 0, 0:KT], tri[:, :], counts[:, :], start=True, stop=True)
            nc.tensor.matmul(acc[:, 1, 0:KT], ones, counts[:, :], start=True, stop=True).then_inc(prep_ps, 1)

            def mix(n, weight):
                pe.wait_ge(mix_in, n + 1)
                nc.tensor.matmul(node_ps[:, 0:PC], weight[:, :], nT[:, 0, :], start=True, stop=True).then_inc(mix_ps, 1)

            for q in range(PIECES):
                mix(q, bd_q)
            gather_first(1)
            with pe.Fori(0, TURNS) as t:
                for r in range(RING):
                    gather_next(1, t, r, range(2))
                    pe.wait_ge(prod_ready, chunk_no(0, t, r))
                    pe.wait_ge(score_copied, t * RING + (r + START))
                    for a in range(2):
                        last = nc.tensor.matmul(acc[:, a, 0:HALF], group_ones[:, :], prod[:, a * HALF:(a + 1) * HALF],
                                                start=True, stop=True)
                    last.then_inc(score_ready, 1)
                    gather_next(1, t, r, range(2, PE_COLS[1]))
            for q in range(PIECES):
                mix(PIECES + q, bd_vo)
            gather_first(2)
            with pe.Fori(0, TURNS) as t:
                for r in range(RING):
                    gather_next(2, t, r, range(PE_COLS[2]))
            for q in range(PIECES):
                mix(2 * PIECES + q, bd_w2)

            def spread(t, r, n):
                pe.wait_ge(weighted_ready[n % 3], t * (6 * RING) + (6 * r + n // 3 + START))
                if n == 0:
                    pe.wait_ge(shT_ready, chunk_no(0, t, r))
                half_n = slice((n % 2) * HALF, (n % 2 + 1) * HALF)
                nc.tensor.matmul(bcast[n % 3][:, 0:HALF], sel[:, n // 2, :], shT[:, half_n],
                                 start=True, stop=True).then_inc(bcast_ready[n % 3], 1)

            def couple(t, r, n):
                pe.wait_ge(weighted_ready[n % 3], t * (6 * RING) + (6 * r + n // 3 + 1 + START))
                if n == 0:
                    pe.wait_ge(msg_copied, t * RING + (r + START))
                nc.tensor.matmul(acc[:, n % 2, 0:HALF], bd_t[:, n // 2, :], weighted[n % 3][:, 0:HALF],
                                 start=(n // 2 == 0), stop=(n // 2 == SH - 1)).then_inc(weighted_used[n % 3], 1)

            gather_first(3)
            with pe.Fori(0, TURNS) as t:
                for r in range(RING):
                    gather_next(3, t, r, range(1))
                    for n in range(3):
                        spread(t, r, n)
                    gather_next(3, t, r, range(1, PE_COLS[3]))
                    for n in range(2 * SH):
                        couple(t, r, n)
                        if n + 3 < 2 * SH:
                            spread(t, r, n + 3)

        @block.vector
        def _(v):
            for s in (*rows_used, *keep_ready, *edge_used, *weighted_ready, one_hot_ready, one_hot_made, counts_added):
                v.sem_inc(s, START)
            steps = [0]

            def link(ins):
                steps[0] += 1
                ins.then_inc(step, 1)
                v.wait_ge(step, steps[0])

            def by_edge(ap):
                return ap.rearrange("p (i j) -> p j i", j=J)

            def pairs(ap):
                return ap.rearrange("p a (n b) -> p a n b", b=2)

            def spread_over(ap, n):
                return ap.unsqueeze(2).broadcast_to([P, ap.shape[1], n])

            nc.vector.memset(bd_w2[:, :], 0.0)
            link(nc.vector.memset(qT, 0.0))
            nc.vector.memset(carry[:, :], 0.0).then_inc(zeros_ready, 1)
            nc.vector.memset(eps[:, :], LN_EPS)
            nc.vector.memset(bd_q[:, :], 0.0)
            nc.vector.memset(bd_vo[:, :], 0.0)
            nc.vector.memset(bd_t[:, :, :], 0.0)
            link(nc.vector.memset(counts[:, :], 0.0))

            def layer_norm(n, q):
                x = xs[:, q * PT:(q + 1) * PT, :]
                xc = nt[:, 0, :].rearrange("p (k f) -> p k f", f=D)
                sq = nt[:, 1, :].rearrange("p (k f) -> p k f", f=D)
                link(nc.vector.reduce_sum(ln[:, 0, :], x, axis=AX_X))
                link(nc.vector.tensor_scalar(ln[:, 0, :], ln[:, 0, :], -1.0 / D, None, ALU.mult))
                link(nc.vector.tensor_tensor(xc, x, spread_over(ln[:, 0, :], D), ALU.add))
                link(nc.vector.tensor_tensor(sq, xc, xc, ALU.mult))
                nc.vector.reduce_sum(ln[:, 1, :], sq, axis=AX_X).then_inc(var_ready, 1)
                v.wait_ge(std_ready, n + 1)
                link(nc.vector.reciprocal(ln[:, 3, :], ln[:, 2, :]))
                if n >= 2:
                    v.wait_ge(h_stored[n % 2], 16 * (n // 2))
                h = h_new[:, n % 2, :]
                nc.vector.scalar_tensor_tensor(out=h.rearrange("p (k f) -> p k f", f=D), in0=xc, scalar=0.0,
                                               in1=spread_over(ln[:, 3, :], D), op0=ALU.max, op1=ALU.mult).then_inc(h_ready, 1)
                v.wait_ge(h_ready, n + 1)
                high, low = (h_parts[:, k, q * PC:(q + 1) * PC] for k in range(2))
                link(nc.vector.tensor_copy(high, h))
                nc.vector.tensor_tensor(low, h, high, ALU.subtract).then_inc(parts_ready, 1)
                v.wait_ge(parts_ready, n + 1)

            v.wait_ge(x_loaded, 16)
            for q in range(PIECES):
                layer_norm(q, q)

            v.wait_ge(consts_loaded, 10 * 16)
            link(nc.vector.tensor_scalar(src_i[1], src_i[0], P.bit_length() - 1, None, ALU.logical_shift_right))
            link(nc.vector.tensor_copy(src_f[0], src_i[1]))
            link(nc.vector.tensor_scalar(src_f[1], src_f[0], 1.0 / H0, 0.5 / H0 - 0.5, ALU.mult, ALU.add))
            link(nc.vector.tensor_scalar(src_f[1], src_f[1], 2.0 ** 23 + 2.0 ** 22, None, ALU.add))
            link(nc.vector.tensor_scalar(src_f[1], src_f[1], -(2.0 ** 23 + 2.0 ** 22), None, ALU.add))
            link(nc.vector.scalar_tensor_tensor(out=src_f[0][:, KEYS:2 * KEYS], in0=src_f[1][:, KEYS:2 * KEYS], scalar=-float(H0),
                                                in1=src_f[0][:, KEYS:2 * KEYS], op0=ALU.mult, op1=ALU.add))
            link(nc.vector.tensor_copy(h0_of[:, :], src_f[0][:, KEYS:2 * KEYS]))
            link(nc.vector.tensor_scalar(src_i[1], src_i[0], P - 1, None, ALU.bitwise_and))
            link(nc.vector.tensor_copy(src_f[0][:, 0:KEYS], src_i[1][:, 0:KEYS]))
            nc.vector.scalar_tensor_tensor(out=key_i16, in0=src_f[1][:, 0:KEYS], scalar=float(P), in1=src_f[0][:, 0:KEYS],
                                           op0=ALU.mult, op1=ALU.add).then_inc(keys_ready, 1)

            def make_one_hot(l, t, i):
                chunk, q = i // PE_COLS[l], i % PE_COLS[l]
                v.wait_ge(keys_loaded[chunk % RING], keys_use(l, t, chunk) * 16)
                by_pair = [P, H1, P // 2, 2]
                if t is not None or one_hot_base[l] + i >= BIT_BUFS[l]:
                    v.wait_ge(one_hot_cast, tile_no(one_hot_base, l, t, i + 1 - BIT_BUFS[l]))
                nc.vector.tensor_tensor(pairs(bit_hots[i % BIT_BUFS[l]]),
                                        pairs(keys[:, chunk % RING, q * P:(q + 1) * P].unsqueeze(1)).broadcast_to(by_pair),
                                        target[:, :, :].unsqueeze(2).broadcast_to(by_pair), ALU.is_equal).then_inc(one_hot_made, 1)

            def mask_h0(l, t, chunk):
                n = PE_COLS[l]
                at = chunk * PE_MAX + PE_MAX - n
                of = h0_of[:, bass.ds(at if t is None else t * (RING * PE_MAX) + at, n)]
                nc.vector.tensor_tensor(h0_mask[:, 0:n, :], of.unsqueeze(2).broadcast_to([P, n, H0]),
                                        iota[:, 0:H0].unsqueeze(1).broadcast_to([P, n, H0]), ALU.is_equal).then_inc(mask_made, 1)

            def pick(l, t, i):
                chunk, q, b = i // PE_COLS[l], i % PE_COLS[l], i % TILE_BUFS[l]
                if q == 0:
                    mask_h0(l, t, chunk)
                    v.wait_ge(mask_made, (t * RING if t is not None else 0) + (l * (NCH + 1) + chunk + 1))
                v.wait_ge(tile_ready, tile_no(tile_base, l, t, i + 1))
                if t is not None or tile_base[l] + i > 0:
                    v.wait_ge(picked, tile_no(tile_base, l, t, i))
                nc.vector.tensor_tensor(tile_rows[:, :].rearrange("p (h f) -> p h f", f=D),
                                        tile_banks[b][:, 0:H0 * D].rearrange("p (h f) -> p h f", f=D),
                                        spread_over(h0_mask[:, q, :], D), ALU.mult).then_inc(tile_used, 1)
                make_one_hot(l, t, i + TILE_BUFS[l])
                v.wait_ge(tile_used, tile_no(tile_base, l, t, i + 1))
                j = J - PE_COLS[l] + q
                nc.vector.reduce_sum(rows[:, chunk % RING, j * D:(j + 1) * D], tile_rows[:, :].rearrange("p (h f) -> p f h", f=D),
                                     axis=AX_X).then_inc(picked, 1)

            def pick_first(l):
                for i in range(TILE_BUFS[l]):
                    make_one_hot(l, None, i)
                for i in range(PE_COLS[l]):
                    pick(l, None, i)

            def pick_next(l, t, r, which):
                for q in which:
                    pick(l, t, (r + 1) * PE_COLS[l] + q)

            def wait_rows(l, t, r):
                v.wait_ge(rows_gathered[l % 2][r], gathers(l, t))
                v.wait_ge(picked, tile_no(tile_base, l, t, (r + 1) * PE_COLS[l]))

            v.wait_ge(weights_loaded, (5 + G) * 16)
            nc.vector.tensor_copy(sel[:, :, :].rearrange("p c m -> p (c m)"), sel_f)
            for n in range(3):
                nc.vector.transpose(w_t[:, n, :], w_in[:, n, :])
            nc.vector.tensor_copy(w3_wide[:, :, 0:8], w3_in[:, :, :])
            for k in range(3):
                last = nc.vector.tensor_copy(w3_wide[:, :, 8 + k:D:3], w3_in[:, :, :])
            link(last)
            for n, m in ((0, 0), (1, 2)):
                last = nc.vector.tensor_copy(w_t_wide[:, n, :].rearrange("p (g f) -> p g f", g=G),
                                             w_t[:, m:m + 1, :].broadcast_to([D, G, D]))
            last.then_inc(prep_lhs, 1)
            v.wait_ge(prep_ps, 1)
            for g in range(G):
                q = slice(D * g, D * g + D)
                nc.vector.tensor_copy(bd_q[q, q], acc[q, 0, 0:D])
                nc.vector.tensor_copy(bd_vo[q, q], acc[q, 0, D:2 * D])
            link(nc.vector.tensor_copy(w3_full[:, :, :].rearrange("p n f -> p (n f)"), acc[:, 1, 0:6 * D]))
            seen = set()
            for n, (c, i) in enumerate(LAYER3_TERMS):
                to = t_tmp[:, :] if c in seen else t_sum[:, c, :]
                link(nc.vector.tensor_tensor(to, w3_full[:, i, :], coupling[:, n, :], ALU.mult))
                if c in seen:
                    link(nc.vector.tensor_tensor(t_sum[:, c, :], t_sum[:, c, :], t_tmp[:, :], ALU.add))
                seen.add(c)
            for g in range(G):
                q = slice(D * g, D * g + D)
                last = nc.vector.tensor_copy(bd_t[q, :, q], t_sum[q, :, :])
            link(last)
            nc.vector.memset(aw[:, :, :], 0.0).then_inc(prep_lhs, 1)

            def start_chunk(l, t, r):
                v.wait_ge(dwin_loaded[r], use(l, t) * (16 * G))
                nc.vector.tensor_tensor(keep, dwin[:, r, 1:CH + 1], dwin[:, r, 0:CH], ALU.is_equal).then_inc(keep_ready[r], 1)

            pick_first(0)
            steps0 = steps[0]
            per_chunk = 5
            with v.Fori(0, TURNS) as t:
                for r in range(RING):
                    at = [0]

                    def then(ins, r=r, at=at, t=t):
                        at[0] += 1
                        ins.then_inc(step, 1)
                        v.wait_ge(step, t * (RING * per_chunk) + (steps0 + r * per_chunk + at[0]))

                    start_chunk(0, t, r)
                    v.wait_ge(dst_loaded[r], use(0, t) * 16)
                    nc.vector.tensor_scalar(dst_parts[:, 0, :], dst_t[:, r, :], P - 1, None, ALU.bitwise_and)
                    then(nc.vector.tensor_scalar(dst_parts[:, 1, :], dst_t[:, r, :], P.bit_length() - 1, None, ALU.logical_shift_right))
                    then(nc.vector.tensor_copy(dst_pairs[:, :, :, :], dst_parts[:, :, :].unsqueeze(3).broadcast_to([P, 2, J, 2])))
                    for to, of, n in ((one_hot_lo, 0, P), (one_hot_hi, 1, KT)):
                        last = nc.vector.tensor_tensor(pairs(to), dst_pairs[:, of, :, :].unsqueeze(2).broadcast_to([P, J, n // 2, 2]),
                                                       pairs(iota[:, 0:n].unsqueeze(1)).broadcast_to([P, J, n // 2, 2]), ALU.is_equal)
                    last.then_inc(one_hot_ready, 1)
                    pick_next(0, t, r, range(2))
                    wait_rows(0, t, r)
                    v.wait_ge(edge_loaded[r], use(0, t) * 16)
                    nc.vector.tensor_tensor(prod, rows[:, r, :], edge_in[:, r, :], ALU.mult).then_inc(rows_used[r], 1)
                    pick_next(0, t, r, range(2, 3))
                    v.wait_ge(rows_used[r], use(0, t, START))
                    then(nc.vector.transpose(by_edge(hT), prod))
                    pick_next(0, t, r, range(3, 4))
                    then(nc.vector.tensor_tensor_scan(O, keep, hT, carry[:, 3:4], ALU.mult, ALU.add))
                    then(nc.vector.tensor_copy(carry[:, 3:4], O[:, CH - 1:CH]))
                    pick_next(0, t, r, range(4, 5))
                    v.wait_ge(outs_stored[r], t * 16 + (0 * TURNS * 16 + START))
                    nc.vector.transpose(outs[:, r, 0:CH], by_edge(O)).then_inc(outs_ready[r], 1)
                    pick_next(0, t, r, range(5, PE_COLS[0]))
                    v.wait_ge(counts_ready, chunk_no(0, t, r))
                    v.wait_ge(counts_added, t * RING + (r + START))
                    nc.vector.tensor_tensor(counts[:, :], counts[:, :], acc[:, 0, 0:KT], ALU.add).then_inc(counts_added, 1)
                    assert at[0] == per_chunk
            steps[0] += NCH * per_chunk

            v.wait_ge(prep_ps, 2)
            A = [work[:, k, 0:KT] for k in (2, 3, 4, 5, 6, 7, 8, 9)]
            end, begin, e, grp, a, b, ne, no = A
            link(nc.vector.tensor_copy(b, acc[:, 1, 0:KT]))
            link(nc.vector.memset(a, 1.0))
            link(nc.vector.tensor_tensor_scan(e, a, b, 0.0, ALU.mult, ALU.add))
            link(nc.vector.tensor_tensor(e, e, b, ALU.subtract))
            link(nc.vector.tensor_tensor(end, e, acc[:, 0, 0:KT], ALU.add))
            link(nc.vector.tensor_tensor(begin, end, counts[:, :], ALU.subtract))
            link(nc.vector.tensor_scalar(ne, counts[:, :], 0.5, None, ALU.is_ge))
            link(nc.vector.tensor_copy(part_mask[:, 0, :], ne))
            for g in range(3):
                link(nc.vector.tensor_scalar(a, begin, float((g + 1) * GE) - 0.5, None, ALU.is_lt))
                link(nc.vector.tensor_scalar(b, end, float((g + 1) * GE) + 0.5, None, ALU.is_gt))
                link(nc.vector.tensor_tensor(part_mask[:, g + 1, :], a, b, ALU.mult))
            link(nc.vector.tensor_scalar(part_bias[:, :, :], part_mask[:, :, :], BIG, -BIG, ALU.mult, ALU.add))
            link(nc.vector.tensor_scalar(a, counts[:, :], 1.0, None, ALU.max))
            link(nc.vector.reciprocal(b, a))
            link(nc.vector.tensor_tensor(part_mean[:, :, :], part_mask[:, :, :],
                                         b.unsqueeze(1).broadcast_to([P, 4, KT]), ALU.mult))

            def row_of(edge):
                link(nc.vector.tensor_scalar(grp, edge, float(GE) - 0.5, None, ALU.is_gt))
                for g in range(2, G):
                    link(nc.vector.tensor_scalar(a, edge, float(g * GE) - 0.5, None, ALU.is_gt))
                    link(nc.vector.tensor_tensor(grp, grp, a, ALU.add))
                link(nc.vector.scalar_tensor_tensor(out=edge, in0=grp, scalar=-float(GE), in1=edge, op0=ALU.mult, op1=ALU.add))
                link(nc.vector.tensor_scalar(a, edge, 1.0 / CH, 0.5 / CH - 0.5, ALU.mult, ALU.add))
                link(nc.vector.tensor_scalar(a, a, 2.0 ** 23 + 2.0 ** 22, None, ALU.add))
                link(nc.vector.tensor_scalar(a, a, -(2.0 ** 23 + 2.0 ** 22), None, ALU.add))
                link(nc.vector.scalar_tensor_tensor(out=edge, in0=a, scalar=float((G - 1) * CH), in1=edge, op0=ALU.mult, op1=ALU.add))
                link(nc.vector.scalar_tensor_tensor(out=edge, in0=grp, scalar=float(CH), in1=edge, op0=ALU.mult, op1=ALU.add))

            link(nc.vector.tensor_scalar(e, end, -1.0, 0.0, ALU.add, ALU.max))
            row_of(e)
            link(nc.vector.tensor_copy(end_row[:, :], e))
            link(nc.vector.tensor_scalar(begin, begin, float(E - 1), None, ALU.min))
            row_of(begin)
            link(nc.vector.tensor_copy(no, iota[:, 0:KT]))
            link(nc.vector.tensor_scalar(no, no, float(P), float(E), ALU.mult, ALU.add))
            link(nc.vector.tensor_scalar(no, no, half[:, 2:3], None, ALU.add))
            link(nc.vector.tensor_tensor(a, begin, no, ALU.subtract))
            link(nc.vector.tensor_tensor(a, a, ne, ALU.mult))
            link(nc.vector.tensor_tensor(a, a, no, ALU.add))
            nc.vector.tensor_copy(begin_row[:, :], a).then_inc(node_index_ready, 1)
            v.wait_ge(node_index_ready, 1)

            def piece(q, width=D, at=0):
                return node_rows[:, q * PT * width:(q + 1) * PT * width].rearrange("p (k f) -> p k f", f=width)[:, :, at:at + D]

            agg = nt[:, 0, :].rearrange("p (k f) -> p k f", f=D)
            part = nt[:, 1, :].rearrange("p (k f) -> p k f", f=D)

            def parts_sum(rows_of_piece, weights):
                link(nc.vector.tensor_tensor(agg, rows_of_piece, spread_over(weights[:, 0, :], D), ALU.mult))
                for g in range(3):
                    link(nc.vector.tensor_tensor(part, spread_over(weights[:, g + 1, :], D),
                                                 border[:, g:g + 1, 0:D].broadcast_to([P, PT, D]), ALU.mult))
                    link(nc.vector.tensor_tensor(agg, agg, part, ALU.add))

            def mixed(n, rows_in, rows_out):
                nc.vector.transpose(nT[:, 0, :], rows_in).then_inc(mix_in, 1)
                v.wait_ge(mix_out, n + 1)
                return nc.vector.transpose(rows_out, nT[:, 1, :])

            def add_h(summand, q):
                high, low = (h_parts[:, k, q * PC:(q + 1) * PC] for k in range(2))
                link(nc.vector.tensor_tensor(nT[:, 0, :], high, low, ALU.add))
                link(nc.vector.tensor_tensor(agg, summand, nT[:, 0, :].rearrange("p (k f) -> p k f", f=D), ALU.add))

            def node_start(l, q):
                if q == 0:
                    v.wait_ge(border_loaded, 16 * (l + 1))
                    v.wait_ge(one_hot_cast, one_hot_base[l + 1])
                v.wait_ge(node_gathered[q], 16 * PT * (l + 1))
                return xs[:, q * PT:(q + 1) * PT, :], slice(q * PT, (q + 1) * PT)

            for q in range(PIECES):
                x, ks = node_start(0, q)
                parts_sum(piece(q), part_mean[:, :, ks])
                add_h(agg, q)
                link(nc.vector.tensor_tensor(x, x, agg, ALU.add))
                layer_norm(PIECES + q, q)
                mixed(q, h_new[:, (PIECES + q) % 2, :], node_rows[:, q * PC:(q + 1) * PC]).then_inc(q_ready, 1)
                v.wait_ge(q_ready, q + 1)

            nc.vector.memset(mx[:, 0:1], -BIG)
            link(nc.vector.memset(carry[:, :], 0.0))
            pick_first(1)
            steps1 = steps[0]
            per_chunk1 = 10
            with v.Fori(0, TURNS) as t:
                for r in range(RING):
                    at = [0]

                    def then(ins, r=r, at=at, t=t):
                        at[0] += 1
                        ins.then_inc(step, 1)
                        v.wait_ge(step, t * (RING * per_chunk1) + (steps1 + r * per_chunk1 + at[0]))

                    n = chunk_no(0, t, r)
                    start_chunk(1, t, r)
                    wait_rows(1, t, r)
                    nc.vector.transpose(by_edge(hT), rows[:, r, :]).then_inc(rows_used[r], 1)
                    v.wait_ge(edge_loaded[r], use(1, t) * 16)
                    nc.vector.transpose(by_edge(qT), edge_in[:, r, :]).then_inc(edge_used[r], 1)
                    v.wait_ge(edge_used[r], t + (1 + START))
                    then(nc.vector.tensor_tensor_scan(qh, keep, qT, carry[:, 0:1], ALU.mult, ALU.add))
                    nc.vector.tensor_tensor(prod, qh, hT, ALU.mult).then_inc(prod_ready, 1)
                    then(nc.vector.tensor_copy(carry[:, 0:1], qh[:, CH - 1:CH]))
                    pick_next(1, t, r, range(2))
                    v.wait_ge(nb_ready, n)
                    v.wait_ge(score_copied, chunk_no(0, t, r, START))
                    nc.vector.tensor_tensor_scan(mx[:, 1:CH + 1], nb, s_sb, mx[:, 0:1], ALU.add, ALU.max).then_inc(mx_ready, 1)
                    v.wait_ge(mx_ready, n)
                    then(nc.vector.tensor_tensor(rise, mx[:, 0:CH], nb, ALU.add))
                    nc.vector.tensor_tensor(rise, s_sb, rise, ALU.subtract).then_inc(rise_ready, 1)
                    pick_next(1, t, r, range(2, PE_COLS[1]))
                    v.wait_ge(decay_ready, n)
                    v.wait_ge(p_ready, n)
                    then(nc.vector.tensor_tensor(ph, d, hT, ALU.mult))
                    then(nc.vector.tensor_tensor_scan(Z, u, d, carry[:, 1:2], ALU.mult, ALU.add))
                    then(nc.vector.tensor_tensor_scan(O, u, ph, carry[:, 2:3], ALU.mult, ALU.add))
                    then(nc.vector.tensor_copy(carry[:, 1:3], work[:, 7:10:2, CH - 1]))
                    v.wait_ge(mz_m_ready, n)
                    then(nc.vector.tensor_copy(mx[:, 0:1], mx[:, CH:CH + 1]))
                    then(nc.vector.scalar_tensor_tensor(out=mz, in0=Z, scalar=half[:, 1:2], in1=mz_m, op0=ALU.mult, op1=ALU.add))
                    v.wait_ge(outs_stored[r], t * 16 + (1 * TURNS * 16 + START))
                    row = outs[:, r, :].rearrange("p (j f) -> p j f", j=J)
                    then(nc.vector.transpose(row[:, :, 0:D], by_edge(O)))
                    nc.vector.transpose(row[:, :, D:2 * D], by_edge(mz)).then_inc(outs_ready[r], 1)
                    assert at[0] == per_chunk1
            steps[0] += NCH * per_chunk1

            for q in range(PIECES):
                x, ks = node_start(1, q)
                at_m, at_z = piece(q, 2 * D, D)[:, :, 0], piece(q, 2 * D, D)[:, :, Z_COL - M_COL]
                w, top, z = aw[:, 0:4, :], aw[:, 4, :], aw[:, 5, :]
                link(nc.vector.tensor_tensor(w[:, 0, :], at_m, part_mask[:, 0, ks], ALU.mult))
                link(nc.vector.tensor_tensor(w[:, 0, :], w[:, 0, :], part_bias[:, 0, ks], ALU.add))
                link(nc.vector.tensor_copy(top, w[:, 0, :]))
                for g in range(3):
                    link(nc.vector.scalar_tensor_tensor(out=w[:, g + 1, :], in0=part_mask[:, g + 1, ks], scalar=border[:, g, M_COL:M_COL + 1],
                                                        in1=part_bias[:, g + 1, ks], op0=ALU.mult, op1=ALU.add))
                    link(nc.vector.tensor_tensor(top, top, w[:, g + 1, :], ALU.max))
                nc.vector.tensor_tensor(w, w, top.unsqueeze(1).broadcast_to([P, 4, PT]), ALU.subtract).then_inc(part_in, 1)
                v.wait_ge(part_exp, q + 1)
                link(nc.vector.tensor_tensor(w, w, part_mask[:, :, ks], ALU.mult))
                link(nc.vector.tensor_tensor(z, w[:, 0, :], at_z, ALU.mult))
                for g in range(3):
                    link(nc.vector.scalar_tensor_tensor(out=z, in0=w[:, g + 1, :], scalar=border[:, g, Z_COL:Z_COL + 1], in1=z,
                                                        op0=ALU.mult, op1=ALU.add))
                link(nc.vector.tensor_scalar(z, z, Z_EPS, None, ALU.add))
                link(nc.vector.reciprocal(top, z))
                link(nc.vector.tensor_tensor(w, w, top.unsqueeze(1).broadcast_to([P, 4, PT]), ALU.mult))
                parts_sum(piece(q, 2 * D), w)
                link(mixed(PIECES + q, nt[:, 0, :], nt[:, 1, :]))
                add_h(part, q)
                link(nc.vector.tensor_tensor(x, x, agg, ALU.add))
                layer_norm(2 * PIECES + q, q)

            def plain_chunk(l, t, r, messages, then):
                then(nc.vector.tensor_tensor_scan(O, keep, messages, carry[:, 3:4], ALU.mult, ALU.add))
                then(nc.vector.tensor_copy(carry[:, 3:4], O[:, CH - 1:CH]))
                v.wait_ge(outs_stored[r], t * 16 + (l * TURNS * 16 + START))
                nc.vector.transpose(outs[:, r, 0:CH], by_edge(O)).then_inc(outs_ready[r], 1)
                v.wait_ge(outs_ready[r], use(l, t))

            link(nc.vector.memset(carry[:, :], 0.0))
            pick_first(2)
            steps2 = steps[0]
            per_chunk2 = 2
            with v.Fori(0, TURNS) as t:
                for r in range(RING):
                    at = [0]

                    def then(ins, r=r, at=at, t=t):
                        at[0] += 1
                        ins.then_inc(step, 1)
                        v.wait_ge(step, t * (RING * per_chunk2) + (steps2 + r * per_chunk2 + at[0]))

                    start_chunk(2, t, r)
                    pick_next(2, t, r, range(PE_COLS[2]))
                    wait_rows(2, t, r)
                    nc.vector.transpose(by_edge(hT), rows[:, r, :]).then_inc(rows_used[r], 1)
                    v.wait_ge(rows_used[r], use(2, t, START))
                    plain_chunk(2, t, r, hT, then)
                    assert at[0] == per_chunk2
            steps[0] += NCH * per_chunk2

            for q in range(PIECES):
                x, ks = node_start(2, q)
                parts_sum(piece(q), part_mask[:, :, ks])
                link(mixed(2 * PIECES + q, nt[:, 0, :], nt[:, 1, :]))
                link(nc.vector.tensor_tensor(x, x, part, ALU.add))
                layer_norm(3 * PIECES + q, q)

            link(nc.vector.memset(carry[:, :], 0.0))
            sh3 = sh_parts.rearrange("p (j c) -> p j c", c=D)
            link(nc.vector.memset(sh_parts, 0.0))

            def split_sh(t, r, then):
                r1 = (r + 1) % RING
                v.wait_ge(edge_loaded[r1], 16 * (2 * TURNS + 1) if t is None else (t + (2 * TURNS + 1 + (r + 1) // RING)) * 16)
                sh_f = edge_in[:, r1, 0:J * SH].rearrange("p (j c) -> p j c", c=SH)
                then(nc.vector.tensor_copy(sh3[:, :, 0:SH], sh_f))
                nc.vector.tensor_tensor(sh_rest, sh_f, sh3[:, :, 0:SH], ALU.subtract).then_inc(edge_used[r1], 1)
                v.wait_ge(edge_used[r1], TURNS + 1 + START if t is None else t + (TURNS + 1 + (r + 1) // RING + START))
                then(nc.vector.tensor_copy(sh3[:, :, SH:2 * SH], sh_rest))
                then(nc.vector.tensor_tensor(sh3[:, :, 2 * SH:3 * SH], sh_rest, sh3[:, :, SH:2 * SH], ALU.subtract))
                if t is not None:
                    v.wait_ge(bcast_ready[2], t * (6 * RING) + 6 * (r + 1))
                nc.vector.transpose(by_edge(shT), sh_parts).then_inc(shT_ready, 1)

            split_sh(None, -1, link)
            pick_first(3)
            PICK_AFTER = [(2 * SH * (k + 1)) // (PE_COLS[3] + 1) for k in range(PE_COLS[3])]
            steps3 = steps[0]
            per_chunk3 = 5
            with v.Fori(0, TURNS) as t:
                for r in range(RING):
                    at = [0]

                    def then(ins, r=r, at=at, t=t):
                        at[0] += 1
                        ins.then_inc(step, 1)
                        v.wait_ge(step, t * (RING * per_chunk3) + (steps3 + r * per_chunk3 + at[0]))

                    wait_rows(3, t, r)
                    nc.vector.transpose(by_edge(hT), rows[:, r, :]).then_inc(rows_used[r], 1)
                    start_chunk(3, t, r)
                    v.wait_ge(rows_used[r], use(3, t, START))
                    for n in range(2 * SH):
                        uses = t * (6 * RING) + (6 * r + n // 3)
                        v.wait_ge(bcast_ready[n % 3], uses + 1)
                        v.wait_ge(weighted_used[n % 3], uses + START)
                        nc.vector.tensor_tensor(weighted[n % 3][:, 0:HALF], bcast[n % 3][:, 0:HALF],
                                                hT[:, (n % 2) * HALF:(n % 2 + 1) * HALF], ALU.mult).then_inc(weighted_ready[n % 3], 1)
                        if n in PICK_AFTER:
                            pick_next(3, t, r, [PICK_AFTER.index(n)])
                    split_sh(t, r, then)
                    v.wait_ge(msg_copied, chunk_no(0, t, r, START))
                    plain_chunk(3, t, r, s_sb, then)
                    assert at[0] == per_chunk3
            steps[0] += NCH * per_chunk3

            for q in range(PIECES):
                x, ks = node_start(3, q)
                parts_sum(piece(q), part_mask[:, :, ks])
                nc.vector.tensor_tensor(x, x, agg, ALU.add).then_inc(x_ready, 1)
                v.wait_ge(x_ready, q + 1)


def coupling_coefficients():
    f = math.factorial

    def coefficient(j1, m1, j2, m2, j3, m3):
        if m3 != m1 + m2:
            return 0.0
        pref = (2 * j3 + 1) * f(j3 + j1 - j2) * f(j3 - j1 + j2) * f(j1 + j2 - j3) / f(j1 + j2 + j3 + 1)
        pref *= f(j3 + m3) * f(j3 - m3) * f(j1 - m1) * f(j1 + m1) * f(j2 - m2) * f(j2 + m2)
        s = 0.0
        for k in range(max(0, j2 - j3 - m1, j1 + m2 - j3), min(j1 + j2 - j3, j1 - m1, j2 + m2) + 1):
            s += (-1) ** k / (f(k) * f(j1 + j2 - j3 - k) * f(j1 - m1 - k) * f(j2 + m2 - k)
                              * f(j3 - j2 + m1 + k) * f(j3 - j1 - m2 + k))
        return math.sqrt(pref) * s

    def complex_cg(l1, l2, l3):
        C = np.zeros((2 * l1 + 1, 2 * l2 + 1, 2 * l3 + 1), np.complex128)
        for m1 in range(-l1, l1 + 1):
            for m2 in range(-l2, l2 + 1):
                if -l3 <= m1 + m2 <= l3:
                    C[m1 + l1, m2 + l2, m1 + m2 + l3] = coefficient(l1, m1, l2, m2, l3, m1 + m2)
        return C

    def to_real(l):
        q = np.zeros((2 * l + 1, 2 * l + 1), np.complex128)
        for m in range(-l, 0):
            q[l + m, l + abs(m)] = 1 / np.sqrt(2)
            q[l + m, l - abs(m)] = -1j / np.sqrt(2)
        q[l, l] = 1.0
        for m in range(1, l + 1):
            q[l + m, l + abs(m)] = (-1) ** m / np.sqrt(2)
            q[l + m, l - abs(m)] = 1j * (-1) ** m / np.sqrt(2)
        return (-1j) ** l * q

    found = []
    for l1, l2, l3 in ((0, 0, 0), (0, 1, 1), (1, 0, 1), (1, 1, 0), (1, 1, 1), (2, 1, 1)):
        C = np.einsum("ij,kl,mn,ikn->jlm", to_real(l1), to_real(l2), np.conj(to_real(l3)).T, complex_cg(l1, l2, l3)).real
        found.append(((l1, l2, l3), (C / np.linalg.norm(C)).astype(np.float32)))
    return found


def constants(KT):
    mul = D // 4
    p = np.arange(P)
    feature, group = p % D, p // D
    inner = np.where(feature < mul, feature, (feature - mul) // 3)
    sel = np.zeros((P, SH, P), np.float32)
    for c in range(SH):
        sel[:, c, :] = (group[:, None] == group[None]) & np.isin(feature, (c, SH + c, 2 * SH + c))[:, None]
    cg = coupling_coefficients()
    first = (0, 1, 4)
    coupling = np.zeros((P, len(LAYER3_TERMS), D), np.float32)
    f_in, f_out = feature, np.arange(D)
    for n, (c, i) in enumerate(LAYER3_TERMS):
        (le, ln, lo), C = cg[i]
        m_in = np.where(f_in < mul, 0, (f_in - mul) % 3)
        m_out = np.where(f_out < mul, 0, (f_out - mul) % 3)
        ok = ((f_in >= mul) == (ln == 1))[:, None] & ((f_out >= mul) == (lo == 1))[None]
        table = C[c - first[le]]
        coupling[:, n, :] = np.where(ok, table[np.minimum(m_in, 2 * ln)[:, None], np.minimum(m_out, 2 * lo)[None]], 0.0)
    half = np.zeros((P, 3), np.float32)
    half[:, 0] = feature < D // 2
    half[:, 1] = feature >= D // 2
    half[:, 2] = p
    return {
        "c_ones": np.ones((P, P), np.float32),
        "c_tri": (p[:, None] <= p[None]).astype(np.float32),
        "c_group": (group[:, None] == group[None]).astype(np.float32),
        "c_iota": np.broadcast_to(p.astype(np.int16), (P, P)).copy(),
        "c_half": half,
        "c_sel": sel.reshape(P, SH * P),
        "c_expand": (np.arange(mul)[:, None] == inner[None]).astype(np.float32),
        "c_coupling": coupling,
        "c_target": np.repeat(p[:, None] + P * np.arange(KT // H0)[None], 2, axis=1).reshape(P, -1, 2).astype(np.int16),
    }


_INS = ("x_in", "src_c", "src_pe", "dst_c", "dst_w", "pattern_c", "sh_c", "wq", "wk", "wv", "wo", "w2", "w3",
        "c_ones", "c_tri", "c_group", "c_iota", "c_half", "c_sel", "c_expand", "c_coupling", "c_target")


def laid_out(a):
    n, e = a["x"].shape[0], a["src"].shape[0]
    KT = -(-n // (P * PT)) * PT
    NCH = e // (G * CH)
    assert NCH * G * CH == e and NCH % RING == 0

    def by_chunk(edges):
        return edges.reshape(G, NCH, D, J, -1).transpose(1, 0, 2, 3, 4).reshape(NCH, P, -1)

    dst = a["dst"]
    before = np.concatenate([np.full(1, -1, dst.dtype), dst[:-1]]).reshape(G, NCH, CH)[:, :, :1]
    windows = np.concatenate([before, dst.reshape(G, NCH, CH)], axis=2).transpose(1, 0, 2)
    sh = np.concatenate([a["edge_weight1"], a["edge_attr_3"], a["edge_attr_5"]], axis=1)
    sh_c = by_chunk(sh)
    src_c = by_chunk(a["src"])
    pe_cols = np.concatenate([src_c, src_c, src_c])[0:NCH + 2, :, J - PE_MAX:J]
    src_pe = np.concatenate([pe_cols.transpose(0, 2, 1).reshape(P, -1), pe_cols.transpose(1, 0, 2).reshape(P, -1)], axis=1)
    x = np.concatenate([a["x"], np.zeros((KT * P - n, D), a["x"].dtype)])
    laid = {
        "x_in": x.reshape(KT, P, D).transpose(1, 0, 2),
        "src_c": src_c, "src_pe": src_pe, "dst_c": by_chunk(dst), "dst_w": windows,
        "pattern_c": by_chunk(a["edge_attr_32"]), "sh_c": np.concatenate([sh_c, sh_c[0:1]]),
        "wq": a["L1_gnn_Wq"], "wk": a["L1_gnn_Wk"], "wv": a["L1_gnn_Wv"], "wo": a["L1_gnn_Wo"],
        "w2": a["L2_gnn_W"], "w3": a["L3_gnn_W"], **constants(KT),
    }
    return {name: np.ascontiguousarray(laid[name]) for name in _INS}


def kernel(**inputs):
    import concourse.bacc as bacc
    from concourse.bass_utils import run_bass_kernel_spmd

    arrays = laid_out({name: np.asarray(a) for name, a in inputs.items()})
    n = inputs["x"].shape[0]
    nc = bacc.Bacc("TRN2", target_bir_lowering=False, num_devices=1)
    args = [nc.dram_tensor(name, a.shape, mybir.dt.from_np(a.dtype), kind="ExternalInput").ap() for name, a in arrays.items()]
    args.append(nc.dram_tensor("out", arrays["x_in"].shape, F32, kind="ExternalOutput").ap())
    gnn_kernel(nc, *args)
    result = run_bass_kernel_spmd(nc, [arrays], core_ids=[0])
    y = result.results[0]["out"]
    return y.transpose(1, 0, 2).reshape(-1, D)[:n]
```
